# Optimizing a Trainium2 kernel written in Bass

```python
import numpy as np
import jax
import jax.numpy as jnp

def _softmax(x, axis=-1):
    return jax.nn.softmax(x, axis=axis)

def _gelu(x):
    return jax.nn.gelu(x, approximate=True)

def _silu(x):
    return jax.nn.silu(x)

def _sigmoid(x):
    return jax.nn.sigmoid(x)

def _layernorm(x, axis=-1, eps=1e-05):
    m = jnp.mean(x, axis=axis, keepdims=True)
    v = jnp.var(x, axis=axis, keepdims=True)
    return (x - m) / jnp.sqrt(v + eps)

def _scatter_add(tgt, idx, src, axis=0):
    return tgt.at[idx].add(src)

def _segment_sum(src, seg, n):
    return jax.ops.segment_sum(src, seg, n)
kernel_name = 'mk_gnn_resnorm_d4_gnn_r32_79ebe5'

def setup_inputs(seed: int=0):
    np.random.seed(seed)
    _w = jnp.asarray

    def _rec_inputs():
        import jax
        import jax.numpy as jnp
        _gk = jax.random.key(seed)
        x = -0.0001538 + 1 * jax.random.normal(jax.random.fold_in(_gk, 1), (256, 768), jnp.float32)
        _s = jax.random.randint(jax.random.fold_in(_gk, 2), (2048,), 0, 256, jnp.int32)
        _d = jax.random.randint(jax.random.fold_in(_gk, 3), (2048,), 0, 256, jnp.int32)
        _loop = jnp.arange(256, dtype=jnp.int32)
        src = jnp.concatenate([_s, _d, _loop])
        dst = jnp.concatenate([_d, _s, _loop])
        _o = jnp.argsort(dst, stable=True)
        src = src[_o]
        dst = dst[_o]
        return (x, src, dst)
    x, src, dst = _rec_inputs()

    def _L0_gnn_setup():
        import jax, jax.numpy as jnp
        import numpy as np
        NEG_SLOPE = 0.2
        EPS = 1e-16
        N_NODES = 256
        N_EDGES = 2048
        D_IN = 768
        D_HID = 768
        H1 = 8
        H2 = 1

        def gat_layer(x, W, a_s, a_d, b, edge_index, concat):
            n = x.shape[0]
            H, C = a_s.shape
            h = (x @ W).reshape(n, H, C)
            src, dst = (edge_index[0], edge_index[1])
            alpha_s = jnp.einsum('nhc,hc->nh', h, a_s)
            alpha_d = jnp.einsum('nhc,hc->nh', h, a_d)
            e = jax.nn.leaky_relu(alpha_s[src] + alpha_d[dst], NEG_SLOPE)
            m = jax.ops.segment_max(e, dst, num_segments=n)
            e = jnp.exp(e - m[dst])
            denom = jax.ops.segment_sum(e, dst, num_segments=n)
            alpha = e / (denom[dst] + EPS)
            msg = h[src] * alpha[:, :, None]
            out = jax.ops.segment_sum(msg, dst, num_segments=n)
            out = out.reshape(n, H * C) if concat else out.mean(axis=1)
            return out + b
        key = jax.random.key(seed)
        ks = jax.random.split(key, 10)
        x = jax.random.normal(ks[0], (N_NODES, D_IN), dtype=jnp.float32)
        edge_list = jax.random.randint(ks[1], (2, N_EDGES), 0, N_NODES, dtype=jnp.int32)
        s = 0.05
        W1 = jax.random.normal(ks[2], (D_IN, H1 * D_HID), dtype=jnp.float32) * s
        a_src1 = jax.random.normal(ks[3], (H1, D_HID), dtype=jnp.float32) * s
        a_dst1 = jax.random.normal(ks[4], (H1, D_HID), dtype=jnp.float32) * s
        b1 = jnp.zeros((H1 * D_HID,), dtype=jnp.float32)
        W2 = jax.random.normal(ks[5], (H1 * D_HID, H2 * D_HID), dtype=jnp.float32) * s
        a_src2 = jax.random.normal(ks[6], (H2, D_HID), dtype=jnp.float32) * s
        a_dst2 = jax.random.normal(ks[7], (H2, D_HID), dtype=jnp.float32) * s
        b2 = jnp.zeros((H2 * D_HID,), dtype=jnp.float32)
        return {'x': x, 'W1': W1, 'a_src1': a_src1, 'a_dst1': a_dst1, 'b1': b1, 'W2': W2, 'a_src2': a_src2, 'a_dst2': a_dst2, 'b2': b2, 'edge_list': edge_list}
    _L0_gnn_all = _L0_gnn_setup()
    _L0_gnn_in = {k: v for k, v in _L0_gnn_all.items() if k in ('W1', 'a_src1', 'a_dst1', 'b1', 'W2', 'a_src2', 'a_dst2', 'b2')}
    del _L0_gnn_all

    def _L1_gnn_setup():
        import jax, jax.numpy as jnp
        import numpy as np
        N_NODES = 10000
        key = jax.random.key(seed)
        k1, k2, k3 = jax.random.split(key, 3)
        x = jax.random.normal(k1, (N_NODES, 768), dtype=jnp.float32)
        edge_index = jax.random.randint(k2, (2, 3125), 0, N_NODES, dtype=jnp.int32)
        W = jax.random.normal(k3, (768, 768), dtype=jnp.float32) * (1.0 / np.sqrt(768))
        b = jnp.zeros((768,), dtype=jnp.float32)
        return {'x': x, 'edge_index': edge_index, 'W': W, 'b': b}
    _L1_gnn_all = _L1_gnn_setup()
    _L1_gnn_in = {k: v for k, v in _L1_gnn_all.items() if k in ('W', 'b')}
    del _L1_gnn_all

    def _L2_gnn_setup():
        import jax, jax.numpy as jnp
        import numpy as np
        N_NODES = 10000
        N_EDGES = 5000
        NEG_SLOPE = 0.2

        def _gat_layer(x, src, dst, W, a_src, a_dst, bias, concat):
            N = x.shape[0]
            H, C = a_src.shape
            h = (x @ W).reshape(N, H, C)
            al_s = jnp.einsum('nhc,hc->nh', h, a_src)
            al_d = jnp.einsum('nhc,hc->nh', h, a_dst)
            e = jax.nn.leaky_relu(al_s[src] + al_d[dst], NEG_SLOPE)
            m = jax.ops.segment_max(e, dst, num_segments=N)
            ex = jnp.exp(e - m[dst])
            denom = jax.ops.segment_sum(ex, dst, num_segments=N)
            alpha = ex / (denom[dst] + 1e-16)
            msg = h[src] * alpha[:, :, None]
            out = jax.ops.segment_sum(msg, dst, num_segments=N)
            out = out.reshape(N, H * C) if concat else out.mean(axis=1)
            return out + bias
        key = jax.random.key(seed)
        ks = jax.random.split(key, 10)
        in_dim, hid, out_dim, heads = (768, 512, 768, 4)
        x = jax.random.normal(ks[0], (N_NODES, in_dim), dtype=jnp.float32)
        edge_index = jax.random.randint(ks[1], (2, N_EDGES), 0, N_NODES, dtype=jnp.int64)
        g = lambda k, shape, fan: jax.random.normal(k, shape, jnp.float32) / np.sqrt(fan)
        return {'x': x, 'edge_index': edge_index, 'W1': g(ks[2], (in_dim, heads * hid), in_dim), 'att_src1': g(ks[3], (heads, hid), hid), 'att_dst1': g(ks[4], (heads, hid), hid), 'b1': jnp.zeros((heads * hid,), jnp.float32), 'W2': g(ks[5], (heads * hid, out_dim), heads * hid), 'att_src2': g(ks[6], (1, out_dim), out_dim), 'att_dst2': g(ks[7], (1, out_dim), out_dim), 'b2': jnp.zeros((out_dim,), jnp.float32)}
    _L2_gnn_all = _L2_gnn_setup()
    _L2_gnn_in = {k: v for k, v in _L2_gnn_all.items() if k in ('W1', 'att_src1', 'att_dst1', 'b1', 'W2', 'att_src2', 'att_dst2', 'b2')}
    del _L2_gnn_all

    def _L3_gnn_setup():
        import jax, jax.numpy as jnp
        import numpy as np
        N = 625
        DEG = 16
        E = N * DEG
        H = 12
        DIN = 64
        DOUT = 64
        NEG_SLOPE = 0.2
        key = jax.random.key(seed)
        k_h, k_src, k_w, k_al, k_ar, k_wr = jax.random.split(key, 6)
        std = 1.414 * np.sqrt(2.0 / (DIN + DOUT))
        h = jax.random.normal(k_h, (N, H * DIN), dtype=jnp.float32)
        src = jax.random.randint(k_src, (E,), 0, N, dtype=jnp.int64)
        dst = jnp.repeat(jnp.arange(N, dtype=jnp.int64), DEG)
        W = jax.random.normal(k_w, (DOUT, DIN), dtype=jnp.float32) * std
        attn_l = jax.random.normal(k_al, (1, H, DOUT), dtype=jnp.float32) * std
        attn_r = jax.random.normal(k_ar, (1, H, DOUT), dtype=jnp.float32) * std
        W_res = jax.random.normal(k_wr, (DOUT, DIN), dtype=jnp.float32) * std
        return {'h': h, 'src': src, 'dst': dst, 'W': W, 'attn_l': attn_l, 'attn_r': attn_r, 'W_res': W_res}
    _L3_gnn_all = _L3_gnn_setup()
    _L3_gnn_in = {k: v for k, v in _L3_gnn_all.items() if k in ('W', 'attn_l', 'attn_r', 'W_res')}
    del _L3_gnn_all
    return {'x': x, 'src': src, 'dst': dst, 'L0_gnn_W1': _L0_gnn_in['W1'], 'L0_gnn_a_src1': _L0_gnn_in['a_src1'], 'L0_gnn_a_dst1': _L0_gnn_in['a_dst1'], 'L0_gnn_b1': _L0_gnn_in['b1'], 'L0_gnn_W2': _L0_gnn_in['W2'], 'L0_gnn_a_src2': _L0_gnn_in['a_src2'], 'L0_gnn_a_dst2': _L0_gnn_in['a_dst2'], 'L0_gnn_b2': _L0_gnn_in['b2'], 'L1_gnn_W': _L1_gnn_in['W'], 'L1_gnn_b': _L1_gnn_in['b'], 'L2_gnn_W1': _L2_gnn_in['W1'], 'L2_gnn_att_src1': _L2_gnn_in['att_src1'], 'L2_gnn_att_dst1': _L2_gnn_in['att_dst1'], 'L2_gnn_b1': _L2_gnn_in['b1'], 'L2_gnn_W2': _L2_gnn_in['W2'], 'L2_gnn_att_src2': _L2_gnn_in['att_src2'], 'L2_gnn_att_dst2': _L2_gnn_in['att_dst2'], 'L2_gnn_b2': _L2_gnn_in['b2'], 'L3_gnn_W': _L3_gnn_in['W'], 'L3_gnn_attn_l': _L3_gnn_in['attn_l'], 'L3_gnn_attn_r': _L3_gnn_in['attn_r'], 'L3_gnn_W_res': _L3_gnn_in['W_res']}

def reference(x, src, dst, L0_gnn_W1, L0_gnn_a_src1, L0_gnn_a_dst1, L0_gnn_b1, L0_gnn_W2, L0_gnn_a_src2, L0_gnn_a_dst2, L0_gnn_b2, L1_gnn_W, L1_gnn_b, L2_gnn_W1, L2_gnn_att_src1, L2_gnn_att_dst1, L2_gnn_b1, L2_gnn_W2, L2_gnn_att_src2, L2_gnn_att_dst2, L2_gnn_b2, L3_gnn_W, L3_gnn_attn_l, L3_gnn_attn_r, L3_gnn_W_res):
    import jax
    import jax.numpy as jnp

    def _L0_gnn_ref(x, W1, a_src1, a_dst1, b1, W2, a_src2, a_dst2, b2, edge_list):
        import jax, jax.numpy as jnp
        import numpy as np
        NEG_SLOPE = 0.2
        EPS = 1e-16
        N_NODES = 256
        N_EDGES = 2048
        D_IN = 768
        D_HID = 768
        H1 = 8
        H2 = 1

        def gat_layer(x, W, a_s, a_d, b, edge_index, concat):
            n = x.shape[0]
            H, C = a_s.shape
            h = (x @ W).reshape(n, H, C)
            src, dst = (edge_index[0], edge_index[1])
            alpha_s = jnp.einsum('nhc,hc->nh', h, a_s)
            alpha_d = jnp.einsum('nhc,hc->nh', h, a_d)
            e = jax.nn.leaky_relu(alpha_s[src] + alpha_d[dst], NEG_SLOPE)
            m = jax.ops.segment_max(e, dst, num_segments=n)
            e = jnp.exp(e - m[dst])
            denom = jax.ops.segment_sum(e, dst, num_segments=n)
            alpha = e / (denom[dst] + EPS)
            msg = h[src] * alpha[:, :, None]
            out = jax.ops.segment_sum(msg, dst, num_segments=n)
            out = out.reshape(n, H * C) if concat else out.mean(axis=1)
            return out + b
        h = gat_layer(x, W1, a_src1, a_dst1, b1, edge_list, concat=True)
        h = jax.nn.elu(h)
        out = gat_layer(h, W2, a_src2, a_dst2, b2, edge_list, concat=True)
        return out

    def _L1_gnn_ref(x, edge_index, W, b):
        import jax, jax.numpy as jnp
        import numpy as np
        N_NODES = 10000
        n = x.shape[0]
        loops = jnp.arange(n, dtype=edge_index.dtype)
        row = jnp.concatenate([edge_index[0], loops])
        col = jnp.concatenate([edge_index[1], loops])
        ones = jnp.ones(row.shape[0], dtype=x.dtype)
        deg = jax.ops.segment_sum(ones, col, num_segments=n)
        dinv = jnp.where(deg > 0, jax.lax.rsqrt(deg), 0.0)
        norm = dinv[row] * dinv[col]
        h = x @ W
        msg = h[row] * norm[:, None]
        out = jax.ops.segment_sum(msg, col, num_segments=n) + b
        return out

    def _L2_gnn_ref(x, edge_index, W1, att_src1, att_dst1, b1, W2, att_src2, att_dst2, b2):
        import jax, jax.numpy as jnp
        import numpy as np
        N_NODES = 10000
        N_EDGES = 5000
        NEG_SLOPE = 0.2

        def _gat_layer(x, src, dst, W, a_src, a_dst, bias, concat):
            N = x.shape[0]
            H, C = a_src.shape
            h = (x @ W).reshape(N, H, C)
            al_s = jnp.einsum('nhc,hc->nh', h, a_src)
            al_d = jnp.einsum('nhc,hc->nh', h, a_dst)
            e = jax.nn.leaky_relu(al_s[src] + al_d[dst], NEG_SLOPE)
            m = jax.ops.segment_max(e, dst, num_segments=N)
            ex = jnp.exp(e - m[dst])
            denom = jax.ops.segment_sum(ex, dst, num_segments=N)
            alpha = ex / (denom[dst] + 1e-16)
            msg = h[src] * alpha[:, :, None]
            out = jax.ops.segment_sum(msg, dst, num_segments=N)
            out = out.reshape(N, H * C) if concat else out.mean(axis=1)
            return out + bias
        N = x.shape[0]
        loops = jnp.arange(N, dtype=edge_index.dtype)
        src = jnp.concatenate([edge_index[0], loops])
        dst = jnp.concatenate([edge_index[1], loops])
        h = jax.nn.elu(_gat_layer(x, src, dst, W1, att_src1, att_dst1, b1, concat=True))
        out = _gat_layer(h, src, dst, W2, att_src2, att_dst2, b2, concat=False)
        return out

    def _L3_gnn_ref(h, src, dst, W, attn_l, attn_r, W_res):
        import jax, jax.numpy as jnp
        import numpy as np
        N = 625
        DEG = 16
        E = N * DEG
        H = 12
        DIN = 64
        DOUT = 64
        NEG_SLOPE = 0.2
        n = h.shape[0]
        hv = h.reshape(n, H, DIN)
        ft = jnp.einsum('nhd,od->nho', hv, W)
        a1 = jnp.sum(ft * attn_l, axis=-1)
        a2 = jnp.sum(ft * attn_r, axis=-1)
        e = jax.nn.leaky_relu(a1[src] + a2[dst], negative_slope=NEG_SLOPE)
        m = jax.ops.segment_max(e, dst, num_segments=n)
        m = jnp.where(jnp.isfinite(m), m, 0.0)
        w = jnp.exp(e - m[dst])
        denom = jax.ops.segment_sum(w, dst, num_segments=n)
        alpha = w / jnp.maximum(denom[dst], 1e-16)
        msg = alpha[:, :, None] * ft[src]
        agg = jax.ops.segment_sum(msg, dst, num_segments=n)
        res = jnp.einsum('nhd,od->nho', hv, W_res)
        out = jax.nn.relu((agg + res).reshape(n, H * DOUT))
        return out
    edge_index = jnp.stack([src, dst])
    x = _layernorm(x + _L0_gnn_ref(x, L0_gnn_W1, L0_gnn_a_src1, L0_gnn_a_dst1, L0_gnn_b1, L0_gnn_W2, L0_gnn_a_src2, L0_gnn_a_dst2, L0_gnn_b2, edge_index), axis=-1)
    x = _layernorm(x + _L1_gnn_ref(x, edge_index, L1_gnn_W, L1_gnn_b), axis=-1)
    x = _layernorm(x + _L2_gnn_ref(x, edge_index, L2_gnn_W1, L2_gnn_att_src1, L2_gnn_att_dst1, L2_gnn_b1, L2_gnn_W2, L2_gnn_att_src2, L2_gnn_att_dst2, L2_gnn_b2), axis=-1)
    x = _layernorm(x + _L3_gnn_ref(x, src, dst, L3_gnn_W, L3_gnn_attn_l, L3_gnn_attn_r, L3_gnn_W_res), axis=-1)
    return x

_drawn_inputs = setup_inputs


def setup_inputs(seed=0):
    import zlib

    import numpy as np

    out = dict(_drawn_inputs(seed))
    spreads = {'L0_gnn_b1': (0.0, 0.1),
     'L0_gnn_b2': (0.0, 0.1),
     'L1_gnn_b': (0.0, 0.1),
     'L2_gnn_b1': (0.0, 0.1),
     'L2_gnn_b2': (0.0, 0.1)}
    factors = {'L2_gnn_att_dst1': 5.488, 'L2_gnn_att_src2': 3.617, 'L2_gnn_att_dst2': 7.184}
    for name, (base, spread) in spreads.items():
        noise = np.random.default_rng([zlib.crc32(name.encode()), seed]).standard_normal(out[name].shape)
        drawn = base * np.exp(spread * noise) if base else spread * noise
        out[name] = jnp.asarray(drawn.astype(out[name].dtype))
    for name, factor in factors.items():
        out[name] = (out[name] * factor).astype(out[name].dtype)
    return out
```

```python
from contextlib import ExitStack

import concourse.bass as bass
from concourse import mybir

F32 = mybir.dt.float32
F32R = mybir.dt.float32r
BF16 = mybir.dt.bfloat16
I32 = mybir.dt.int32
ALU = mybir.AluOpType
ACT = mybir.ActivationFunctionType

P = 128
BANK = 512
NEG_SLOPE = 0.2
ATT_EPS = 1e-16
LN_EPS = 1e-5
MASKED = -1e30


class GatLayer:

    def __init__(self, heads, width, att, head, pair, w1, w2, w2_used, w1_k, w2_k):
        self.heads, self.width = heads, width
        self.att, self.head, self.pair = att, head, pair
        self.w1, self.w2, self.w2_used = w1, w2, w2_used
        self.w1_k, self.w2_k = w1_k, w2_k
        self.blocks = width // P
        self.pairs = self.blocks // 2


def gnn_kernel(nc, x, src, dst,
               l0_w1, l0_as1, l0_ad1, l0_b1, l0_w2, l0_as2, l0_ad2, l0_b2,
               l1_w, l1_b,
               l2_w1, l2_as1, l2_ad1, l2_b1, l2_w2, l2_as2, l2_ad2, l2_b2,
               l3_w, l3_al, l3_ar, l3_wres, out):
    N, D = x.shape
    T = N // P
    KD = D // P
    XP = KD // 2
    EC = src.shape[0] // P
    H0, C0 = l0_as1.shape
    H2, C2 = l2_as1.shape
    H3, C3 = l3_al.shape[1], l3_al.shape[2]
    assert T == 2 and KD % 2 == 0 and C0 == D and H3 * C3 == D and 2 * C3 == P and EC % 2 == 0
    KU = KD // 2
    UNIT = KU * D

    L0 = GatLayer(H0, C0, att=0, head=0, pair=0, w1=0, w2=0, w2_used=0, w1_k=KU, w2_k=KU)
    L2 = GatLayer(H2, C2, att=H0 + 1, head=H0, pair=H0 * L0.pairs, w1=H0, w2=H0 + 1,
                  w2_used=2 * H0, w1_k=KU, w2_k=C2 // P // 2)

    HEAD_PIECES = {D: [(0, BANK), (BANK, D - BANK)], C2: [(0, C2)]}
    ACC_PIECES = [[(0, BANK), (BANK, D - BANK)], [(0, D - BANK), (D - BANK, BANK)]]

    with ExitStack() as ctx:
        def sb(name, shape, dt=F32):
            return ctx.enter_context(nc.sbuf_tensor(name, shape, dt))

        def sem(name):
            return ctx.enter_context(nc.semaphore(name))

        w_raw = sb("w_raw", [P, 4, UNIT])
        w_hi = sb("w_hi", [P, 4, UNIT], F32R)
        w_lo = sb("w_lo", [P, 4, UNIT], F32R)
        x_nat = sb("x_nat", [P, T, D])
        xb = sb("xb", [P, T, D])
        xt_hi = sb("xt_hi", [P, KD, N], F32R)
        xt_lo = sb("xt_lo", [P, KD, N], F32R)
        h_raw = sb("h_raw", [P, T, D])
        h_hi = sb("h_hi", [P, T, D], F32R)
        h_lo = sb("h_lo", [P, T, D], F32R)
        z = sb("z", [P, KD, N])
        z_pos = sb("z_pos", [P, 2, N])
        z_hi = sb("z_hi", [P, KD, N], F32R)
        z_lo = sb("z_lo", [P, KD, N], F32R)
        att_vec = sb("att_vec", [P, 2, D])
        product = sb("product", [P, 2, D], BF16)
        count = sb("count", [P, T, N])
        absent = sb("absent", [P, T, N])
        count_loop = sb("count_loop", [P, T, N])
        absent_loop = sb("absent_loop", [P, T, N])
        conv_t = sb("conv_t", [P, T, N])
        score_src = sb("score_src", [P, T])
        score_dst = sb("score_dst", [P, T])
        score_diag = sb("score_diag", [P, T, P])
        logit = sb("logit", [P, T, N])
        top = sb("top", [P, T])
        neg_top = sb("neg_top", [P, T])
        neg_max = sb("neg_max", [P, T])
        expd = sb("expd", [P, T, N])
        attn = sb("attn", [P, T, N])
        denom = sb("denom", [P, T])
        rdenom = sb("rdenom", [P, T])
        at_hi = sb("at_hi", [P, T, N], F32R)
        at_lo = sb("at_lo", [P, T, N], F32R)
        at_f32 = z_pos[:, :, :]
        NB = L0.heads * L0.blocks + L2.heads * L2.blocks
        bias_col = sb("bias_col", [P, 3, NB])
        bias_now = sb("bias_now", [P, 3, L0.blocks])
        y = z[:, :, :].rearrange("p k n -> p (k n)").rearrange("p (t d) -> p t d", t=T)
        stats = sb("stats", [P, T, 2, 6])
        mean_var = sb("mean_var", [P, T, 2])
        var_eps = sb("var_eps", [P, T])
        rstd = sb("rstd", [P, T])
        minus_half = sb("minus_half", [P, T])
        ident = sb("ident", [P, P])
        ones = sb("ones", [P, P])
        zeros = sb("zeros", [P, P], F32R)
        iota_i = sb("iota_i", [P, N], I32)
        iota_b = sb("iota_b", [P, N], BF16)
        edge_i = sb("edge_i", [P, 2, EC], I32)
        edge_f = sb("edge_f", [P, 2, EC])
        degree = sb("degree", [P, T])
        dinv = sb("dinv", [P, T])
        w3 = sb("w3", [P, P])
        w3res = sb("w3res", [P, P])
        attn3_t = sb("attn3_t", [P, 2 * H3])
        w3_att = sb("w3_att", [P, KD, 2 * H3])
        onehot = h_raw[:, :, :].rearrange("p t d -> p (t d)").bitcast(BF16)[:, 0:2 * 2 * N]\
            .rearrange("p (c e n) -> p c e n", c=2, e=2)
        padded = z[:, :, :].rearrange("p k n -> p (k n)")[:, 0:5 * P].rearrange("p (a n) -> p a n", a=5)
        scratch = w_raw[:, :, :].rearrange("p a n -> p (a n)")
        logit3 = scratch[:, 0:H3 * T * N].rearrange("p (h t n) -> p h t n", h=H3, t=T)
        xt3 = scratch[:, H3 * T * N:H3 * T * N + KD * N].rearrange("p (k n) -> p k n", k=KD)
        spare3 = scratch[:, (H3 * T + KD) * N:(H3 * T + KD + 2 * T) * N].rearrange("p (a t n) -> p a t n", a=2, t=T)
        expd3 = [expd[:, :, :], spare3[:, 0, :, :]]
        attn3 = [attn[:, :, :], spare3[:, 1, :, :]]
        at3 = [z_pos[:, :, :], z[:, 0:2, :]]
        diag3 = [score_diag[:, :, :], z[:, 2, :].rearrange("p (t n) -> p t n", t=T)]
        score3 = sb("score3", [P, T, 2 * H3])
        top3 = sb("top3", [P, H3, T])
        neg_top3 = sb("neg_top3", [P, H3, T])
        neg_max3 = sb("neg_max3", [P, H3, T])
        denom3 = sb("denom3", [P, H3, T])
        rdenom3 = sb("rdenom3", [P, H3, T])

        heads_ps = ctx.enter_context(nc.psum_tensor("heads_ps", [P, 4 * BANK], F32))
        acc_ps = ctx.enter_context(nc.psum_tensor("acc_ps", [P, 3 * BANK], F32))
        misc_ps = ctx.enter_context(nc.psum_tensor("misc_ps", [P, BANK], F32))
        AGG_BANK = [0, 2, 3]

        x_landed = sem("x_landed")
        edges_landed = sem("edges_landed")
        padded_landed = sem("padded_landed")
        bias_landed = sem("bias_landed")
        vec_landed = sem("vec_landed")
        raw_landed = [sem(f"raw_landed{j}") for j in range(4)]
        split_hi = [sem(f"split_hi{j}") for j in range(4)]
        split_lo = [sem(f"split_lo{j}") for j in range(4)]
        consts_zeroed = sem("consts_zeroed")
        consts_ready = sem("consts_ready")
        padded_zeroed = sem("padded_zeroed")
        iota_ready = sem("iota_ready")
        edges_ready = sem("edges_ready")
        onehot_ready = sem("onehot_ready")
        onehot_used = sem("onehot_used")
        count_ready = sem("count_ready")
        degree_ready = sem("degree_ready")
        dinv_ready = sem("dinv_ready")
        conv_scaled = sem("conv_scaled")
        conv_turned = sem("conv_turned")
        conv_ready = sem("conv_ready")
        padded_turned = sem("padded_turned")
        padded_copied = sem("padded_copied")
        w3_scored = sem("w3_scored")
        w3_ready = sem("w3_ready")
        bias_now_ready = sem("bias_now_ready")
        xt_turned = sem("xt_turned")
        xt_hi_ready = sem("xt_hi_ready")
        xt_lo_ready = sem("xt_lo_ready")
        h_done = sem("h_done")
        w2_used = sem("w2_used")
        h_copied = sem("h_copied")
        h_hi_ready = sem("h_hi_ready")
        h_lo_ready = sem("h_lo_ready")
        scores_ready = sem("scores_ready")
        diag_ready = sem("diag_ready")
        scores_spread = sem("scores_spread")
        logit_masked = sem("logit_masked")
        logit_summed = sem("logit_summed")
        logit_ready = sem("logit_ready")
        exp_ready = sem("exp_ready")
        exp_counted = sem("exp_counted")
        rdenom_ready = sem("rdenom_ready")
        attn_ready = sem("attn_ready")
        attn_turned = sem("attn_turned")
        at_hi_ready = sem("at_hi_ready")
        at_lo_ready = sem("at_lo_ready")
        at_f32_ready = sem("at_f32_ready")
        agg_done = sem("agg_done")
        elu_exp = sem("elu_exp")
        elu_pos = sem("elu_pos")
        z_ready = sem("z_ready")
        z_hi_ready = sem("z_hi_ready")
        z_lo_ready = sem("z_lo_ready")
        out_done = sem("out_done")
        y_ready = sem("y_ready")
        stats_ready = sem("stats_ready")
        var_ready = sem("var_ready")
        eps_added = sem("eps_added")
        rstd_ready = sem("rstd_ready")
        x_ready = sem("x_ready")
        xb_ready = sem("xb_ready")
        xt3_ready = sem("xt3_ready")
        score3_done = sem("score3_done")
        ft3_done = sem("ft3_done")
        score3_ready = sem("score3_ready")
        ft3_ready = sem("ft3_ready")
        diag3_ready = sem("diag3_ready")
        spread3_done = sem("spread3_done")
        masked3 = sem("masked3")
        neg_top3_ready = sem("neg_top3_ready")
        neg_max3_ready = sem("neg_max3_ready")
        summed3 = sem("summed3")
        logit3_ready = sem("logit3_ready")
        exp3_ready = sem("exp3_ready")
        counted3 = sem("counted3")
        rdenom3_ready = sem("rdenom3_ready")
        attn3_ready = sem("attn3_ready")
        turned3 = sem("turned3")
        at3_ready = sem("at3_ready")
        agg3_done = sem("agg3_done")
        stored = sem("stored")

        block = ctx.enter_context(nc.Block())

        def pair_ps(ps, p):
            return ps[:, p * BANK:(p + 1) * BANK].rearrange("p (c n) -> p c n", c=2)

        def spread(row, rows=P):
            return row.rearrange("(a n) -> a n", a=1).broadcast_to([rows, row.shape[0]])

        @block.sync
        def _(sp):
            def load_first(L, w1, i):
                w = w1.rearrange("(k p) n -> p k n", p=P)
                for j in range(2):
                    if not (L is L0 and isinstance(i, int) and i == 0):
                        sp.wait_ge(split_lo[j], i + L.w1)
                    sp.dma_start(
                        w_raw[:, j, 0:L.w1_k * L.width].rearrange("p (k n) -> p k n", k=L.w1_k),
                        w[:, j * L.w1_k:(j + 1) * L.w1_k, bass.ds(i * L.width, L.width)],
                    ).then_inc(raw_landed[j], 16)

            def load_second(L, w2, i):
                w = w2.rearrange("(k p) n -> p k n", p=P)
                for j in range(2):
                    if not (L is L0 and isinstance(i, int) and i == 0):
                        sp.wait_ge(split_lo[2 + j], i + L.w2)
                    sp.dma_start(
                        w_raw[:, 2 + j, 0:L.w2_k * D].rearrange("p (k n) -> p k n", k=L.w2_k),
                        w[:, bass.ds(i * L.blocks + j * L.w2_k, L.w2_k), :],
                    ).then_inc(raw_landed[2 + j], 16)

            def load_vectors(L, a_src, a_dst, i):
                width = a_src.shape[1]
                if not (L is L0 and isinstance(i, int) and i == 0):
                    sp.wait_ge(scores_ready, i * 2 * T + 2 * T * L.att)
                for e, a in enumerate((a_src, a_dst)):
                    row = a[bass.ds(i, 1), :] if a.shape[0] > 1 else a[0:1, :]
                    sp.dma_start(att_vec[:, e, 0:width], row.broadcast_to([P, width]))\
                        .then_inc(vec_landed, 16)

            def load_vectors2(L, a_src, a_dst):
                sp.wait_ge(scores_ready, 2 * T * (L.att + L.heads))
                for e, a in enumerate((a_src, a_dst)):
                    sp.dma_start(att_vec[:, e, :], a[0:1, :].broadcast_to([P, D])).then_inc(vec_landed, 16)

            def load_bias(l, b):
                if l:
                    sp.wait_ge(y_ready, T * l)
                for t in range(T):
                    sp.dma_start(xb[:, t, :], spread(b)).then_inc(bias_landed, 16)

            sp.dma_start(x_nat[:, :, :], x.rearrange("(t p) n -> p t n", p=P)).then_inc(x_landed, 16)
            load_first(L0, l0_w1, 0)
            load_vectors(L0, l0_as1, l0_ad1, 0)
            load_second(L0, l0_w2, 0)
            load_bias(0, l0_b2)
            load_first(L0, l0_w1, 1)
            with sp.Fori(1, L0.heads - 1) as i:
                load_vectors(L0, l0_as1, l0_ad1, i)
                load_first(L0, l0_w1, i + 1)
                load_second(L0, l0_w2, i)
            load_vectors(L0, l0_as1, l0_ad1, H0 - 1)
            load_first(L2, l2_w1, 0)
            load_second(L0, l0_w2, H0 - 1)
            load_vectors2(L0, l0_as2, l0_ad2)
            w = l1_w.rearrange("(k p) n -> p k n", p=P)
            for j in range(2):
                sp.wait_ge(split_lo[2 + j], H0)
                sp.dma_start(w_raw[:, 2 + j, :].rearrange("p (k n) -> p k n", k=KU),
                             w[:, j * KU:(j + 1) * KU, :]).then_inc(raw_landed[2 + j], 16)
            load_first(L2, l2_w1, 1)
            load_vectors(L2, l2_as1, l2_ad1, 0)
            load_second(L2, l2_w2, 0)
            load_bias(1, l1_b)
            load_bias(2, l2_b2)
            with sp.Fori(1, L2.heads - 1) as i:
                load_vectors(L2, l2_as1, l2_ad1, i)
                load_first(L2, l2_w1, i + 1)
                load_second(L2, l2_w2, i)
            load_vectors(L2, l2_as1, l2_ad1, H2 - 1)
            load_second(L2, l2_w2, H2 - 1)
            load_vectors2(L2, l2_as2, l2_ad2)
            for t in range(T):
                sp.wait_ge(x_ready, T * 3 + t + 1)
                sp.dma_start(out[t * P:(t + 1) * P, :], x_nat[:, t, :]).then_inc(stored, 16)
            sp.wait_ge(stored, 16 * T)

        @block.scalar
        def _(act):
            act.dma_start(edge_i[:, 0, :], dst.rearrange("(p c) -> p c", p=P)).then_inc(edges_landed, 16)
            act.dma_start(edge_i[:, 1, :], src.rearrange("(p c) -> p c", p=P)).then_inc(edges_landed, 16)
            act.wait_ge(padded_zeroed, 1)
            nb0 = L0.heads * L0.blocks
            nb2 = L2.heads * L2.blocks
            act.dma_start(padded[0:nb0, 0, :], l0_b1.rearrange("(a p) -> a p", p=P)).then_inc(padded_landed, 16)
            act.dma_start(padded[0:nb2, 1, :], l2_b1.rearrange("(a p) -> a p", p=P)).then_inc(padded_landed, 16)
            for c in range(2):
                act.dma_start(padded[0:C3, 2, c * C3:(c + 1) * C3], l3_w).then_inc(padded_landed, 16)
                act.dma_start(padded[0:C3, 3, c * C3:(c + 1) * C3], l3_wres).then_inc(padded_landed, 16)
            act.dma_start(padded[0:H3, 4, 0:C3], l3_al[0, :, :]).then_inc(padded_landed, 16)
            act.dma_start(padded[H3:2 * H3, 4, 0:C3], l3_ar[0, :, :]).then_inc(padded_landed, 16)

            def split_slot(j, use, size):
                act.wait_ge(raw_landed[j], 16 * use + 16)
                act.activation(w_hi[:, j, 0:size], w_raw[:, j, 0:size], ACT.Copy).then_inc(split_hi[j], 1)

            def first_slots(L, i):
                for j in range(2):
                    if not (L is L0 and isinstance(i, int) and i == 0):
                        act.wait_ge(h_done, T * (L.head + i))
                    split_slot(j, i + L.w1, L.w1_k * L.width)

            def second_slot(L, i, j):
                if L is L2 and isinstance(i, int) and i == 0:
                    act.wait_ge(out_done, T * 2)
                elif not (isinstance(i, int) and i == 0):
                    act.wait_ge(w2_used, i * 2 + (L.w2_used - 2 + j + 1))
                split_slot(2 + j, i + L.w2, L.w2_k * D)

            def xt_high(e):
                for p in range(XP):
                    act.wait_ge(xt_turned, XP * e + p + 1)
                    act.activation(xt_hi[:, 2 * p:2 * p + 2, :], pair_ps(acc_ps, p), ACT.Copy)\
                        .then_inc(xt_hi_ready, 1)

            def exps(a):
                act.wait_ge(logit_ready, 2 * a + 2)
                for d in range(T):
                    act.activation(expd[:, d, :], logit[:, d, :], ACT.Exp, bias=neg_max[:, d:d + 1])\
                        .then_inc(exp_ready, 1)

            def head(L, i, next_first):
                a = i + L.att
                first = L is L0 and isinstance(i, int) and i == 0
                for t in range(T):
                    act.wait_ge(h_done, (i + L.head) * T + t + 1)
                    if t == 0 and not first:
                        act.wait_ge(h_lo_ready, i + L.head)
                    act.activation(h_raw[:, t, 0:L.width], heads_ps[:, 2 * t * BANK:2 * t * BANK + L.width],
                                   ACT.Copy).then_inc(h_copied, 1)
                    act.wait_ge(h_copied, a * T + t + 1)
                    act.activation(h_hi[:, t, 0:L.width], h_raw[:, t, 0:L.width], ACT.Copy)\
                        .then_inc(h_hi_ready, 1)
                if next_first is not None:
                    first_slots(*next_first)
                exps(a)
                second_slot(L, i, 0)
                act.wait_ge(attn_turned, a + 1)
                act.activation(at_hi[:, :, :].rearrange("p s n -> p (s n)"), misc_ps[:, :], ACT.Copy)\
                    .then_inc(at_hi_ready, 1)
                act.wait_ge(bias_now_ready, i + (L.head + 1))

                def elu_half(p):
                    g = i * L.pairs + (L.pair + p)
                    act.wait_ge(agg_done, g + 1)
                    if not first:
                        act.wait_ge(z_lo_ready, i * L.pairs + (L.pair + p + 1 - L.pairs))
                    for c in range(2):
                        k = 2 * p + c
                        act.activation(z[:, k, :], pair_ps(heads_ps, AGG_BANK[p])[:, c, :], ACT.Exp,
                                       bias=bias_now[:, 0, k:k + 1]).then_inc(elu_exp, 1)

                def z_high(p):
                    act.wait_ge(z_ready, i * L.pairs + (L.pair + p + 1))
                    act.activation(z_hi[:, 2 * p:2 * p + 2, :], z[:, 2 * p:2 * p + 2, :], ACT.Copy)\
                        .then_inc(z_hi_ready, 1)

                for p in range(L.pairs):
                    elu_half(p)
                    if p:
                        z_high(p - 1)
                z_high(L.pairs - 1)
                second_slot(L, i, 1)

            def second_attention(L):
                a = L.att + L.heads
                act.wait_ge(w2_used, L.w2_used + 2 * L.heads)
                act.wait_ge(h_lo_ready, L.head + L.heads)
                for t in range(T):
                    act.activation(h_raw[:, t, :], acc_ps[:, t * D:(t + 1) * D], ACT.Copy)\
                        .then_inc(h_copied, 1)
                exps(a)
                act.wait_ge(attn_turned, a + 1)
                act.activation(at_f32.rearrange("p s n -> p (s n)"), misc_ps[:, :], ACT.Copy)\
                    .then_inc(at_f32_ready, 1)

            xt_high(0)
            first_slots(L0, 0)
            act.wait_ge(conv_turned, 1)
            act.wait_ge(dinv_ready, 1)
            for s in range(T):
                act.activation(conv_t[:, s, :], pair_ps(heads_ps, 1)[:, s, :], ACT.Copy,
                               scale=dinv[:, s:s + 1]).then_inc(conv_ready, 1)
            head(L0, 0, (L0, 1))
            with act.Fori(1, L0.heads - 1) as i:
                head(L0, i, (L0, i + 1))
            head(L0, L0.heads - 1, (L2, 0))
            for j in range(2):
                act.wait_ge(w2_used, 2 * H0 - 1 + j)
                split_slot(2 + j, H0, UNIT)
            second_attention(L0)
            xt_high(1)
            xt_high(2)
            head(L2, 0, (L2, 1))
            with act.Fori(1, L2.heads - 1) as i:
                head(L2, i, (L2, i + 1))
            head(L2, L2.heads - 1, None)
            second_attention(L2)
            for p in range(XP):
                act.wait_ge(xt_turned, XP * 3 + p + 1)
                act.activation(xt3[:, 2 * p:2 * p + 2, :], pair_ps(acc_ps, p), ACT.Copy).then_inc(xt3_ready, 1)
            act.wait_ge(score3_done, T)
            act.activation(score3[:, :, :].rearrange("p t h -> p (t h)"), misc_ps[:, 0:T * 2 * H3], ACT.Copy)\
                .then_inc(score3_ready, 1)
            act.wait_ge(score3_ready, 1)
            for h in range(H3):
                if h == 2:
                    act.wait_ge(ft3_done, T)
                    for t in range(T):
                        act.activation(h_raw[:, t, :], heads_ps[:, 2 * t * BANK:2 * t * BANK + D], ACT.Copy)\
                            .then_inc(ft3_ready, 1)
                if h >= 2:
                    act.wait_ge(spread3_done, h - 1)
                for s in range(T):
                    act.activation(diag3[h % 2][:, s, :], ident[:, :], ACT.Copy,
                                   scale=score3[:, s, h:h + 1]).then_inc(diag3_ready, 1)
            act.wait_ge(neg_max3_ready, 1)

            def exps3(h):
                act.wait_ge(logit3_ready, h + 1)
                if h >= 2:
                    act.wait_ge(counted3, T * (h - 1))
                for d in range(T):
                    act.activation(expd3[h % 2][:, d, :], logit3[:, h, d, :], ACT.Exp,
                                   bias=neg_max3[:, h, d:d + 1]).then_inc(exp3_ready, 1)

            def at_copy3(h):
                act.wait_ge(turned3, h + 1)
                if h >= 2:
                    act.wait_ge(agg3_done, h - 1)
                act.activation(at3[h % 2].rearrange("p s n -> p (s n)"),
                               heads_ps[:, (2 + h % 2) * BANK:(3 + h % 2) * BANK], ACT.Copy)\
                    .then_inc(at3_ready, 1)

            for h in range(H3 + 2):
                if h < H3:
                    exps3(h)
                if h >= 2:
                    at_copy3(h - 2)

        @block.gpsimd
        def _(pool):
            pool.memset(z[:, :, :], 0.0).then_inc(padded_zeroed, 1)
            pool.iota(iota_i[:, :], pattern=[[1, N]], base=0, channel_multiplier=0).then_inc(iota_ready, 1)
            pool.memset(ident[:, :], 0.0).then_inc(consts_zeroed, 1)
            pool.memset(ones[:, :], 1.0)
            pool.memset(zeros[:, :].bitcast(F32), 0.0)
            pool.memset(w3[:, :], 0.0)
            pool.memset(w3res[:, :], 0.0)
            pool.memset(w3_att[:, :, :], 0.0)
            pool.memset(minus_half[:, :], -0.5)
            pool.wait_ge(consts_zeroed, 1)
            pool.affine_select(out=ident[:, :], in_=ident[:, :], compare_op=ALU.not_equal, fill=1.0,
                               base=0, pattern=[[-1, P]], channel_multiplier=1).then_inc(consts_ready, 1)

            def low_slot(j, use, size):
                pool.wait_ge(split_hi[j], use + 1)
                pool.tensor_tensor(w_lo[:, j, 0:size], w_raw[:, j, 0:size], w_hi[:, j, 0:size].bitcast(F32),
                                   ALU.subtract).then_inc(split_lo[j], 1)

            def head(L, i, next_first):
                if next_first is not None:
                    Ln, n = next_first
                    low_slot(1, n + Ln.w1, Ln.w1_k * Ln.width)
                for p in range(L.pairs):
                    pool.wait_ge(z_hi_ready, i * L.pairs + (L.pair + p + 1))
                    ks = slice(2 * p, 2 * p + 2)
                    pool.tensor_tensor(z_lo[:, ks, :], z[:, ks, :], z_hi[:, ks, :].bitcast(F32),
                                       ALU.subtract).then_inc(z_lo_ready, 1)
                low_slot(3, i + L.w2, L.w2_k * D)

            def rstd_of(l):
                for t in range(T):
                    pool.wait_ge(var_ready, T * l + t + 1)
                    pool.tensor_scalar(var_eps[:, t:t + 1], mean_var[:, t, 1:2], LN_EPS, None, ALU.add)\
                        .then_inc(eps_added, 1)
                    pool.wait_ge(eps_added, T * l + t + 1)
                    pool.tensor_tensor(rstd[:, t:t + 1], var_eps[:, t:t + 1], minus_half[:, t:t + 1], ALU.pow)\
                        .then_inc(rstd_ready, 1)

            def add_bias(l):
                pool.wait_ge(bias_landed, 16 * T * (l + 1))
                for t in range(T):
                    if l:
                        pool.wait_ge(x_ready, T * (l - 1) + t + 1)
                    pool.tensor_tensor(xb[:, t, :], xb[:, t, :], x_nat[:, t, :], ALU.add)\
                        .then_inc(xb_ready, 1)

            pool.wait_ge(degree_ready, 1)
            pool.tensor_tensor(dinv[:, :], degree[:, :], minus_half[:, :], ALU.pow).then_inc(dinv_ready, 1)
            low_slot(1, 0, UNIT)
            pool.wait_ge(x_landed, 16)
            add_bias(0)
            head(L0, 0, (L0, 1))
            with pool.Fori(1, L0.heads - 1) as i:
                head(L0, i, (L0, i + 1))
            head(L0, L0.heads - 1, (L2, 0))
            low_slot(3, H0, UNIT)
            rstd_of(0)
            add_bias(1)
            rstd_of(1)
            add_bias(2)
            head(L2, 0, (L2, 1))
            with pool.Fori(1, L2.heads - 1) as i:
                head(L2, i, (L2, i + 1))
            head(L2, L2.heads - 1, None)
            rstd_of(2)
            for h in range(H3):
                pool.wait_ge(rdenom3_ready, h + 1)
                if h >= 2:
                    pool.wait_ge(turned3, h - 1)
                for d in range(T):
                    pool.tensor_scalar(attn3[h % 2][:, d, :], attn3[h % 2][:, d, :], rdenom3[:, h, d:d + 1],
                                       None, ALU.mult).then_inc(attn3_ready, 1)
            rstd_of(3)

        @block.vector
        def _(dve):
            def low_slot(j, use, size):
                dve.wait_ge(split_hi[j], use + 1)
                dve.tensor_tensor(w_lo[:, j, 0:size], w_raw[:, j, 0:size], w_hi[:, j, 0:size].bitcast(F32),
                                  ALU.subtract).then_inc(split_lo[j], 1)

            def xt_low(e):
                for p in range(XP):
                    dve.wait_ge(xt_hi_ready, XP * e + p + 1)
                    ks = slice(2 * p, 2 * p + 2)
                    dve.tensor_tensor(xt_lo[:, ks, :], pair_ps(acc_ps, p), xt_hi[:, ks, :].bitcast(F32),
                                      ALU.subtract).then_inc(xt_lo_ready, 1)

            def attention(a, width, masks, low_h):
                counts, missing = masks
                dve.wait_ge(vec_landed, a * 32 + 32)
                for t in range(T):
                    dve.wait_ge(h_copied, a * T + t + 1)
                    for e, score in enumerate((score_src, score_dst)):
                        if t:
                            dve.wait_ge(scores_ready, a * 2 * T + e + 1)
                        dve.tensor_tensor_reduce(product[:, e, 0:width], h_raw[:, t, 0:width],
                                                 att_vec[:, e, 0:width], 1.0, 0.0, ALU.mult, ALU.add,
                                                   score[:, t:t + 1]).then_inc(scores_ready, 1)
                dve.wait_ge(scores_ready, a * 2 * T + 2 * T)
                for t in range(T):
                    ins = dve.tensor_scalar(score_diag[:, t, :], ident[:, :], score_src[:, t:t + 1], None, ALU.mult)
                ins.then_inc(diag_ready, 1)
                if low_h is not None:
                    low_h()
                else:
                    dve.wait_ge(scores_spread, a + 1)
                for d in range(T):
                    ins = dve.tensor_tensor_reduce(logit[:, d, :], misc_ps[:, 0:N], missing[:, d, :], 1.0, -3e38,
                                                   ALU.add, ALU.max, top[:, d:d + 1])
                ins.then_inc(logit_masked, 1)
                dve.wait_ge(logit_masked, a + 1)
                dve.scalar_tensor_tensor(neg_top[:, :], top[:, :], -1.0, score_dst[:, :], ALU.mult, ALU.subtract)
                for d in range(T):
                    ins = dve.tensor_scalar(logit[:, d, :], logit[:, d, :], score_dst[:, d:d + 1], None, ALU.add)
                ins.then_inc(logit_summed, 1)
                dve.wait_ge(logit_summed, a + 1)
                dve.scalar_tensor_tensor(neg_max[:, :], neg_top[:, :], NEG_SLOPE, neg_top[:, :], ALU.mult, ALU.min)\
                    .then_inc(logit_ready, 1)
                dve.scalar_tensor_tensor(logit[:, :, :], logit[:, :, :], NEG_SLOPE, logit[:, :, :], ALU.mult, ALU.max)\
                    .then_inc(logit_ready, 1)
                for d in range(T):
                    dve.wait_ge(exp_ready, a * T + d + 1)
                    ins = dve.tensor_tensor_reduce(attn[:, d, :], expd[:, d, :], counts[:, d, :], 1.0, ATT_EPS,
                                                   ALU.mult, ALU.add, denom[:, d:d + 1])
                ins.then_inc(exp_counted, 1)
                dve.wait_ge(exp_counted, a + 1)
                dve.reciprocal(rdenom[:, :], denom[:, :]).then_inc(rdenom_ready, 1)

            def head(L, i, masks, next_first):
                a = i + L.att
                first = L is L0 and isinstance(i, int) and i == 0
                nb = 0 if L is L0 else L0.heads * L0.blocks
                dve.tensor_copy(bias_now[:, :, 0:L.blocks], bias_col[:, :, bass.ds(i * L.blocks + nb, L.blocks)])\
                    .then_inc(bias_now_ready, 1)

                def low_h():
                    for t in range(T):
                        dve.wait_ge(h_hi_ready, (i + L.head) * T + t + 1)
                        if t == T - 1:
                            dve.wait_ge(scores_spread, a + 1)
                        ins = dve.tensor_tensor(h_lo[:, t, 0:L.width], h_raw[:, t, 0:L.width],
                                                h_hi[:, t, 0:L.width].bitcast(F32), ALU.subtract)
                    ins.then_inc(h_lo_ready, 1)

                attention(a, L.width, masks, low_h)
                dve.wait_ge(rdenom_ready, a + 1)
                for d in range(T):
                    ins = dve.tensor_scalar(attn[:, d, :], attn[:, d, :], rdenom[:, d:d + 1], None, ALU.mult)
                ins.then_inc(attn_ready, 1)
                dve.wait_ge(at_hi_ready, i + (L.head + 1))
                dve.tensor_tensor(at_lo[:, :, :].rearrange("p s n -> p (s n)"), misc_ps[:, :],
                                  at_hi[:, :, :].rearrange("p s n -> p (s n)").bitcast(F32), ALU.subtract)\
                    .then_inc(at_lo_ready, 1)
                if next_first is not None:
                    Ln, n = next_first
                    low_slot(0, n + Ln.w1, Ln.w1_k * Ln.width)
                for p in range(L.pairs):
                    dve.wait_ge(elu_exp, i * (2 * L.pairs) + 2 * (L.pair + p + 1))
                    if p:
                        dve.wait_ge(z_ready, i * L.pairs + (L.pair + p))
                    for c in range(2):
                        k = 2 * p + c
                        ins = dve.tensor_scalar(z_pos[:, c, :], pair_ps(heads_ps, AGG_BANK[p])[:, c, :],
                                                bias_now[:, 1, k:k + 1], bias_now[:, 2, k:k + 1], ALU.max, ALU.add)
                    ins.then_inc(elu_pos, 1)
                    dve.wait_ge(elu_pos, i * L.pairs + (L.pair + p + 1))
                    ks = slice(2 * p, 2 * p + 2)
                    dve.scalar_tensor_tensor(z[:, ks, :], z[:, ks, :], 1.0, z_pos[:, :, :], ALU.min, ALU.add)\
                        .then_inc(z_ready, 1)
                low_slot(2, i + L.w2, L.w2_k * D)

            def layer_norm(l, sum_tile):
                for t in range(T):
                    if l < 3:
                        dve.wait_ge(out_done, T * l + t + 1)
                    sum_tile(t).then_inc(y_ready, 1)
                    dve.wait_ge(y_ready, T * l + t + 1)
                    for c in range(2):
                        ins = dve.bn_stats(stats[:, t, c, :], y[:, t, c * (D // 2):(c + 1) * (D // 2)])
                    ins.then_inc(stats_ready, 1)
                    dve.wait_ge(stats_ready, T * l + t + 1)
                    dve.bn_aggr(mean_var[:, t, :], stats[:, t, :, :].rearrange("p c s -> p (c s)"))\
                        .then_inc(var_ready, 1)
                for t in range(T):
                    dve.wait_ge(rstd_ready, T * l + t + 1)
                    dve.tensor_scalar(x_nat[:, t, :], y[:, t, :], mean_var[:, t, 0:1], rstd[:, t:t + 1],
                                      ALU.subtract, ALU.mult).then_inc(x_ready, 1)

            def second_attention(L, l, masks):
                attention(L.att + L.heads, D, masks, None)
                dve.wait_ge(rdenom_ready, L.att + L.heads + 1)
                dve.wait_ge(xb_ready, T * (l + 1))

                def attended(t):
                    return dve.scalar_tensor_tensor(y[:, t, :], heads_ps[:, 2 * t * BANK:2 * t * BANK + D],
                                                    rdenom[:, t:t + 1], xb[:, t, :], ALU.mult, ALU.add)

                layer_norm(l, attended)

            dve.wait_ge(iota_ready, 1)
            dve.tensor_copy(iota_b[:, :], iota_i[:, :])
            dve.wait_ge(edges_landed, 32)
            dve.tensor_copy(edge_f[:, :, :], edge_i[:, :, :]).then_inc(edges_ready, 1)
            dve.wait_ge(edges_ready, 1)

            def onehots(c, b):
                for e in range(2):
                    ins = dve.tensor_scalar(onehot[:, b, e, :], iota_b[:, :], edge_f[:, e, bass.ds(c, 1)], None,
                                            ALU.is_equal)
                ins.then_inc(onehot_ready, 1)

            for b in range(2):
                onehots(b, b)
            with dve.Fori(1, EC // 2) as c:
                for b in range(2):
                    dve.wait_ge(onehot_used, c * 2 + (b - 1))
                    onehots(c * 2 + b, b)
            xt_low(0)
            dve.wait_ge(onehot_used, EC)
            dve.tensor_copy(count[:, :, :].rearrange("p t n -> p (t n)"), misc_ps[:, :]).then_inc(count_ready, 1)
            dve.wait_ge(count_ready, 1)
            dve.wait_ge(consts_ready, 1)
            dve.tensor_scalar(absent[:, :, :], count[:, :, :], 0.0, MASKED, ALU.is_equal, ALU.mult)
            dve.tensor_copy(count_loop[:, :, :], count[:, :, :]).then_inc(count_ready, 1)
            dve.wait_ge(count_ready, 2)
            for t in range(T):
                diagonal = count_loop[:, t, t * P:(t + 1) * P]
                ins = dve.tensor_tensor(diagonal, diagonal, ident[:, :], ALU.add)
            ins.then_inc(count_ready, 1)
            dve.wait_ge(count_ready, 3)
            dve.tensor_scalar(absent_loop[:, :, :], count_loop[:, :, :], 0.0, MASKED, ALU.is_equal, ALU.mult)
            dve.tensor_reduce(degree[:, :], count_loop[:, :, :], mybir.AxisListType.X, ALU.add)\
                .then_inc(degree_ready, 1)
            low_slot(0, 0, UNIT)
            dve.wait_ge(dinv_ready, 1)
            for t in range(T):
                ins = dve.tensor_scalar(attn[:, t, :], count_loop[:, t, :], dinv[:, t:t + 1], None, ALU.mult)
            ins.then_inc(conv_scaled, 1)
            nb0 = L0.heads * L0.blocks
            dve.wait_ge(padded_turned, 1)
            dve.tensor_copy(bias_col[:, 0, 0:nb0], acc_ps[:, 0:nb0])
            dve.tensor_copy(bias_col[:, 0, nb0:NB], acc_ps[:, P:P + NB - nb0])
            for c in range(2):
                q = slice(c * C3, (c + 1) * C3)
                dve.tensor_copy(w3[q, q], acc_ps[q, 2 * P:2 * P + C3])
                dve.tensor_copy(w3res[q, q], acc_ps[q, 3 * P:3 * P + C3])
            dve.tensor_copy(attn3_t[:, :], acc_ps[:, BANK:BANK + 2 * H3]).then_inc(padded_copied, 1)
            dve.wait_ge(padded_copied, 1)
            dve.tensor_scalar(bias_col[:, 1, :], bias_col[:, 0, :], -1.0, None, ALU.mult)
            dve.tensor_scalar(bias_col[:, 2, :], bias_col[:, 0, :], -1.0, None, ALU.add).then_inc(padded_copied, 1)
            dve.wait_ge(w3_scored, 1)
            for k in range(KD):
                for c in range(2):
                    h = 2 * k + c
                    q = slice(c * C3, (c + 1) * C3)
                    ins = dve.tensor_copy(w3_att[q, k, h:h + H3 + 1:H3], acc_ps[q, BANK + 2 * P + h:BANK + 2 * P + h + H3 + 1:H3])
            ins.then_inc(w3_ready, 1)
            dve.wait_ge(padded_copied, 2)

            plain, looped = (count, absent), (count_loop, absent_loop)
            head(L0, 0, plain, (L0, 1))
            with dve.Fori(1, L0.heads - 1) as i:
                head(L0, i, plain, (L0, i + 1))
            head(L0, L0.heads - 1, plain, (L2, 0))
            low_slot(2, H0, UNIT)
            second_attention(L0, 0, plain)
            xt_low(1)
            dve.wait_ge(xb_ready, T * 2)
            layer_norm(1, lambda t: dve.tensor_tensor(y[:, t, :], heads_ps[:, 2 * t * BANK:2 * t * BANK + D],
                                                      xb[:, t, :], ALU.add))
            xt_low(2)
            head(L2, 0, looped, (L2, 1))
            with dve.Fori(1, L2.heads - 1) as i:
                head(L2, i, looped, (L2, i + 1))
            head(L2, L2.heads - 1, looped, None)
            second_attention(L2, 2, looped)
            for h in range(H3):
                dve.wait_ge(spread3_done, h + 1)
                spread3 = misc_ps[:, 0:N] if h % 2 == 0 else heads_ps[:, 3 * BANK:3 * BANK + N]
                for d in range(T):
                    ins = dve.tensor_tensor_reduce(logit3[:, h, d, :], spread3, absent[:, d, :], 1.0, -3e38,
                                                   ALU.add, ALU.max, top3[:, h, d:d + 1])
                ins.then_inc(masked3, 1)
            score3_dst = score3[:, :, H3:2 * H3].rearrange("p t h -> p h t")
            dve.wait_ge(masked3, H3)
            dve.scalar_tensor_tensor(neg_top3[:, :, :], top3[:, :, :], -1.0, score3_dst, ALU.mult, ALU.subtract)\
                .then_inc(neg_top3_ready, 1)
            dve.wait_ge(neg_top3_ready, 1)
            dve.scalar_tensor_tensor(neg_max3[:, :, :], neg_top3[:, :, :], NEG_SLOPE, neg_top3[:, :, :],
                                     ALU.mult, ALU.min).then_inc(neg_max3_ready, 1)

            def logits3(h):
                for d in range(T):
                    ins = dve.tensor_scalar(logit3[:, h, d, :], logit3[:, h, d, :],
                                            score3[:, d, H3 + h:H3 + h + 1], None, ALU.add)
                ins.then_inc(summed3, 1)
                dve.wait_ge(summed3, h + 1)
                dve.scalar_tensor_tensor(logit3[:, h, :, :], logit3[:, h, :, :], NEG_SLOPE, logit3[:, h, :, :],
                                         ALU.mult, ALU.max).then_inc(logit3_ready, 1)

            def count3(h):
                if h >= 2:
                    dve.wait_ge(turned3, h - 1)
                for d in range(T):
                    dve.wait_ge(exp3_ready, T * h + d + 1)
                    dve.tensor_tensor_reduce(attn3[h % 2][:, d, :], expd3[h % 2][:, d, :], count[:, d, :], 1.0,
                                             ATT_EPS, ALU.mult, ALU.add, denom3[:, h, d:d + 1]).then_inc(counted3, 1)
                dve.wait_ge(counted3, T * (h + 1))
                dve.reciprocal(rdenom3[:, h, :], denom3[:, h, :]).then_inc(rdenom3_ready, 1)

            for h in range(H3 + 1):
                if h < H3:
                    logits3(h)
                if h >= 1:
                    count3(h - 1)
            dve.wait_ge(agg3_done, H3)
            layer_norm(3, lambda t: dve.scalar_tensor_tensor(y[:, t, :], acc_ps[:, t * D:(t + 1) * D], 0.0,
                                                             x_nat[:, t, :], ALU.max, ALU.add))

        @block.tensor
        def _(pe):
            def product_d(slots, width, use, per_slot):
                for t in range(T):
                    for k in range(KD):
                        j = slots + k // per_slot
                        o = (k % per_slot) * width
                        if t == 0 and k % per_slot == 0:
                            pe.wait_ge(split_lo[j], use + 1)
                        tile_k = slice(t * P, (t + 1) * P)
                        for x_part, w_parts in ((xt_hi, (w_hi, w_lo)), (xt_lo, (w_hi,))):
                            for w_part in w_parts:
                                for at, size in HEAD_PIECES[width]:
                                    ins = pe.matmul(heads_ps[:, 2 * t * BANK + at:2 * t * BANK + at + size],
                                                    x_part[:, k, tile_k], w_part[:, j, o + at:o + at + size],
                                                    start=(k == 0 and x_part is xt_hi and w_part is w_hi),
                                                    stop=(k == KD - 1 and x_part is xt_lo))
                    yield ins

            def product_z(L, i, ks):
                for k in ks:
                    j = 2 + k // L.w2_k
                    o = (k % L.w2_k) * D
                    if k % 2 == 0:
                        pe.wait_ge(z_lo_ready, i * L.pairs + (L.pair + k // 2 + 1))
                    if k % L.w2_k == 0:
                        pe.wait_ge(split_lo[j], i + (L.w2 + 1))
                    for t in range(T):
                        for z_part, w_parts in ((z_hi, (w_hi, w_lo)), (z_lo, (w_hi,))):
                            for w_part in w_parts:
                                for at, size in ACC_PIECES[t]:
                                    ins = pe.matmul(acc_ps[:, t * D + at:t * D + at + size],
                                                    z_part[:, k, t * P:(t + 1) * P],
                                                    w_part[:, j, o + at:o + at + size],
                                                    start=False, stop=False, skip_group_check=True)
                    if k % L.w2_k == L.w2_k - 1:
                        ins.then_inc(w2_used, 1)

            def spread_scores(a):
                pe.wait_ge(diag_ready, a + 1)
                pe.matmul(misc_ps[:, 0:N], ones[:, :], score_diag[:, :, :].rearrange("p t n -> p (t n)"),
                          start=True, stop=True).then_inc(scores_spread, 1)

            def turn_attention(a, ready, value):
                pe.wait_ge(ready, value)
                for s in range(T):
                    for d in range(T):
                        o = s * N + d * P
                        ins = pe.transpose(misc_ps[:, o:o + P], attn[:, d, s * P:(s + 1) * P], ident[:, :])
                ins.then_inc(attn_turned, 1)

            def head(L, i):
                a = i + L.att
                first = L is L0 and isinstance(i, int) and i == 0
                fresh = isinstance(i, int) and i == 0
                if not fresh:
                    pe.wait_ge(z_ready, i * L.pairs + (L.pair + 1 - L.pairs))
                for t, ins in enumerate(product_d(0, L.width, i + L.w1, L.w1_k)):
                    ins.then_inc(h_done, 1)
                    if t == 0 and not fresh:
                        pe.wait_ge(z_ready, i * L.pairs + L.pair)
                if not fresh:
                    product_z(L, i - 1, range(0, 2))
                spread_scores(a)
                if not fresh:
                    product_z(L, i - 1, range(2, L.blocks - 1))
                turn_attention(a, attn_ready, i + (L.head + 1))
                if not fresh:
                    product_z(L, i - 1, range(L.blocks - 1, L.blocks))
                pe.wait_ge(h_lo_ready, i + (L.head + 1))
                pe.wait_ge(at_lo_ready, i + (L.head + 1))
                for p in range(L.pairs):
                    for c in range(2):
                        block_k = slice((2 * p + c) * P, (2 * p + c + 1) * P)
                        for s in range(T):
                            for h_part, a_part in ((h_hi, at_hi), (h_hi, at_lo), (h_lo, at_hi)):
                                ins = pe.matmul(pair_ps(heads_ps, AGG_BANK[p])[:, c, :], h_part[:, s, block_k],
                                                a_part[:, s, :], start=(s == 0 and a_part is at_hi and h_part is h_hi),
                                                stop=(s == T - 1 and h_part is h_lo))
                    ins.then_inc(agg_done, 1)

            def clear_sums():
                for b in range(3):
                    pe.matmul(acc_ps[:, b * BANK:(b + 1) * BANK], zeros[:, :],
                              xt_hi[:, 0:2, :].rearrange("p k n -> p (k n)"), start=True, stop=False,
                              skip_group_check=True)

            def second_attention(L, l):
                a = L.att + L.heads
                spread_scores(a)
                turn_attention(a, rdenom_ready, a + 1)
                pe.wait_ge(at_f32_ready, l // 2 + 1)
                for t in range(T):
                    for s in range(T):
                        for at, size in HEAD_PIECES[D]:
                            ins = pe.matmul(heads_ps[:, 2 * t * BANK + at:2 * t * BANK + at + size],
                                            at_f32[:, s, t * P:(t + 1) * P], h_raw[:, s, at:at + size],
                                            start=(s == 0), stop=(s == T - 1))
                    ins.then_inc(out_done, 1)

            def turn_x():
                for p in range(XP):
                    for c in range(2):
                        k = 2 * p + c
                        for t in range(T):
                            ins = pe.transpose(pair_ps(acc_ps, p)[:, c, t * P:(t + 1) * P],
                                               x_nat[:, t, k * P:(k + 1) * P], ident[:, :])
                    ins.then_inc(xt_turned, 1)

            pe.wait_ge(x_landed, 16)
            pe.wait_ge(consts_ready, 1)
            turn_x()

            def count_chunk(b, start, stop):
                for t in range(T):
                    ins = pe.matmul(misc_ps[:, t * N:(t + 1) * N], onehot[:, b, 0, t * P:(t + 1) * P],
                                    onehot[:, b, 1, :], start=start and t == 0, stop=stop and t == T - 1,
                                    skip_group_check=True)
                return ins

            for b in range(2):
                pe.wait_ge(onehot_ready, b + 1)
                count_chunk(b, b == 0, False).then_inc(onehot_used, 1)
            with pe.Fori(1, EC // 2) as c:
                for b in range(2):
                    pe.wait_ge(onehot_ready, c * 2 + (b + 1))
                    count_chunk(b, False, False).then_inc(onehot_used, 1)
            pe.wait_ge(padded_landed, 16 * 8)
            pe.wait_ge(xt_lo_ready, XP)
            for n in range(5):
                ins = pe.transpose(acc_ps[:, n * P:(n + 1) * P], padded[:, n, :], ident[:, :])
            ins.then_inc(padded_turned, 1)
            pe.wait_ge(conv_scaled, 1)
            for s in range(T):
                for d in range(T):
                    o = BANK + s * N + d * P
                    ins = pe.transpose(heads_ps[:, o:o + P], attn[:, d, s * P:(s + 1) * P], ident[:, :])
            ins.then_inc(conv_turned, 1)
            pe.wait_ge(padded_copied, 1)
            pe.matmul(acc_ps[:, BANK + 2 * P:BANK + 2 * P + 2 * H3], padded[:, 2, :], attn3_t[:, :],
                      start=True, stop=True).then_inc(w3_scored, 1)
            pe.wait_ge(w3_ready, 1)
            pe.wait_ge(conv_ready, T)

            clear_sums()
            head(L0, 0)
            with pe.Fori(1, L0.heads) as i:
                head(L0, i)
            product_z(L0, L0.heads - 1, range(L0.blocks))
            second_attention(L0, 0)
            pe.wait_ge(x_ready, T)
            for p in range(XP):
                for c in range(2):
                    k = 2 * p + c
                    for s in range(T):
                        ins = pe.matmul(pair_ps(acc_ps, p)[:, c, :], x_nat[:, s, k * P:(k + 1) * P],
                                        conv_t[:, s, :], start=(s == 0), stop=(s == T - 1))
                ins.then_inc(xt_turned, 1)
            pe.wait_ge(xt_lo_ready, XP * 2)
            for ins in product_d(2, D, H0, KU):
                ins.then_inc(out_done, 1)
            pe.wait_ge(x_ready, T * 2)
            turn_x()
            pe.wait_ge(xt_lo_ready, XP * 3)
            clear_sums()
            head(L2, 0)
            with pe.Fori(1, L2.heads) as i:
                head(L2, i)
            product_z(L2, L2.heads - 1, range(L2.blocks))
            second_attention(L2, 2)
            pe.wait_ge(x_ready, T * 3)
            turn_x()
            pe.wait_ge(xt3_ready, XP)
            for t in range(T):
                for k in range(KD):
                    o = t * 2 * H3
                    ins = pe.matmul(misc_ps[:, o:o + 2 * H3], xt3[:, k, t * P:(t + 1) * P], w3_att[:, k, :],
                                    start=(k == 0), stop=(k == KD - 1))
                ins.then_inc(score3_done, 1)

            for t in range(T):
                for k in range(KD):
                    o = 2 * t * BANK + k * P
                    ins = pe.matmul(heads_ps[:, o:o + P], xt3[:, k, t * P:(t + 1) * P], w3[:, :],
                                    start=True, stop=True)
                ins.then_inc(ft3_done, 1)
            for t in range(T):
                for k in range(KD):
                    o = t * D + k * P
                    pe.matmul(acc_ps[:, o:o + P], xt3[:, k, t * P:(t + 1) * P], w3res[:, :],
                              start=(o % BANK == 0), stop=False, skip_group_check=True)
            for h in range(H3):
                spread3 = misc_ps[:, 0:N] if h % 2 == 0 else heads_ps[:, 3 * BANK:3 * BANK + N]
                if h >= 2:
                    pe.wait_ge(masked3, h - 1)
                if h == 1:
                    pe.wait_ge(ft3_ready, T)
                pe.wait_ge(diag3_ready, T * (h + 1))
                pe.matmul(spread3, ones[:, :], diag3[h % 2].rearrange("p t n -> p (t n)"),
                          start=True, stop=True).then_inc(spread3_done, 1)

            def turn3(h):
                pe.wait_ge(attn3_ready, T * (h + 1))
                if h >= 2:
                    pe.wait_ge(at3_ready, h - 1)
                for s in range(T):
                    for d in range(T):
                        o = (2 + h % 2) * BANK + s * N + d * P
                        ins = pe.transpose(heads_ps[:, o:o + P], attn3[h % 2][:, d, s * P:(s + 1) * P], ident[:, :])
                ins.then_inc(turned3, 1)

            def aggregate3(h):
                pe.wait_ge(at3_ready, h + 1)
                for t in range(T):
                    for s in range(T):
                        o = t * D + h * C3
                        ins = pe.matmul(acc_ps[:, o:o + C3], at3[h % 2][:, s, t * P:(t + 1) * P],
                                        h_raw[:, s, h * C3:(h + 1) * C3], start=False, stop=False,
                                        skip_group_check=True)
                ins.then_inc(agg3_done, 1)

            for h in range(H3 + 1):
                if h < H3:
                    turn3(h)
                if h >= 1:
                    aggregate3(h - 1)


_INS = ["x", "src", "dst",
        "L0_gnn_W1", "L0_gnn_a_src1", "L0_gnn_a_dst1", "L0_gnn_b1",
        "L0_gnn_W2", "L0_gnn_a_src2", "L0_gnn_a_dst2", "L0_gnn_b2",
        "L1_gnn_W", "L1_gnn_b",
        "L2_gnn_W1", "L2_gnn_att_src1", "L2_gnn_att_dst1", "L2_gnn_b1",
        "L2_gnn_W2", "L2_gnn_att_src2", "L2_gnn_att_dst2", "L2_gnn_b2",
        "L3_gnn_W", "L3_gnn_attn_l", "L3_gnn_attn_r", "L3_gnn_W_res"]


def kernel(**inputs):
    import numpy as np
    import concourse.bacc as bacc
    from concourse.bass_utils import run_bass_kernel_spmd

    nc = bacc.Bacc("TRN2", target_bir_lowering=False, num_devices=1)
    arrays, args = {}, []
    for name in _INS:
        a = np.ascontiguousarray(inputs[name])
        arrays[f"in_{name}"] = a
        args.append(nc.dram_tensor(f"in_{name}", a.shape, mybir.dt.from_np(a.dtype), kind="ExternalInput").ap())
    out = nc.dram_tensor("out", inputs["x"].shape, F32, kind="ExternalOutput").ap()
    gnn_kernel(nc, *args, out)
    return run_bass_kernel_spmd(nc, [arrays], core_ids=[0]).results[0]["out"]
```

```python
from contextlib import ExitStack

import concourse.bass as bass
from concourse import mybir

F32 = mybir.dt.float32
F32R = mybir.dt.float32r
BF16 = mybir.dt.bfloat16
I32 = mybir.dt.int32
ALU = mybir.AluOpType
ACT = mybir.ActivationFunctionType

P = 128
BANK = 512
NEG_SLOPE = 0.2
ATT_EPS = 1e-16
LN_EPS = 1e-5
MASKED = -1e30


class GatLayer:

    def __init__(self, heads, width, att, head, pair, w1, w2, w2_used, w1_k, w2_k):
        self.heads, self.width = heads, width
        self.att, self.head, self.pair = att, head, pair
        self.w1, self.w2, self.w2_used = w1, w2, w2_used
        self.w1_k, self.w2_k = w1_k, w2_k
        self.blocks = width // P
        self.pairs = self.blocks // 2


def gnn_kernel(nc, x, src, dst,
               l0_w1, l0_as1, l0_ad1, l0_b1, l0_w2, l0_as2, l0_ad2, l0_b2,
               l1_w, l1_b,
               l2_w1, l2_as1, l2_ad1, l2_b1, l2_w2, l2_as2, l2_ad2, l2_b2,
               l3_w, l3_al, l3_ar, l3_wres, out):
    N, D = x.shape
    T = N // P
    KD = D // P
    XP = KD // 2
    EC = src.shape[0] // P
    H0, C0 = l0_as1.shape
    H2, C2 = l2_as1.shape
    H3, C3 = l3_al.shape[1], l3_al.shape[2]
    assert T == 2 and KD % 2 == 0 and C0 == D and H3 * C3 == D and 2 * C3 == P and EC % 2 == 0
    KU = KD // 2
    UNIT = KU * D
    RING = T * D // N
    LEAD = EC % RING + RING

    L0 = GatLayer(H0, C0, att=0, head=0, pair=0, w1=0, w2=0, w2_used=0, w1_k=KU, w2_k=KU)
    L2 = GatLayer(H2, C2, att=H0 + 1, head=H0, pair=H0 * L0.pairs, w1=H0, w2=H0 + 1,
                  w2_used=2 * H0, w1_k=KU, w2_k=C2 // P // 2)

    HEAD_PIECES = {D: [(0, BANK), (BANK, D - BANK)], C2: [(0, C2)]}
    HEAD_AT = {D: 0, C2: BANK}
    ACC_PIECES = [[(0, BANK), (BANK, D - BANK)], [(0, D - BANK), (D - BANK, BANK)]]

    with ExitStack() as ctx:
        def sb(name, shape, dt=F32):
            return ctx.enter_context(nc.sbuf_tensor(name, shape, dt))

        def sem(name):
            return ctx.enter_context(nc.semaphore(name))

        w_raw = sb("w_raw", [P, 4, UNIT])
        w_hi = sb("w_hi", [P, 4, UNIT], F32R)
        w_lo = sb("w_lo", [P, 4, UNIT], F32R)
        x_nat = sb("x_nat", [P, T, D])
        xb = sb("xb", [P, T, D])
        xt_hi = sb("xt_hi", [P, KD, N], F32R)
        xt_lo = sb("xt_lo", [P, KD, N], F32R)
        h_raw = sb("h_raw", [P, T, D])
        h_hi = sb("h_hi", [P, T, D], F32R)
        h_lo = sb("h_lo", [P, T, D], F32R)
        z = sb("z", [P, KD, N])
        z_pos = sb("z_pos", [P, 2, N])
        z_hi = sb("z_hi", [P, KD, N], F32R)
        z_lo = sb("z_lo", [P, KD, N], F32R)
        att_vec = sb("att_vec", [P, 2, D])
        product = sb("product", [P, 2, D], BF16)
        count = sb("count", [P, T, N])
        absent = sb("absent", [P, T, N])
        count_loop = sb("count_loop", [P, T, N])
        absent_loop = sb("absent_loop", [P, T, N])
        conv_t = sb("conv_t", [P, T, N])
        score_src = sb("score_src", [P, T])
        score_dst = sb("score_dst", [P, T])
        score_diag = sb("score_diag", [P, T, P])
        logit = sb("logit", [P, T, N])
        top = sb("top", [P, T])
        neg_top = sb("neg_top", [P, T])
        neg_max = sb("neg_max", [P, T])
        expd = sb("expd", [P, T, N])
        attn = sb("attn", [P, T, N])
        denom = sb("denom", [P, T])
        rdenom = sb("rdenom", [P, T])
        at_hi = sb("at_hi", [P, T, N], F32R)
        at_lo = sb("at_lo", [P, T, N], F32R)
        at_f32 = z_pos[:, :, :]
        NB = L0.heads * L0.blocks + L2.heads * L2.blocks
        bias_col = sb("bias_col", [P, 3, NB])
        bias_now = sb("bias_now", [P, 3, L0.blocks])
        y = z[:, :, :].rearrange("p k n -> p (k n)").rearrange("p (t d) -> p t d", t=T)
        stats = sb("stats", [P, T, 2, 6])
        mean_var = sb("mean_var", [P, T, 2])
        var_eps = sb("var_eps", [P, T])
        rstd = sb("rstd", [P, T])
        minus_half = sb("minus_half", [P, T])
        ident = sb("ident", [P, P])
        ones = sb("ones", [P, P])
        zeros = sb("zeros", [P, P], F32R)
        iota_i = sb("iota_i", [P, N], I32)
        iota_b = sb("iota_b", [P, N], BF16)
        edge_i = sb("edge_i", [P, 2, EC], I32)
        edge_f = sb("edge_f", [P, 2, EC])
        degree = sb("degree", [P, T])
        dinv = sb("dinv", [P, T])
        w3 = sb("w3", [P, P])
        w3res = sb("w3res", [P, P])
        attn3_t = sb("attn3_t", [P, 2 * H3])
        w3_att = sb("w3_att", [P, KD, 4])
        onehot = h_raw[:, :, :].rearrange("p t d -> p (t d)").bitcast(BF16)[:, 0:RING * 2 * N]\
            .rearrange("p (c e n) -> p c e n", c=RING, e=2)
        padded = z[:, :, :].rearrange("p k n -> p (k n)")[:, 0:5 * P].rearrange("p (a n) -> p a n", a=5)
        HG = H3 // 2
        KC = P + 4
        whole = w_raw[:, :, :].rearrange("p a n -> p (a n)")
        taken = [0]

        def cut(size):
            taken[0] += size
            return whole[:, taken[0] - size:taken[0]]

        xt3 = cut(KD * N).rearrange("p (k n) -> p k n", k=KD)
        w3_wide = cut(KD * KC).rearrange("p (k n) -> p k n", k=KD)
        ft3 = cut(T * H3 * (C3 + 1)).rearrange("p (t h c) -> p t h c", t=T, h=H3)
        count_t = cut(T * N).rearrange("p (t n) -> p t n", t=T)
        exp3 = cut(2 * 2 * T * N).rearrange("p (b e t n) -> p b e t n", b=2, e=2, t=T)
        weight3 = cut(2 * T * N).rearrange("p (b t n) -> p b t n", b=2, t=T)
        discard3 = z[:, :, :].rearrange("p k n -> p (k n)").bitcast(BF16).rearrange("p (j n) -> p j n", n=N)
        sel3 = w_hi[0:2 * H3, 0, 0:H3 * P].rearrange("p (h n) -> p h n", h=H3)
        src_rows = w_hi[0:2 * H3, 1, 0:N]
        dst_rows = w_hi[0:2 * H3, 1, N:3 * N]
        src_parts = w_hi[:, 1, 3 * N:3 * N + T * 2 * H3].rearrange("p (t a h) -> p t a h", t=T, a=2)
        dst_parts = w_hi[:, 2, 0:T * 4 * H3].rearrange("p (t r a h) -> p t r a h", t=T, r=2, a=2)
        sel_col = sb("sel_col", [P, H3])
        score3 = sb("score3", [P, T, 2, H3])
        fifth3 = sb("fifth3", [P, T, 2, H3])
        top3 = sb("top3", [P, T, H3])
        neg_top3 = sb("neg_top3", [P, T, H3])
        neg_max3 = sb("neg_max3", [P, T, H3])
        shift3 = sb("shift3", [P, T, 2, H3])
        denom3 = sb("denom3", [P, T, H3])
        rdenom3 = sb("rdenom3", [P, T, H3])

        heads_ps = ctx.enter_context(nc.psum_tensor("heads_ps", [P, 4 * BANK], F32))
        acc_ps = ctx.enter_context(nc.psum_tensor("acc_ps", [P, 3 * BANK], F32))
        misc_ps = ctx.enter_context(nc.psum_tensor("misc_ps", [P, BANK], F32))
        AGG_BANK = [0, 2, 3]
        WARM_HEAD, WARM_SCORES, WARM_SOFTMAX, WARM_NORM, WARM_SHIFTS, WARM_EXPS = 10, 15, 14, 14, 14, 12
        WARM_HEAD3 = 2

        x_landed = sem("x_landed")
        edges_landed = sem("edges_landed")
        padded_landed = sem("padded_landed")
        bias_landed = sem("bias_landed")
        vec_landed = sem("vec_landed")
        raw_landed = [sem(f"raw_landed{j}") for j in range(4)]
        split_hi = [sem(f"split_hi{j}") for j in range(4)]
        split_lo = [sem(f"split_lo{j}") for j in range(4)]
        consts_zeroed = sem("consts_zeroed")
        consts_ready = sem("consts_ready")
        padded_zeroed = sem("padded_zeroed")
        iota_ready = sem("iota_ready")
        edges_ready = sem("edges_ready")
        onehot_ready = sem("onehot_ready")
        onehot_used = sem("onehot_used")
        count_ready = sem("count_ready")
        degree_ready = sem("degree_ready")
        dinv_ready = sem("dinv_ready")
        conv_scaled = sem("conv_scaled")
        conv_turned = sem("conv_turned")
        conv_ready = sem("conv_ready")
        padded_turned = sem("padded_turned")
        padded_copied = sem("padded_copied")
        w3_scored = sem("w3_scored")
        w3_ready = sem("w3_ready")
        bias_now_ready = sem("bias_now_ready")
        xt_turned = sem("xt_turned")
        xt_hi_ready = sem("xt_hi_ready")
        xt_lo_ready = sem("xt_lo_ready")
        h_done = sem("h_done")
        w2_used = sem("w2_used")
        h_copied = sem("h_copied")
        h_hi_ready = sem("h_hi_ready")
        h_lo_ready = sem("h_lo_ready")
        scores_ready = sem("scores_ready")
        diag_ready = sem("diag_ready")
        scores_spread = sem("scores_spread")
        logit_masked = sem("logit_masked")
        logit_summed = sem("logit_summed")
        logit_ready = sem("logit_ready")
        exp_ready = sem("exp_ready")
        exp_counted = sem("exp_counted")
        rdenom_ready = sem("rdenom_ready")
        attn_ready = sem("attn_ready")
        attn_turned = sem("attn_turned")
        at_hi_ready = sem("at_hi_ready")
        at_lo_ready = sem("at_lo_ready")
        at_f32_ready = sem("at_f32_ready")
        agg_done = sem("agg_done")
        elu_exp = sem("elu_exp")
        elu_pos = sem("elu_pos")
        z_ready = sem("z_ready")
        z_hi_ready = sem("z_hi_ready")
        z_lo_ready = sem("z_lo_ready")
        out_done = sem("out_done")
        y_ready = sem("y_ready")
        stats_ready = sem("stats_ready")
        var_ready = sem("var_ready")
        eps_added = sem("eps_added")
        rstd_ready = sem("rstd_ready")
        x_ready = sem("x_ready")
        xb_ready = sem("xb_ready")
        w3_widened = sem("w3_widened")
        count_turned = sem("count_turned")
        count_t_ready = sem("count_t_ready")
        sel_col_ready = sem("sel_col_ready")
        sel_ready = sem("sel_ready")
        xt3_ready = sem("xt3_ready")
        ft3_done = sem("ft3_done")
        ft3_ready = sem("ft3_ready")
        res3_done = sem("res3_done")
        res3_ready = sem("res3_ready")
        score3_ready = sem("score3_ready")
        src_split = sem("src_split")
        src_turned = sem("src_turned")
        src_rows_ready = sem("src_rows_ready")
        src_spread = sem("src_spread")
        masked3 = sem("masked3")
        neg_top3_ready = sem("neg_top3_ready")
        neg_max3_ready = sem("neg_max3_ready")
        shift3_ready = sem("shift3_ready")
        dst_split = sem("dst_split")
        dst_turned = sem("dst_turned")
        dst_rows_ready = sem("dst_rows_ready")
        dst_spread = sem("dst_spread")
        exp3_ready = sem("exp3_ready")
        exp3_maxed = sem("exp3_maxed")
        weight3_ready = sem("weight3_ready")
        agg3_done = sem("agg3_done")
        denom3_ready = sem("denom3_ready")
        rdenom3_ready = sem("rdenom3_ready")
        scaled3 = sem("scaled3")
        summed3 = [sem("summed3_first"), sem("summed3_second")]
        stored = sem("stored")

        block = ctx.enter_context(nc.Block())

        def pair_ps(ps, p):
            return ps[:, p * BANK:(p + 1) * BANK].rearrange("p (c n) -> p c n", c=2)

        def src_bank(p):
            return pair_ps(misc_ps, 0) if p == 0 else pair_ps(acc_ps, p % 3)

        def wide_ps(t, g):
            o = (2 * t + g) * BANK
            return heads_ps[:, o:o + KD // 2 * KC].rearrange("p (k n) -> p k n", k=KD // 2)

        def features_ps(t, g):
            return wide_ps(t, g)[:, :, 0:P].rearrange("p k (c n) -> p k c n", c=2)

        def sums_ps(t, g):
            o = (2 * t + g) * BANK
            return heads_ps[:, o:o + HG * (C3 + 1)].rearrange("p (h n) -> p h n", h=HG)

        def spread(row, rows=P):
            return row.rearrange("(a n) -> a n", a=1).broadcast_to([rows, row.shape[0]])

        def add_residuals(engine, g):
            cols = slice(g * HG * C3, (g + 1) * HG * C3)
            for t in range(T):
                engine.wait_ge(scaled3, g * T + t + 1)
                engine.tensor_tensor(y[:, t, cols], y[:, t, cols], xb[:, t, cols], ALU.add)\
                    .then_inc(summed3[g], 1)

        @block.sync
        def _(sp):
            def load_first(L, w1, i):
                w = w1.rearrange("(k p) n -> p k n", p=P)
                for j in range(2):
                    if not (L is L0 and isinstance(i, int) and i == 0):
                        sp.wait_ge(split_lo[j], i + L.w1)
                    sp.dma_start(
                        w_raw[:, j, 0:L.w1_k * L.width].rearrange("p (k n) -> p k n", k=L.w1_k),
                        w[:, j * L.w1_k:(j + 1) * L.w1_k, bass.ds(i * L.width, L.width)],
                    ).then_inc(raw_landed[j], 16)

            def load_second(L, w2, i):
                w = w2.rearrange("(k p) n -> p k n", p=P)
                for j in range(2):
                    if not (L is L0 and isinstance(i, int) and i == 0):
                        sp.wait_ge(split_lo[2 + j], i + L.w2)
                    sp.dma_start(
                        w_raw[:, 2 + j, 0:L.w2_k * D].rearrange("p (k n) -> p k n", k=L.w2_k),
                        w[:, bass.ds(i * L.blocks + j * L.w2_k, L.w2_k), :],
                    ).then_inc(raw_landed[2 + j], 16)

            def load_vectors(L, a_src, a_dst, i):
                width = a_src.shape[1]
                if not (L is L0 and isinstance(i, int) and i == 0):
                    sp.wait_ge(scores_ready, i * 2 * T + 2 * T * L.att)
                for e, a in enumerate((a_src, a_dst)):
                    row = a[bass.ds(i, 1), :] if a.shape[0] > 1 else a[0:1, :]
                    sp.dma_start(att_vec[:, e, 0:width], row.broadcast_to([P, width]))\
                        .then_inc(vec_landed, 16)

            def load_vectors2(L, a_src, a_dst):
                sp.wait_ge(scores_ready, 2 * T * (L.att + L.heads))
                for e, a in enumerate((a_src, a_dst)):
                    sp.dma_start(att_vec[:, e, :], a[0:1, :].broadcast_to([P, D])).then_inc(vec_landed, 16)

            def load_bias(l, b):
                if l:
                    sp.wait_ge(y_ready, 2 * T * l)
                for t in range(T):
                    sp.dma_start(xb[:, t, :], spread(b)).then_inc(bias_landed, 16)

            sp.dma_start(edge_i[:, 0, :], dst.rearrange("(p c) -> p c", p=P)).then_inc(edges_landed, 16)
            sp.dma_start(x_nat[:, :, :], x.rearrange("(t p) n -> p t n", p=P)).then_inc(x_landed, 16)
            load_first(L0, l0_w1, 0)
            sp.wait_ge(padded_zeroed, 1)
            nb0 = L0.heads * L0.blocks
            nb2 = L2.heads * L2.blocks
            sp.dma_start(padded[0:nb0, 0, :], l0_b1.rearrange("(a p) -> a p", p=P)).then_inc(padded_landed, 16)
            sp.dma_start(padded[0:nb2, 1, :], l2_b1.rearrange("(a p) -> a p", p=P)).then_inc(padded_landed, 16)
            for c in range(2):
                sp.dma_start(padded[0:C3, 2, c * C3:(c + 1) * C3], l3_w).then_inc(padded_landed, 16)
                sp.dma_start(padded[0:C3, 3, c * C3:(c + 1) * C3], l3_wres).then_inc(padded_landed, 16)
            sp.dma_start(padded[0:H3, 4, 0:C3], l3_al[0, :, :]).then_inc(padded_landed, 16)
            sp.dma_start(padded[H3:2 * H3, 4, 0:C3], l3_ar[0, :, :]).then_inc(padded_landed, 16)
            load_vectors(L0, l0_as1, l0_ad1, 0)
            load_second(L0, l0_w2, 0)
            load_bias(0, l0_b2)
            load_first(L0, l0_w1, 1)
            with sp.Fori(1, L0.heads - 1) as i:
                load_vectors(L0, l0_as1, l0_ad1, i)
                load_first(L0, l0_w1, i + 1)
                load_second(L0, l0_w2, i)
            load_vectors(L0, l0_as1, l0_ad1, H0 - 1)
            load_first(L2, l2_w1, 0)
            load_second(L0, l0_w2, H0 - 1)
            load_vectors2(L0, l0_as2, l0_ad2)
            w = l1_w.rearrange("(k p) n -> p k n", p=P)
            for j in range(2):
                sp.wait_ge(split_lo[2 + j], H0)
                sp.dma_start(w_raw[:, 2 + j, :].rearrange("p (k n) -> p k n", k=KU),
                             w[:, j * KU:(j + 1) * KU, :]).then_inc(raw_landed[2 + j], 16)
            load_first(L2, l2_w1, 1)
            load_vectors(L2, l2_as1, l2_ad1, 0)
            load_second(L2, l2_w2, 0)
            load_bias(1, l1_b)
            load_bias(2, l2_b2)
            with sp.Fori(1, L2.heads - 1) as i:
                load_vectors(L2, l2_as1, l2_ad1, i)
                load_first(L2, l2_w1, i + 1)
                load_second(L2, l2_w2, i)
            load_vectors(L2, l2_as1, l2_ad1, H2 - 1)
            load_second(L2, l2_w2, H2 - 1)
            load_vectors2(L2, l2_as2, l2_ad2)
            for t in range(T):
                sp.wait_ge(x_ready, T * 3 + t + 1)
                sp.dma_start(out[t * P:(t + 1) * P, :], x_nat[:, t, :]).then_inc(stored, 16)
            sp.wait_ge(stored, 16 * T)

        @block.scalar
        def _(act):
            act.dma_start(edge_i[:, 1, :], src.rearrange("(p c) -> p c", p=P)).then_inc(edges_landed, 16)

            def split_slot(j, use, size):
                act.wait_ge(raw_landed[j], 16 * use + 16)
                act.activation(w_hi[:, j, 0:size], w_raw[:, j, 0:size], ACT.Copy).then_inc(split_hi[j], 1)

            def first_slots(L, i):
                for j in range(2):
                    if not (L is L0 and isinstance(i, int) and i == 0):
                        act.wait_ge(h_done, T * (L.head + i))
                    split_slot(j, i + L.w1, L.w1_k * L.width)

            def second_slot(L, i, j):
                if L is L2 and isinstance(i, int) and i == 0:
                    act.wait_ge(out_done, 2 * T * 2)
                elif not (isinstance(i, int) and i == 0):
                    act.wait_ge(w2_used, i * 2 + (L.w2_used - 2 + j + 1))
                split_slot(2 + j, i + L.w2, L.w2_k * D)

            def xt_high(e):
                for p in range(XP):
                    act.wait_ge(xt_turned, XP * e + p + 1)
                    act.activation(xt_hi[:, 2 * p:2 * p + 2, :], pair_ps(acc_ps, p), ACT.Copy)\
                        .then_inc(xt_hi_ready, 1)

            def exps(a):
                act.wait_ge(logit_ready, 2 * a + 2)
                for d in range(T):
                    act.activation(expd[:, d, :], logit[:, d, :], ACT.Exp, bias=neg_max[:, d:d + 1])\
                        .then_inc(exp_ready, 1)

            def copy_h(L, i, t):
                first = L is L0 and isinstance(i, int) and i == 0
                act.wait_ge(h_done, (i + L.head) * T + t + 1)
                if t == 0 and not first:
                    act.wait_ge(h_lo_ready, i + L.head)
                if t == 0 and first:
                    act.wait_ge(onehot_used, EC)
                at = HEAD_AT[L.width] + 2 * t * BANK
                act.activation(h_raw[:, t, 0:L.width], heads_ps[:, at:at + L.width], ACT.Copy)\
                    .then_inc(h_copied, 1)

            def head(L, i, next_first):
                a = i + L.att
                first = L is L0 and isinstance(i, int) and i == 0
                last = isinstance(i, int) and i == L.heads - 1
                for t in range(T):
                    if t or L is L0 or (isinstance(i, int) and i == 0):
                        copy_h(L, i, t)
                    act.wait_ge(h_copied, a * T + t + 1)
                    act.activation(h_hi[:, t, 0:L.width], h_raw[:, t, 0:L.width], ACT.Copy)\
                        .then_inc(h_hi_ready, 1)
                if first:
                    act.wait_ge(conv_turned, 1)
                    act.wait_ge(dinv_ready, 1)
                    for s in range(T):
                        act.activation(conv_t[:, s, :], pair_ps(misc_ps, 0)[:, s, :], ACT.Copy,
                                       scale=dinv[:, s:s + 1]).then_inc(conv_ready, 1)
                if next_first is not None:
                    first_slots(*next_first)
                exps(a)
                second_slot(L, i, 0)
                act.wait_ge(attn_turned, a + 1)
                act.activation(at_hi[:, :, :].rearrange("p s n -> p (s n)"), misc_ps[:, :], ACT.Copy)\
                    .then_inc(at_hi_ready, 1)
                if last:
                    second_slot(L, i, 1)
                elif L is L2:
                    copy_h(L, i + 1, 0)
                act.wait_ge(bias_now_ready, i + (L.head + 1))

                def elu_half(p):
                    g = i * L.pairs + (L.pair + p)
                    act.wait_ge(agg_done, g + 1)
                    if not first:
                        act.wait_ge(z_lo_ready, i * L.pairs + (L.pair + p + 1 - L.pairs))
                    for c in range(2):
                        k = 2 * p + c
                        act.activation(z[:, k, :], pair_ps(heads_ps, AGG_BANK[p])[:, c, :], ACT.Exp,
                                       bias=bias_now[:, 0, k:k + 1]).then_inc(elu_exp, 1)

                def z_high(p):
                    act.wait_ge(z_ready, i * L.pairs + (L.pair + p + 1))
                    act.activation(z_hi[:, 2 * p:2 * p + 2, :], z[:, 2 * p:2 * p + 2, :], ACT.Copy)\
                        .then_inc(z_hi_ready, 1)

                for p in range(L.pairs):
                    elu_half(p)
                    if p:
                        z_high(p - 1)
                z_high(L.pairs - 1)
                if not last:
                    second_slot(L, i, 1)

            def second_attention(L, next_slots):
                a = L.att + L.heads
                act.wait_ge(w2_used, L.w2_used + 2 * L.heads)
                for j in next_slots:
                    split_slot(j, H0, UNIT)
                act.wait_ge(h_lo_ready, L.head + L.heads)
                act.wait_ge(scores_ready, 2 * T * (a + 1))
                for t in range(T):
                    act.activation(h_raw[:, t, :], acc_ps[:, t * D:(t + 1) * D], ACT.Copy)\
                        .then_inc(h_copied, 1)
                exps(a)
                act.wait_ge(attn_turned, a + 1)
                act.activation(at_f32.rearrange("p s n -> p (s n)"), misc_ps[:, :], ACT.Copy)\
                    .then_inc(at_f32_ready, 1)

            xt_high(0)
            first_slots(L0, 0)
            head(L0, 0, (L0, 1))
            with act.Fori(1, L0.heads - 1) as i:
                head(L0, i, (L0, i + 1))
            head(L0, L0.heads - 1, (L2, 0))
            second_attention(L0, [2, 3])
            xt_high(1)
            xt_high(2)
            head(L2, 0, (L2, 1))
            with act.Fori(1, L2.heads - 1) as i:
                head(L2, i, (L2, i + 1))
            head(L2, L2.heads - 1, None)
            second_attention(L2, [])
            act.wait_ge(count_turned, 1)
            act.activation(count_t[:, :, :].rearrange("p t n -> p (t n)"), misc_ps[:, :], ACT.Copy)\
                .then_inc(count_t_ready, 1)
            for p in range(XP):
                act.wait_ge(xt_turned, XP * 3 + p + 1)
                act.activation(xt3[:, 2 * p:2 * p + 2, :], pair_ps(acc_ps, p), ACT.Copy).then_inc(xt3_ready, 1)
            act.wait_ge(src_turned, 1)
            act.activation(src_rows, misc_ps[0:2 * H3, 0:N], ACT.Copy).then_inc(src_rows_ready, 1)
            for t in range(T):
                for g in range(2):
                    act.activation(ft3[:, t, g * HG:(g + 1) * HG, 0:C3], features_ps(t, g), ACT.Copy)\
                        .then_inc(ft3_ready, 1)
            act.wait_ge(res3_done, 1)
            for t in range(T):
                act.activation(xb[:, t, :], heads_ps[:, 2 * t * BANK:2 * t * BANK + D], ACT.Copy)\
                    .then_inc(res3_ready, 1)
            act.wait_ge(dst_turned, 1)
            act.activation(dst_rows, misc_ps[0:2 * H3, :], ACT.Copy).then_inc(dst_rows_ready, 1)
            for h in range(H3):
                act.wait_ge(dst_spread, h + 1)
                if h >= 2:
                    act.wait_ge(exp3_maxed, h - 1)
                for s in range(T):
                    for e, by_src in enumerate((score3, fifth3)):
                        ins = act.activation(exp3[:, h % 2, e, s, :], pair_ps(acc_ps, h % 3)[:, e, :], ACT.Exp,
                                             bias=by_src[:, s, 0, h:h + 1])
                ins.then_inc(exp3_ready, 1)

        @block.gpsimd
        def _(pool):
            pool.memset(z[:, :, :], 0.0).then_inc(padded_zeroed, 1)
            pool.iota(iota_i[:, :], pattern=[[1, N]], base=0, channel_multiplier=0).then_inc(iota_ready, 1)
            pool.memset(ident[:, :], 0.0).then_inc(consts_zeroed, 1)
            pool.memset(ones[:, :], 1.0)
            pool.memset(zeros[:, :].bitcast(F32), 0.0)
            pool.memset(w3[:, :], 0.0)
            pool.memset(w3res[:, :], 0.0)
            pool.memset(w3_att[:, :, :], 0.0)
            pool.memset(minus_half[:, :], -0.5)
            pool.wait_ge(consts_zeroed, 1)
            pool.affine_select(out=ident[:, :], in_=ident[:, :], compare_op=ALU.not_equal, fill=1.0,
                               base=0, pattern=[[-1, P]], channel_multiplier=1).then_inc(consts_ready, 1)

            def low_slot(j, use, size):
                pool.wait_ge(split_hi[j], use + 1)
                pool.tensor_tensor(w_lo[:, j, 0:size], w_raw[:, j, 0:size], w_hi[:, j, 0:size].bitcast(F32),
                                   ALU.subtract).then_inc(split_lo[j], 1)

            def head(L, i, next_first):
                last = isinstance(i, int) and i == L.heads - 1
                if last:
                    low_slot(3, i + L.w2, L.w2_k * D)
                else:
                    Ln, n = next_first
                    if L is L2:
                        low_slot(0, n + Ln.w1, Ln.w1_k * Ln.width)
                    low_slot(1, n + Ln.w1, Ln.w1_k * Ln.width)
                for p in range(L.pairs):
                    pool.wait_ge(z_hi_ready, i * L.pairs + (L.pair + p + 1))
                    ks = slice(2 * p, 2 * p + 2)
                    pool.tensor_tensor(z_lo[:, ks, :], z[:, ks, :], z_hi[:, ks, :].bitcast(F32),
                                       ALU.subtract).then_inc(z_lo_ready, 1)
                if not last:
                    low_slot(3, i + L.w2, L.w2_k * D)
                elif next_first is not None:
                    Ln, n = next_first
                    low_slot(1, n + Ln.w1, Ln.w1_k * Ln.width)

            def rstd_of(l):
                for t in range(T):
                    pool.wait_ge(var_ready, T * l + t + 1)
                    pool.tensor_scalar(var_eps[:, t:t + 1], mean_var[:, t, 1:2], LN_EPS, None, ALU.add)\
                        .then_inc(eps_added, 1)
                    pool.wait_ge(eps_added, T * l + t + 1)
                    pool.tensor_tensor(rstd[:, t:t + 1], var_eps[:, t:t + 1], minus_half[:, t:t + 1], ALU.pow)\
                        .then_inc(rstd_ready, 1)

            def add_bias(l):
                pool.wait_ge(bias_landed, 16 * T * (l + 1))
                for t in range(T):
                    if l:
                        pool.wait_ge(x_ready, T * (l - 1) + t + 1)
                    pool.tensor_tensor(xb[:, t, :], xb[:, t, :], x_nat[:, t, :], ALU.add)\
                        .then_inc(xb_ready, 1)

            low_slot(0, 0, UNIT)
            pool.wait_ge(degree_ready, 1)
            pool.tensor_tensor(dinv[:, :], degree[:, :], minus_half[:, :], ALU.pow).then_inc(dinv_ready, 1)
            pool.wait_ge(x_landed, 16)
            add_bias(0)
            head(L0, 0, (L0, 1))
            with pool.Fori(1, L0.heads - 1) as i:
                head(L0, i, (L0, i + 1))
            head(L0, L0.heads - 1, (L2, 0))
            low_slot(3, H0, UNIT)
            rstd_of(0)
            add_bias(1)
            rstd_of(1)
            add_bias(2)
            head(L2, 0, (L2, 1))
            with pool.Fori(1, L2.heads - 1) as i:
                head(L2, i, (L2, i + 1))
            head(L2, L2.heads - 1, None)
            pool.wait_ge(w2_used, L2.w2_used + 2 * H2)
            pool.tensor_copy(w3_wide[:, :, 0:P], w3[:, :].rearrange("p (a n) -> p a n", a=1).broadcast_to([P, KD, P]))
            pool.tensor_copy(w3_wide[:, :, P:KC], w3_att[:, :, :]).then_inc(w3_widened, 1)
            pool.memset(ft3[:, :, :, C3:C3 + 1], 1.0)
            pool.tensor_tensor(sel_col[0:2 * H3, :], ident[0:2 * H3, 0:H3], ident[0:2 * H3, H3:2 * H3], ALU.add)\
                .then_inc(sel_col_ready, 1)
            pool.wait_ge(sel_col_ready, 1)
            pool.tensor_copy(sel3, sel_col[0:2 * H3, :].rearrange("p (h a) -> p h a", a=1)
                             .broadcast_to([2 * H3, H3, P])).then_inc(sel_ready, 1)
            rstd_of(2)
            pool.wait_ge(res3_ready, T)
            add_residuals(pool, 0)
            rstd_of(3)

        @block.vector
        def _(dve):
            def low_slot(j, use, size):
                dve.wait_ge(split_hi[j], use + 1)
                dve.tensor_tensor(w_lo[:, j, 0:size], w_raw[:, j, 0:size], w_hi[:, j, 0:size].bitcast(F32),
                                  ALU.subtract).then_inc(split_lo[j], 1)

            def xt_low(e):
                for p in range(XP):
                    dve.wait_ge(xt_hi_ready, XP * e + p + 1)
                    ks = slice(2 * p, 2 * p + 2)
                    dve.tensor_tensor(xt_lo[:, ks, :], pair_ps(acc_ps, p), xt_hi[:, ks, :].bitcast(F32),
                                      ALU.subtract).then_inc(xt_lo_ready, 1)

            def attention(a, width, masks, tile_of, tile_ready, value, meanwhile):
                counts, missing = masks
                dve.wait_ge(vec_landed, a * 32 + 32)
                for t in range(T):
                    dve.wait_ge(tile_ready, value + t)
                    for e, score in enumerate((score_src, score_dst)):
                        if t:
                            dve.wait_ge(scores_ready, a * 2 * T + e + 1)
                        dve.tensor_tensor_reduce(product[:, e, 0:width], tile_of(t),
                                                 att_vec[:, e, 0:width], 1.0, 0.0, ALU.mult, ALU.add,
                                                 score[:, t:t + 1]).then_inc(scores_ready, 1)
                dve.wait_ge(scores_ready, a * 2 * T + 2 * T)
                for t in range(T):
                    ins = dve.tensor_scalar(score_diag[:, t, :], ident[:, :], score_src[:, t:t + 1], None, ALU.mult)
                ins.then_inc(diag_ready, 1)
                meanwhile()
                for d in range(T):
                    ins = dve.tensor_tensor_reduce(logit[:, d, :], misc_ps[:, 0:N], missing[:, d, :], 1.0, -3e38,
                                                   ALU.add, ALU.max, top[:, d:d + 1])
                ins.then_inc(logit_masked, 1)
                dve.wait_ge(logit_masked, a + 1)
                dve.scalar_tensor_tensor(neg_top[:, :], top[:, :], -1.0, score_dst[:, :], ALU.mult, ALU.subtract)
                for d in range(T):
                    ins = dve.tensor_scalar(logit[:, d, :], logit[:, d, :], score_dst[:, d:d + 1], None, ALU.add)
                ins.then_inc(logit_summed, 1)
                dve.wait_ge(logit_summed, a + 1)
                dve.scalar_tensor_tensor(neg_max[:, :], neg_top[:, :], NEG_SLOPE, neg_top[:, :], ALU.mult, ALU.min)\
                    .then_inc(logit_ready, 1)
                dve.scalar_tensor_tensor(logit[:, :, :], logit[:, :, :], NEG_SLOPE, logit[:, :, :], ALU.mult, ALU.max)\
                    .then_inc(logit_ready, 1)
                for d in range(T):
                    dve.wait_ge(exp_ready, a * T + d + 1)
                    ins = dve.tensor_tensor_reduce(attn[:, d, :], expd[:, d, :], counts[:, d, :], 1.0, ATT_EPS,
                                                   ALU.mult, ALU.add, denom[:, d:d + 1])
                ins.then_inc(exp_counted, 1)
                dve.wait_ge(exp_counted, a + 1)
                dve.reciprocal(rdenom[:, :], denom[:, :]).then_inc(rdenom_ready, 1)

            def collect_w3():
                dve.wait_ge(w3_scored, 1)
                for c in range(2):
                    q = slice(c * C3, (c + 1) * C3)
                    scored = acc_ps[q, BANK + 2 * P:BANK + 2 * P + 2 * H3].rearrange("p (e k c) -> p k e c", e=2, c=2)
                    ins = dve.tensor_copy(w3_att[q, :, c:c + 3:2], scored[:, :, :, c])
                ins.then_inc(w3_ready, 1)

            def head(L, i, masks, next_first):
                a = i + L.att
                first = L is L0 and isinstance(i, int) and i == 0
                nb = 0 if L is L0 else L0.heads * L0.blocks
                late = isinstance(i, int) and (i == 0 or (L is L2 and i == L.heads - 1))
                dve.tensor_copy(bias_now[:, :, 0:L.blocks], bias_col[:, :, bass.ds(i * L.blocks + nb, L.blocks)])\
                    .then_inc(bias_now_ready, 1)

                def low_h():
                    for t in range(T):
                        dve.wait_ge(h_hi_ready, (i + L.head) * T + t + 1)
                        if t == T - 1:
                            dve.wait_ge(scores_spread, a + 1)
                        ins = dve.tensor_tensor(h_lo[:, t, 0:L.width], h_raw[:, t, 0:L.width],
                                                h_hi[:, t, 0:L.width].bitcast(F32), ALU.subtract)
                    ins.then_inc(h_lo_ready, 1)

                def await_spread():
                    if first:
                        collect_w3()
                    dve.wait_ge(scores_spread, a + 1)

                attention(a, L.width, masks, lambda t: h_raw[:, t, 0:L.width], h_copied, a * T + 1,
                          await_spread if late else low_h)
                dve.wait_ge(rdenom_ready, a + 1)
                for d in range(T):
                    ins = dve.tensor_scalar(attn[:, d, :], attn[:, d, :], rdenom[:, d:d + 1], None, ALU.mult)
                ins.then_inc(attn_ready, 1)
                if late:
                    low_h()
                dve.wait_ge(at_hi_ready, i + (L.head + 1))
                dve.tensor_tensor(at_lo[:, :, :].rearrange("p s n -> p (s n)"), misc_ps[:, :],
                                  at_hi[:, :, :].rearrange("p s n -> p (s n)").bitcast(F32), ALU.subtract)\
                    .then_inc(at_lo_ready, 1)
                last = isinstance(i, int) and i == L.heads - 1
                if last or L is L2:
                    low_slot(2, i + L.w2, L.w2_k * D)
                else:
                    Ln, n = next_first
                    low_slot(0, n + Ln.w1, Ln.w1_k * Ln.width)
                for p in range(L.pairs):
                    dve.wait_ge(elu_exp, i * (2 * L.pairs) + 2 * (L.pair + p + 1))
                    if p:
                        dve.wait_ge(z_ready, i * L.pairs + (L.pair + p))
                    for c in range(2):
                        k = 2 * p + c
                        ins = dve.tensor_scalar(z_pos[:, c, :], pair_ps(heads_ps, AGG_BANK[p])[:, c, :],
                                                bias_now[:, 1, k:k + 1], bias_now[:, 2, k:k + 1], ALU.max, ALU.add)
                    ins.then_inc(elu_pos, 1)
                    dve.wait_ge(elu_pos, i * L.pairs + (L.pair + p + 1))
                    ks = slice(2 * p, 2 * p + 2)
                    dve.scalar_tensor_tensor(z[:, ks, :], z[:, ks, :], 1.0, z_pos[:, :, :], ALU.min, ALU.add)\
                        .then_inc(z_ready, 1)
                if not last and L is L0:
                    low_slot(2, i + L.w2, L.w2_k * D)
                elif last and next_first is not None:
                    Ln, n = next_first
                    low_slot(0, n + Ln.w1, Ln.w1_k * Ln.width)

            sums = [0]

            def sum_piece(t, c, ins):
                sums[0] += 1
                ins.then_inc(y_ready, 1)
                dve.wait_ge(y_ready, sums[0])
                dve.bn_stats(stats[:, t, c, :], y[:, t, c * (D // 2):(c + 1) * (D // 2)]).then_inc(stats_ready, 1)

            def variance(l, t):
                dve.wait_ge(stats_ready, sums[0])
                dve.bn_aggr(mean_var[:, t, :], stats[:, t, :, :].rearrange("p c s -> p (c s)"))\
                    .then_inc(var_ready, 1)

            def normalise(l):
                for t in range(T):
                    dve.wait_ge(rstd_ready, T * l + t + 1)
                    dve.tensor_scalar(x_nat[:, t, :], y[:, t, :], mean_var[:, t, 0:1], rstd[:, t:t + 1],
                                      ALU.subtract, ALU.mult).then_inc(x_ready, 1)

            def layer_norm(l, piece):
                for t in range(T):
                    for c, (at, size) in enumerate(HEAD_PIECES[D]):
                        dve.wait_ge(out_done, 2 * (T * l + t) + c + 1)
                        sum_piece(t, c, piece(t, slice(at, at + size), heads_ps[:, 2 * t * BANK + at:
                                                                                2 * t * BANK + at + size]))
                    variance(l, t)
                normalise(l)

            def second_attention(L, l, masks):
                attention(L.att + L.heads, D, masks, lambda t: acc_ps[:, t * D:(t + 1) * D],
                          w2_used, L.w2_used + 2 * L.heads - 1,
                          lambda: dve.wait_ge(scores_spread, L.att + L.heads + 1))
                if L is L0:
                    low_slot(2, H0, UNIT)
                dve.wait_ge(rdenom_ready, L.att + L.heads + 1)
                dve.wait_ge(xb_ready, T * (l + 1))

                layer_norm(l, lambda t, q, ps: dve.scalar_tensor_tensor(
                    y[:, t, q], ps, rdenom[:, t:t + 1], xb[:, t, q], ALU.mult, ALU.add))

            dve.wait_ge(iota_ready, 1)
            dve.tensor_copy(iota_b[:, :], iota_i[:, :])
            dve.wait_ge(edges_landed, 32)
            dve.tensor_copy(edge_f[:, :, :], edge_i[:, :, :]).then_inc(edges_ready, 1)
            dve.wait_ge(edges_ready, 1)

            def onehots(c, b):
                for e in range(2):
                    ins = dve.tensor_scalar(onehot[:, b, e, :], iota_b[:, :], edge_f[:, e, bass.ds(c, 1)], None,
                                            ALU.is_equal)
                ins.then_inc(onehot_ready, 1)

            for c in range(LEAD):
                if c >= RING:
                    dve.wait_ge(onehot_used, c - RING + 1)
                onehots(c, c % RING)
            with dve.Fori(0, (EC - LEAD) // RING - 1) as g:
                for b in range(RING):
                    dve.wait_ge(onehot_used, g * RING + (LEAD + b - RING + 1))
                    onehots(g * RING + (LEAD + b), (LEAD + b) % RING)
            xt_low(0)
            low_slot(1, 0, UNIT)
            for c in range(EC - RING, EC):
                dve.wait_ge(onehot_used, c - RING + 1)
                onehots(c, c % RING)
            dve.wait_ge(onehot_used, EC)
            dve.tensor_copy(count[:, :, :].rearrange("p t n -> p (t n)"), misc_ps[:, :]).then_inc(count_ready, 1)
            dve.wait_ge(count_ready, 1)
            dve.wait_ge(consts_ready, 1)
            dve.tensor_copy(count_loop[:, :, :], count[:, :, :]).then_inc(count_ready, 1)
            dve.wait_ge(count_ready, 2)
            for t in range(T):
                diagonal = count_loop[:, t, t * P:(t + 1) * P]
                ins = dve.tensor_tensor(diagonal, diagonal, ident[:, :], ALU.add)
            ins.then_inc(count_ready, 1)
            dve.wait_ge(count_ready, 3)
            dve.tensor_reduce(degree[:, :], count_loop[:, :, :], mybir.AxisListType.X, ALU.add)\
                .then_inc(degree_ready, 1)
            dve.tensor_scalar(absent[:, :, :], count[:, :, :], 0.0, MASKED, ALU.is_equal, ALU.mult)
            dve.tensor_scalar(absent_loop[:, :, :], count_loop[:, :, :], 0.0, MASKED, ALU.is_equal, ALU.mult)
            nb0 = L0.heads * L0.blocks
            dve.wait_ge(padded_turned, 1)
            dve.tensor_copy(attn3_t[:, :], acc_ps[:, BANK:BANK + 2 * H3])
            dve.tensor_copy(bias_col[:, 0, 0:nb0], acc_ps[:, 0:nb0])
            dve.tensor_copy(bias_col[:, 0, nb0:NB], acc_ps[:, P:P + NB - nb0])
            for c in range(2):
                q = slice(c * C3, (c + 1) * C3)
                dve.tensor_copy(w3[q, q], acc_ps[q, 2 * P:2 * P + C3])
                ins = dve.tensor_copy(w3res[q, q], acc_ps[q, 3 * P:3 * P + C3])
            ins.then_inc(padded_copied, 1)
            dve.wait_ge(dinv_ready, 1)
            for t in range(T):
                ins = dve.tensor_scalar(attn[:, t, :], count_loop[:, t, :], dinv[:, t:t + 1], None, ALU.mult)
            ins.then_inc(conv_scaled, 1)
            dve.wait_ge(padded_copied, 1)
            dve.tensor_scalar(bias_col[:, 1, :], bias_col[:, 0, :], -1.0, None, ALU.mult)
            dve.tensor_scalar(bias_col[:, 2, :], bias_col[:, 0, :], -1.0, None, ALU.add).then_inc(padded_copied, 1)
            dve.wait_ge(padded_copied, 2)

            plain, looped = (count, absent), (count_loop, absent_loop)
            head(L0, 0, plain, (L0, 1))
            with dve.Fori(1, L0.heads - 1) as i:
                head(L0, i, plain, (L0, i + 1))
            head(L0, L0.heads - 1, plain, (L2, 0))
            second_attention(L0, 0, plain)
            xt_low(1)
            dve.wait_ge(xb_ready, T * 2)
            layer_norm(1, lambda t, q, ps: dve.tensor_tensor(y[:, t, q], ps, xb[:, t, q], ALU.add))
            xt_low(2)
            head(L2, 0, looped, (L2, 1))
            with dve.Fori(1, L2.heads - 1) as i:
                head(L2, i, looped, (L2, i + 1))
            head(L2, L2.heads - 1, looped, None)
            second_attention(L2, 2, looped)
            for t in range(T):
                dve.wait_ge(ft3_done, t + 1)
                for g in range(2):
                    scored = wide_ps(t, g)[:, :, P:KC].rearrange("p k (e c) -> p e k c", e=2)
                    ins = dve.tensor_copy(score3[:, t, :, g * HG:(g + 1) * HG]
                                          .rearrange("p e (k c) -> p e k c", c=2), scored)
            ins.then_inc(score3_ready, 1)
            dve.wait_ge(score3_ready, 1)
            dve.tensor_copy(src_parts[:, :, 0, :], score3[:, :, 0, :]).then_inc(src_split, 1)
            dve.tensor_scalar(fifth3[:, :, :, :], score3[:, :, :, :], NEG_SLOPE, None, ALU.mult)\
                .then_inc(score3_ready, 1)
            dve.wait_ge(src_split, 1)
            dve.tensor_tensor(src_parts[:, :, 1, :], score3[:, :, 0, :], src_parts[:, :, 0, :].bitcast(F32),
                              ALU.subtract).then_inc(src_split, 1)
            for p in range(H3 // 2):
                dve.wait_ge(src_spread, p + 1)
                if p >= 3:
                    dve.wait_ge(masked3, p - 2)
                ps = src_bank(p)
                for c in range(2):
                    for d in range(T):
                        ins = dve.tensor_tensor_reduce(discard3[:, (4 * p + 2 * c + d) % 12, :], ps[:, c, :],
                                                       absent[:, d, :], 1.0, -3e38, ALU.add, ALU.max,
                                                       top3[:, d, 2 * p + c:2 * p + c + 1])
                ins.then_inc(masked3, 1)
            dve.wait_ge(masked3, H3 // 2)
            dve.scalar_tensor_tensor(neg_top3[:, :, :], top3[:, :, :], -1.0, score3[:, :, 1, :], ALU.mult, ALU.subtract)\
                .then_inc(neg_top3_ready, 1)
            dve.wait_ge(neg_top3_ready, 1)
            dve.scalar_tensor_tensor(neg_max3[:, :, :], neg_top3[:, :, :], NEG_SLOPE, neg_top3[:, :, :],
                                     ALU.mult, ALU.min).then_inc(neg_max3_ready, 1)
            dve.wait_ge(neg_max3_ready, 1)
            dve.tensor_tensor(shift3[:, :, 0, :], score3[:, :, 1, :], neg_max3[:, :, :], ALU.add)
            dve.tensor_tensor(shift3[:, :, 1, :], fifth3[:, :, 1, :], neg_max3[:, :, :], ALU.add)\
                .then_inc(shift3_ready, 1)
            dve.wait_ge(shift3_ready, 1)
            dve.tensor_copy(dst_parts[:, :, :, 0, :], shift3[:, :, :, :]).then_inc(dst_split, 1)
            dve.wait_ge(dst_split, 1)
            dve.tensor_tensor(dst_parts[:, :, :, 1, :], shift3[:, :, :, :], dst_parts[:, :, :, 0, :].bitcast(F32),
                              ALU.subtract).then_inc(dst_split, 1)

            def invert3(g):
                dve.wait_ge(agg3_done, HG * (g + 1))
                hs = slice(g * HG, (g + 1) * HG)
                for t in range(T):
                    ins = dve.tensor_scalar(denom3[:, t, hs], sums_ps(t, g)[:, :, C3], ATT_EPS, None, ALU.max)
                ins.then_inc(denom3_ready, 1)
                dve.wait_ge(denom3_ready, g + 1)
                dve.reciprocal(rdenom3[:, :, hs], denom3[:, :, hs]).then_inc(rdenom3_ready, 1)

            def scale3(g, t):
                dve.wait_ge(rdenom3_ready, g + 1)
                inverse = rdenom3[:, t, g * HG:(g + 1) * HG].rearrange("p (h a) -> p h a", a=1)\
                    .broadcast_to([P, HG, C3])
                dve.tensor_tensor(y[:, t, g * HG * C3:(g + 1) * HG * C3].rearrange("p (h c) -> p h c", h=HG),
                                  sums_ps(t, g)[:, :, 0:C3], inverse, ALU.mult).then_inc(scaled3, 1)

            dve.wait_ge(count_t_ready, 1)
            for h in range(H3):
                dve.wait_ge(exp3_ready, h + 1)
                if h >= 2:
                    dve.wait_ge(agg3_done, h - 1)
                b = h % 2
                dve.tensor_tensor(weight3[:, b, :, :], exp3[:, b, 0, :, :], exp3[:, b, 1, :, :], ALU.max)\
                    .then_inc(exp3_maxed, 1)
                dve.wait_ge(exp3_maxed, h + 1)
                dve.scalar_tensor_tensor(weight3[:, b, :, :], weight3[:, b, :, :], 1.0, count_t[:, :, :],
                                         ALU.min, ALU.mult).then_inc(weight3_ready, 1)
                if h == HG + 2:
                    invert3(0)
                if h >= HG + 3 and h < HG + 3 + T:
                    scale3(0, h - HG - 3)

            def rectified(t, g):
                dve.wait_ge(summed3[g], t + 1)
                q = slice(g * HG * C3, (g + 1) * HG * C3)
                sum_piece(t, g, dve.scalar_tensor_tensor(y[:, t, q], y[:, t, q], 0.0, x_nat[:, t, q],
                                                         ALU.max, ALU.add))

            for t in range(T):
                rectified(t, 0)
            invert3(1)
            for t in range(T):
                scale3(1, t)
            add_residuals(dve, 1)
            for t in range(T):
                rectified(t, 1)
                variance(3, t)
            normalise(3)

        @block.tensor
        def _(pe):
            def product_d(slots, width, use, per_slot, tiles=range(T), turns=None):
                for t in tiles:
                    for k in range(KD):
                        j = slots + k // per_slot
                        o = (k % per_slot) * width
                        if t == 0 and k % per_slot == 0:
                            pe.wait_ge(split_lo[j], use + 1)
                        if turns is not None and t == 0 and k % 2 == 0:
                            pe.wait_ge(xt_lo_ready, XP * turns + k // 2 + 1)
                        tile_k = slice(t * P, (t + 1) * P)
                        for x_part, w_parts in ((xt_hi, (w_hi, w_lo)), (xt_lo, (w_hi,))):
                            for w_part in w_parts:
                                for at, size in HEAD_PIECES[width]:
                                    to = HEAD_AT[width] + 2 * t * BANK + at
                                    ins = pe.matmul(heads_ps[:, to:to + size],
                                                    x_part[:, k, tile_k], w_part[:, j, o + at:o + at + size],
                                                    start=(k == 0 and x_part is xt_hi and w_part is w_hi),
                                                    stop=(k == KD - 1 and x_part is xt_lo))
                        if k % per_slot == per_slot - 1:
                            yield t, k == KD - 1, ins

            def product_z_last(L):
                i = L.heads - 1
                for k in range(L.blocks):
                    j = 2 + k // L.w2_k
                    o = (k % L.w2_k) * D
                    if k % 2 == 0:
                        pe.wait_ge(z_hi_ready, i * L.pairs + (L.pair + k // 2 + 1))
                    if k % L.w2_k == 0:
                        pe.wait_ge(split_lo[j], i + (L.w2 + 1))
                    for t in range(T):
                        for w_part in (w_hi, w_lo):
                            for at, size in ACC_PIECES[t]:
                                pe.matmul(acc_ps[:, t * D + at:t * D + at + size],
                                          z_hi[:, k, t * P:(t + 1) * P], w_part[:, j, o + at:o + at + size],
                                          start=False, stop=False, skip_group_check=True)
                for t in range(T):
                    for at, size in ACC_PIECES[t]:
                        for k in range(L.blocks):
                            j = 2 + k // L.w2_k
                            o = (k % L.w2_k) * D
                            if t == 0 and at == 0 and k % 2 == 0:
                                pe.wait_ge(z_lo_ready, i * L.pairs + (L.pair + k // 2 + 1))
                            ins = pe.matmul(acc_ps[:, t * D + at:t * D + at + size],
                                            z_lo[:, k, t * P:(t + 1) * P], w_hi[:, j, o + at:o + at + size],
                                            start=False, stop=False, skip_group_check=True)
                        if (t, at) in ((1, 0), (1, D - BANK)):
                            ins.then_inc(w2_used, 1)

            def product_z(L, i, ks):
                for z_part, w_parts, ready in ((z_hi, (w_hi, w_lo), z_hi_ready), (z_lo, (w_hi,), z_lo_ready)):
                    for k in ks:
                        j = 2 + k // L.w2_k
                        o = (k % L.w2_k) * D
                        if k % 2 == 0:
                            pe.wait_ge(ready, i * L.pairs + (L.pair + k // 2 + 1))
                        if k % L.w2_k == 0 and z_part is z_hi:
                            pe.wait_ge(split_lo[j], i + (L.w2 + 1))
                        for t in range(T):
                            for w_part in w_parts:
                                for at, size in ACC_PIECES[t]:
                                    ins = pe.matmul(acc_ps[:, t * D + at:t * D + at + size],
                                                    z_part[:, k, t * P:(t + 1) * P],
                                                    w_part[:, j, o + at:o + at + size],
                                                    start=False, stop=False, skip_group_check=True)
                        if k % L.w2_k == L.w2_k - 1 and z_part is z_lo:
                            ins.then_inc(w2_used, 1)

            def spread_scores(a):
                pe.wait_ge(diag_ready, a + 1)
                pe.matmul(misc_ps[:, 0:N], ones[:, :], score_diag[:, :, :].rearrange("p t n -> p (t n)"),
                          start=True, stop=True).then_inc(scores_spread, 1)

            def turn_attention(a, ready, value):
                pe.wait_ge(ready, value)
                for s in range(T):
                    for d in range(T):
                        o = s * N + d * P
                        ins = pe.transpose(misc_ps[:, o:o + P], attn[:, d, s * P:(s + 1) * P], ident[:, :])
                ins.then_inc(attn_turned, 1)

            def turn_padded():
                pe.wait_ge(padded_landed, 16 * 8)
                for n in range(5):
                    ins = pe.transpose(acc_ps[:, n * P:(n + 1) * P], padded[:, n, :], ident[:, :])
                ins.then_inc(padded_turned, 1)

            def turn_conv():
                pe.wait_ge(padded_copied, 1)
                pe.matmul(acc_ps[:, BANK + 2 * P:BANK + 2 * P + 2 * H3], padded[:, 2, :], attn3_t[:, :],
                          start=True, stop=True).then_inc(w3_scored, 1)
                pe.wait_ge(conv_scaled, 1)
                for s in range(T):
                    for d in range(T):
                        o = s * N + d * P
                        ins = pe.transpose(misc_ps[:, o:o + P], attn[:, d, s * P:(s + 1) * P], ident[:, :])
                ins.then_inc(conv_turned, 1)

            def count_chunk(b, start, stop):
                for t in range(T):
                    ins = pe.matmul(misc_ps[:, t * N:(t + 1) * N], onehot[:, b, 0, t * P:(t + 1) * P],
                                    onehot[:, b, 1, :], start=start and t == 0, stop=stop and t == T - 1,
                                    skip_group_check=True)
                ins.then_inc(onehot_used, 1)

            def keep_warm(ps, count):
                for _ in range(count):
                    pe.matmul(ps, zeros[:, :], xt_hi[:, 0:2, :].rearrange("p k n -> p (k n)"),
                              start=True, stop=True)

            def head(L, i):
                a = i + L.att
                first = L is L0 and isinstance(i, int) and i == 0
                fresh = isinstance(i, int) and i == 0
                ahead = L is L2
                if ahead and not fresh:
                    tiles = range(1, T)
                else:
                    tiles = range(T)
                    if not fresh:
                        pe.wait_ge(z_ready, i * L.pairs + (L.pair + 1 - L.pairs))
                turns = (0 if first else 2) if fresh else None
                for t, tile_done, ins in product_d(0, L.width, i + L.w1, L.w1_k, tiles, turns):
                    if tile_done:
                        ins.then_inc(h_done, 1)
                        if t == 0 and not fresh:
                            pe.wait_ge(z_ready, i * L.pairs + L.pair)
                        if t == 0 and first:
                            for c in range(EC - RING, EC):
                                pe.wait_ge(onehot_ready, c + 1)
                                count_chunk(c % RING, False, False)
                    elif t == 0 and first:
                        turn_padded()
                if first:
                    turn_conv()
                if fresh:
                    pe.wait_ge(h_copied, a * T + 1)
                    keep_warm(heads_ps[:, 0:BANK], WARM_HEAD)
                if first:
                    pe.wait_ge(conv_ready, T)
                if not fresh:
                    product_z(L, i - 1, range(0, 2))
                spread_scores(a)
                if fresh:
                    keep_warm(heads_ps[:, 0:BANK], WARM_HEAD)
                    if first:
                        pe.wait_ge(w3_ready, 1)
                    clear_sums()
                else:
                    product_z(L, i - 1, range(2, L.blocks if ahead else L.blocks - 1))
                next_tile = None
                if ahead and not (isinstance(i, int) and i == L.heads - 1):
                    next_tile = product_d(0, L.width, i + (L.w1 + 1), L.w1_k, range(1))
                    next(next_tile)
                alone = first or (ahead and isinstance(i, int) and i == L.heads - 1)
                if alone:
                    keep_warm(heads_ps[:, 0:BANK], WARM_HEAD if first else WARM_HEAD // 3)
                turn_attention(a, attn_ready, i + (L.head + 1))
                if alone:
                    keep_warm(heads_ps[:, 0:BANK], WARM_HEAD // 2)
                if next_tile is not None:
                    t, tile_done, ins = next(next_tile)
                    ins.then_inc(h_done, 1)
                if not fresh and not ahead:
                    product_z(L, i - 1, range(L.blocks - 1, L.blocks))
                pe.wait_ge(h_lo_ready, i + (L.head + 1))
                pe.wait_ge(at_lo_ready, i + (L.head + 1))
                for p in range(L.pairs):
                    for c in range(2):
                        block_k = slice((2 * p + c) * P, (2 * p + c + 1) * P)
                        for s in range(T):
                            for h_part, a_part in ((h_hi, at_hi), (h_hi, at_lo), (h_lo, at_hi)):
                                ins = pe.matmul(pair_ps(heads_ps, AGG_BANK[p])[:, c, :], h_part[:, s, block_k],
                                                a_part[:, s, :], start=(s == 0 and a_part is at_hi and h_part is h_hi),
                                                stop=(s == T - 1 and h_part is h_lo))
                    ins.then_inc(agg_done, 1)

            def clear_sums():
                for b in range(3):
                    pe.matmul(acc_ps[:, b * BANK:(b + 1) * BANK], zeros[:, :],
                              xt_hi[:, 0:2, :].rearrange("p k n -> p (k n)"), start=True, stop=False,
                              skip_group_check=True)

            def second_attention(L, l):
                a = L.att + L.heads
                keep_warm(heads_ps[:, 0:BANK], WARM_SCORES)
                spread_scores(a)
                keep_warm(heads_ps[:, 0:BANK], WARM_SOFTMAX)
                turn_attention(a, exp_counted, a + 1)
                pe.wait_ge(h_copied, T * (a + 1))
                pe.wait_ge(at_f32_ready, l // 2 + 1)
                for t in range(T):
                    for at, size in HEAD_PIECES[D]:
                        for s in range(T):
                            ins = pe.matmul(heads_ps[:, 2 * t * BANK + at:2 * t * BANK + at + size],
                                            at_f32[:, s, t * P:(t + 1) * P], h_raw[:, s, at:at + size],
                                            start=(s == 0), stop=(s == T - 1))
                        ins.then_inc(out_done, 1)

            def turn_x(ready, values):
                for t in range(T):
                    pe.wait_ge(ready, values[t])
                    for p in range(XP):
                        for c in range(2):
                            k = 2 * p + c
                            ins = pe.transpose(pair_ps(acc_ps, p)[:, c, t * P:(t + 1) * P],
                                               x_nat[:, t, k * P:(k + 1) * P], ident[:, :])
                        if t == T - 1:
                            ins.then_inc(xt_turned, 1)

            for c in range(LEAD):
                pe.wait_ge(onehot_ready, c + 1)
                count_chunk(c % RING, c == 0, False)
            pe.wait_ge(consts_ready, 1)
            turn_x(x_landed, [16] * T)
            with pe.Fori(0, (EC - LEAD) // RING - 1) as g:
                for b in range(RING):
                    pe.wait_ge(onehot_ready, g * RING + (LEAD + b + 1))
                    count_chunk((LEAD + b) % RING, False, False)

            head(L0, 0)
            with pe.Fori(1, L0.heads) as i:
                head(L0, i)
            product_z_last(L0)
            second_attention(L0, 0)
            keep_warm(misc_ps[:, :], WARM_NORM)
            pe.wait_ge(x_ready, T)
            for p in range(XP):
                for c in range(2):
                    k = 2 * p + c
                    for s in range(T):
                        ins = pe.matmul(pair_ps(acc_ps, p)[:, c, :], x_nat[:, s, k * P:(k + 1) * P],
                                        conv_t[:, s, :], start=(s == 0), stop=(s == T - 1))
                ins.then_inc(xt_turned, 1)
            for t, tile_done, ins in product_d(2, D, H0, KU, turns=1):
                if tile_done:
                    ins.then_inc(out_done, 2)
            keep_warm(misc_ps[:, :], WARM_NORM)
            turn_x(x_ready, [T * 1 + t + 1 for t in range(T)])
            head(L2, 0)
            with pe.Fori(1, L2.heads - 1) as i:
                head(L2, i)
            head(L2, L2.heads - 1)
            product_z_last(L2)
            second_attention(L2, 2)
            for s in range(T):
                for d in range(T):
                    o = s * N + d * P
                    ins = pe.transpose(misc_ps[:, o:o + P], count[:, d, s * P:(s + 1) * P], ident[:, :])
            ins.then_inc(count_turned, 1)
            keep_warm(acc_ps[:, 0:BANK], WARM_NORM)
            turn_x(x_ready, [T * 2 + t + 1 for t in range(T)])
            pe.wait_ge(w3_widened, 1)
            for t in range(T):
                for k in range(KD):
                    if t == 0 and k % 2 == 0:
                        pe.wait_ge(xt3_ready, k // 2 + 1)
                    ins = pe.matmul(wide_ps(t, k // (KD // 2))[:, k % (KD // 2), :],
                                    xt3[:, k, t * P:(t + 1) * P], w3_wide[:, k, :], start=True, stop=True)
                ins.then_inc(ft3_done, 1)
            pe.wait_ge(src_split, 2)
            pe.wait_ge(count_t_ready, 1)
            for t in range(T):
                ins = pe.transpose(misc_ps[0:2 * H3, t * P:(t + 1) * P],
                                   src_parts[:, t, :, :].bitcast(F32).rearrange("p a h -> p (a h)"), ident[:, :])
            ins.then_inc(src_turned, 1)
            pe.wait_ge(sel_ready, 1)
            pe.wait_ge(src_rows_ready, 1)
            for p in range(H3 // 2):
                if p == 4:
                    pe.wait_ge(ft3_ready, T * 2)
                    for t in range(T):
                        for k in range(KD):
                            o = 2 * t * BANK + k * P
                            ins = pe.matmul(heads_ps[:, o:o + P], xt3[:, k, t * P:(t + 1) * P], w3res[:, :],
                                            start=True, stop=True)
                    ins.then_inc(res3_done, 1)
                if p >= 4:
                    pe.wait_ge(masked3, p - 2)
                for c in range(2):
                    ins = pe.matmul(src_bank(p)[:, c, :], sel3[:, 2 * p + c, :], src_rows, start=True, stop=True)
                ins.then_inc(src_spread, 1)
            keep_warm(misc_ps[:, :], WARM_SHIFTS)
            pe.wait_ge(dst_split, 2)
            for r in range(2):
                for t in range(T):
                    o = r * N + t * P
                    ins = pe.transpose(misc_ps[0:2 * H3, o:o + P],
                                       dst_parts[:, t, r, :, :].bitcast(F32).rearrange("p a h -> p (a h)"), ident[:, :])
            ins.then_inc(dst_turned, 1)
            pe.wait_ge(dst_rows_ready, 1)
            pe.wait_ge(res3_ready, T)
            pe.wait_ge(masked3, H3 // 2)

            def spread3(h):
                if h >= 3:
                    pe.wait_ge(exp3_ready, h - 2)
                pe.matmul(acc_ps[:, h % 3 * BANK:(h % 3 + 1) * BANK], sel3[:, h, :], dst_rows,
                          start=True, stop=True).then_inc(dst_spread, 1)

            def aggregate3(h):
                pe.wait_ge(weight3_ready, h + 1)
                for t in range(T):
                    for s in range(T):
                        ins = pe.matmul(sums_ps(t, h // HG)[:, h % HG, :], weight3[:, h % 2, s, t * P:(t + 1) * P],
                                        ft3[:, s, h, :], start=(s == 0), stop=(s == T - 1))
                ins.then_inc(agg3_done, 1)

            for h in range(H3 + 3):
                if h < H3:
                    spread3(h)
                if h == 2:
                    keep_warm(misc_ps[:, :], WARM_EXPS)
                if h >= 3:
                    aggregate3(h - 3)
                    if h < H3:
                        keep_warm(misc_ps[:, :], WARM_HEAD3)


_INS = ["x", "src", "dst",
        "L0_gnn_W1", "L0_gnn_a_src1", "L0_gnn_a_dst1", "L0_gnn_b1",
        "L0_gnn_W2", "L0_gnn_a_src2", "L0_gnn_a_dst2", "L0_gnn_b2",
        "L1_gnn_W", "L1_gnn_b",
        "L2_gnn_W1", "L2_gnn_att_src1", "L2_gnn_att_dst1", "L2_gnn_b1",
        "L2_gnn_W2", "L2_gnn_att_src2", "L2_gnn_att_dst2", "L2_gnn_b2",
        "L3_gnn_W", "L3_gnn_attn_l", "L3_gnn_attn_r", "L3_gnn_W_res"]


def kernel(**inputs):
    import numpy as np
    import concourse.bacc as bacc
    from concourse.bass_utils import run_bass_kernel_spmd

    nc = bacc.Bacc("TRN2", target_bir_lowering=False, num_devices=1)
    arrays, args = {}, []
    for name in _INS:
        a = np.ascontiguousarray(inputs[name])
        arrays[f"in_{name}"] = a
        args.append(nc.dram_tensor(f"in_{name}", a.shape, mybir.dt.from_np(a.dtype), kind="ExternalInput").ap())
    out = nc.dram_tensor("out", inputs["x"].shape, F32, kind="ExternalOutput").ap()
    gnn_kernel(nc, *args, out)
    return run_bass_kernel_spmd(nc, [arrays], core_ids=[0]).results[0]["out"]
```

```python
from contextlib import ExitStack

import concourse.bass as bass
from concourse import mybir

F32 = mybir.dt.float32
F32R = mybir.dt.float32r
BF16 = mybir.dt.bfloat16
I32 = mybir.dt.int32
ALU = mybir.AluOpType
ACT = mybir.ActivationFunctionType

P = 128
BANK = 512
NEG_SLOPE = 0.2
ATT_EPS = 1e-16
LN_EPS = 1e-5
MASKED = -1e30


class GatLayer:

    def __init__(self, heads, width, att, head, pair, w1, w2, w2_used, w1_k, w2_k):
        self.heads, self.width = heads, width
        self.att, self.head, self.pair = att, head, pair
        self.w1, self.w2, self.w2_used = w1, w2, w2_used
        self.w1_k, self.w2_k = w1_k, w2_k
        self.blocks = width // P
        self.pairs = self.blocks // 2

    def steps(self, i):
        last = isinstance(i, int) and i == self.heads - 1
        return last, self.blocks if last else self.pairs


def gnn_kernel(nc, x, src, dst,
               l0_w1, l0_as1, l0_ad1, l0_b1, l0_w2, l0_as2, l0_ad2, l0_b2,
               l1_w, l1_b,
               l2_w1, l2_as1, l2_ad1, l2_b1, l2_w2, l2_as2, l2_ad2, l2_b2,
               l3_w, l3_al, l3_ar, l3_wres, out):
    N, D = x.shape
    T = N // P
    KD = D // P
    XP = KD // 2
    EC = src.shape[0] // P
    H0, C0 = l0_as1.shape
    H2, C2 = l2_as1.shape
    H3, C3 = l3_al.shape[1], l3_al.shape[2]
    assert T == 2 and KD % 2 == 0 and C0 == D and H3 * C3 == D and 2 * C3 == P and EC % 2 == 0
    KU = KD // 2
    UNIT = KU * D
    RING = T * D // N
    LEAD = EC % RING + RING
    LATE = 3 * RING

    L0 = GatLayer(H0, C0, att=0, head=0, pair=0, w1=0, w2=0, w2_used=0, w1_k=KU, w2_k=KU)
    L2 = GatLayer(H2, C2, att=H0 + 1, head=H0, pair=H0 * L0.pairs + L0.blocks - L0.pairs, w1=H0, w2=H0 + 1,
                  w2_used=2 * H0, w1_k=KU, w2_k=C2 // P // 2)

    HEAD_PIECES = {D: [(0, BANK), (BANK, D - BANK)], C2: [(0, C2)]}
    HEAD_AT = {D: 0, C2: BANK}
    ACC_PIECES = [[(0, BANK), (BANK, D - BANK)], [(0, D - BANK), (D - BANK, BANK)]]

    with ExitStack() as ctx:
        def sb(name, shape, dt=F32):
            return ctx.enter_context(nc.sbuf_tensor(name, shape, dt))

        def sem(name):
            return ctx.enter_context(nc.semaphore(name))

        w_raw = sb("w_raw", [P, 4, UNIT])
        w_hi = sb("w_hi", [P, 4, UNIT], F32R)
        w_lo = sb("w_lo", [P, 4, UNIT], F32R)
        x_nat = sb("x_nat", [P, T, D])
        xb = sb("xb", [P, T, D])
        xt_hi = sb("xt_hi", [P, KD, N], F32R)
        xt_lo = sb("xt_lo", [P, KD, N], F32R)
        h_raw = sb("h_raw", [P, T, D])
        h_hi = sb("h_hi", [P, T, D], F32R)
        h_lo = sb("h_lo", [P, T, D], F32R)
        z = sb("z", [P, KD, N])
        z_pos = sb("z_pos", [P, 2, N])
        z_hi = sb("z_hi", [P, KD, N], F32R)
        z_lo = sb("z_lo", [P, KD, N], F32R)
        att_vec = sb("att_vec", [P, 2, D])
        product = sb("product", [P, 2, D], BF16)
        count = sb("count", [P, T, N])
        absent = sb("absent", [P, T, N])
        count_loop = sb("count_loop", [P, T, N])
        absent_loop = sb("absent_loop", [P, T, N])
        conv_t = sb("conv_t", [P, T, N])
        score_src = sb("score_src", [P, T])
        score_dst = sb("score_dst", [P, T])
        logit = sb("logit", [P, T, N])
        top = sb("top", [P, T])
        neg_top = sb("neg_top", [P, T])
        neg_max = sb("neg_max", [P, T])
        expd = sb("expd", [P, T, N])
        attn = sb("attn", [P, T, N])
        denom = sb("denom", [P, T])
        rdenom = sb("rdenom", [P, T])
        at_hi = sb("at_hi", [P, T, N], F32R)
        at_lo = sb("at_lo", [P, T, N], F32R)
        NB = L0.heads * L0.blocks + L2.heads * L2.blocks
        bias_col = sb("bias_col", [P, 3, NB])
        bias_now = sb("bias_now", [P, 3, L0.blocks])
        y = z[:, :, :].rearrange("p k n -> p (k n)").rearrange("p (t d) -> p t d", t=T)
        stats = sb("stats", [P, T, 2, 6])
        mean_var = sb("mean_var", [P, T, 2])
        var_eps = sb("var_eps", [P, T])
        rstd = sb("rstd", [P, T])
        minus_half = sb("minus_half", [P, T])
        ident = sb("ident", [P, P])
        zeros = sb("zeros", [P, P], F32R)
        iota_i = sb("iota_i", [P, N], I32)
        iota_b = sb("iota_b", [P, N], BF16)
        edge_i = sb("edge_i", [P, 2, EC], I32)
        edge_f = sb("edge_f", [P, 2, EC])
        degree = sb("degree", [P, T])
        dinv = sb("dinv", [P, T])
        w3 = sb("w3", [P, P])
        w3res = sb("w3res", [P, P])
        attn3_t = sb("attn3_t", [P, 2 * H3])
        w3_att = sb("w3_att", [P, KD, 4])
        onehot = h_raw[:, :, :].rearrange("p t d -> p (t d)").bitcast(BF16)[:, 0:RING * 2 * N]\
            .rearrange("p (c e n) -> p c e n", c=RING, e=2)
        padded = z[:, :, :].rearrange("p k n -> p (k n)")[:, 0:5 * P].rearrange("p (a n) -> p a n", a=5)
        HG = H3 // 2
        KC = P + 4
        whole = w_raw[:, :, :].rearrange("p a n -> p (a n)")
        taken = [0]

        def cut(size):
            taken[0] += size
            return whole[:, taken[0] - size:taken[0]]

        xt3 = cut(KD * N).rearrange("p (k n) -> p k n", k=KD)
        w3_wide = cut(KD * KC).rearrange("p (k n) -> p k n", k=KD)
        ft3 = cut(T * H3 * (C3 + 1)).rearrange("p (t h c) -> p t h c", t=T, h=H3)
        count_t = cut(T * N).rearrange("p (t n) -> p t n", t=T)
        exp3 = cut(2 * 2 * T * N).rearrange("p (b e t n) -> p b e t n", b=2, e=2, t=T)
        weight3 = cut(2 * T * N).rearrange("p (b t n) -> p b t n", b=2, t=T)
        discard3 = z[:, :, :].rearrange("p k n -> p (k n)").bitcast(BF16).rearrange("p (j n) -> p j n", n=N)
        sel3 = w_hi[0:2 * H3, 0, 0:H3 * P].rearrange("p (h n) -> p h n", h=H3)
        dst_rows = w_hi[0:2 * H3, 1, 0:2 * N]
        dst_parts = w_hi[:, 2, 0:T * 4 * H3].rearrange("p (t r a h) -> p t r a h", t=T, r=2, a=2)
        sel_col = sb("sel_col", [P, H3])
        score3 = sb("score3", [P, T, 2, H3])
        fifth3 = sb("fifth3", [P, T, 2, H3])
        top3 = sb("top3", [P, T, H3])
        neg_top3 = sb("neg_top3", [P, T, H3])
        neg_max3 = sb("neg_max3", [P, T, H3])
        shift3 = sb("shift3", [P, T, 2, H3])
        denom3 = sb("denom3", [P, T, H3])
        rdenom3 = sb("rdenom3", [P, T, H3])

        heads_ps = ctx.enter_context(nc.psum_tensor("heads_ps", [P, 4 * BANK], F32))
        acc_ps = ctx.enter_context(nc.psum_tensor("acc_ps", [P, 3 * BANK], F32))
        misc_ps = ctx.enter_context(nc.psum_tensor("misc_ps", [P, BANK], F32))
        AGG_BANK = [0, 2, 3]
        LAST_AGG = [heads_ps[:, b * BANK:b * BANK + N] for b in range(4)] + [misc_ps[:, 0:N], heads_ps[:, N:2 * N]]
        WARM_HEAD, WARM_SCORES, WARM_SOFTMAX, WARM_NORM, WARM_SHIFTS, WARM_EXPS = 8, 12, 14, 10, 15, 12
        WARM_START, WARM_HEAD3 = 18, 2

        x_landed = sem("x_landed")
        edges_landed = sem("edges_landed")
        padded_landed = sem("padded_landed")
        bias_landed = sem("bias_landed")
        vec_landed = sem("vec_landed")
        raw_landed = [sem(f"raw_landed{j}") for j in range(4)]
        split_hi = [sem(f"split_hi{j}") for j in range(4)]
        split_lo = [sem(f"split_lo{j}") for j in range(4)]
        consts_zeroed = sem("consts_zeroed")
        consts_ready = sem("consts_ready")
        padded_zeroed = sem("padded_zeroed")
        iota_ready = sem("iota_ready")
        edges_ready = sem("edges_ready")
        onehot_ready = sem("onehot_ready")
        onehot_used = sem("onehot_used")
        count_ready = sem("count_ready")
        degree_ready = sem("degree_ready")
        dinv_ready = sem("dinv_ready")
        conv_scaled = sem("conv_scaled")
        conv_turned = sem("conv_turned")
        conv_ready = sem("conv_ready")
        padded_turned = sem("padded_turned")
        padded_copied = sem("padded_copied")
        w3_scored = sem("w3_scored")
        w3_ready = sem("w3_ready")
        bias_now_ready = sem("bias_now_ready")
        xt_turned = sem("xt_turned")
        xt_hi_ready = sem("xt_hi_ready")
        xt_lo_ready = sem("xt_lo_ready")
        h_done = sem("h_done")
        w2_used = sem("w2_used")
        h_copied = sem("h_copied")
        h_hi_ready = sem("h_hi_ready")
        h_lo_ready = sem("h_lo_ready")
        scores_ready = sem("scores_ready")
        scores_spread = sem("scores_spread")
        logit_masked = sem("logit_masked")
        logit_summed = sem("logit_summed")
        logit_ready = sem("logit_ready")
        exp_ready = sem("exp_ready")
        exp_counted = sem("exp_counted")
        rdenom_ready = sem("rdenom_ready")
        attn_ready = sem("attn_ready")
        attn_turned = sem("attn_turned")
        at_hi_ready = sem("at_hi_ready")
        at_lo_ready = sem("at_lo_ready")
        h2_hi_ready = sem("h2_hi_ready")
        h2_lo_ready = sem("h2_lo_ready")
        at2_hi_ready = sem("at2_hi_ready")
        at2_lo_ready = sem("at2_lo_ready")
        agg_done = sem("agg_done")
        elu_exp = sem("elu_exp")
        elu_pos = sem("elu_pos")
        z_ready = sem("z_ready")
        z_hi_ready = sem("z_hi_ready")
        z_lo_ready = sem("z_lo_ready")
        out_done = sem("out_done")
        y_ready = sem("y_ready")
        stats_ready = sem("stats_ready")
        var_ready = sem("var_ready")
        eps_added = sem("eps_added")
        rstd_ready = sem("rstd_ready")
        x_ready = sem("x_ready")
        xb_ready = sem("xb_ready")
        w3_widened = sem("w3_widened")
        count_turned = sem("count_turned")
        count_t_ready = sem("count_t_ready")
        sel_col_ready = sem("sel_col_ready")
        sel_ready = sem("sel_ready")
        xt3_ready = sem("xt3_ready")
        ft3_done = sem("ft3_done")
        ft3_ready = sem("ft3_ready")
        res3_done = sem("res3_done")
        res3_ready = sem("res3_ready")
        score3_ready = sem("score3_ready")
        src_spread = sem("src_spread")
        masked3 = sem("masked3")
        neg_top3_ready = sem("neg_top3_ready")
        neg_max3_ready = sem("neg_max3_ready")
        shift3_ready = sem("shift3_ready")
        dst_split = sem("dst_split")
        dst_turned = sem("dst_turned")
        dst_rows_ready = sem("dst_rows_ready")
        dst_spread = sem("dst_spread")
        exp3_ready = sem("exp3_ready")
        exp3_maxed = sem("exp3_maxed")
        weight3_ready = sem("weight3_ready")
        agg3_done = sem("agg3_done")
        denom3_ready = sem("denom3_ready")
        rdenom3_ready = sem("rdenom3_ready")
        scaled3 = sem("scaled3")
        first_summed3 = sem("first_summed3")
        first_rectified3 = sem("first_rectified3")
        first_ready3 = sem("first_ready3")
        summed3 = sem("summed3")
        stored = sem("stored")

        block = ctx.enter_context(nc.Block())

        def pair_ps(ps, p):
            return ps[:, p * BANK:(p + 1) * BANK].rearrange("p (c n) -> p c n", c=2)

        def src_bank(p):
            return pair_ps(misc_ps, 0) if p == 0 else pair_ps(acc_ps, p % 3)

        def wide_ps(t, g):
            o = (2 * t + g) * BANK
            return heads_ps[:, o:o + KD // 2 * KC].rearrange("p (k n) -> p k n", k=KD // 2)

        def features_ps(t, g):
            return wide_ps(t, g)[:, :, 0:P].rearrange("p k (c n) -> p k c n", c=2)

        def sums_ps(t, g):
            o = (2 * t + g) * BANK
            return heads_ps[:, o:o + HG * (C3 + 1)].rearrange("p (h n) -> p h n", h=HG)

        def step_ps(last, u):
            return LAST_AGG[u].rearrange("p (c n) -> p c n", c=1) if last else pair_ps(heads_ps, AGG_BANK[u])

        def step_blocks(last, u):
            return slice(u, u + 1) if last else slice(2 * u, 2 * u + 2)

        def spread(row, rows=P):
            return row.rearrange("(a n) -> a n", a=1).broadcast_to([rows, row.shape[0]])

        @block.sync
        def _(sp):
            def load_first(L, w1, i):
                w = w1.rearrange("(k p) n -> p k n", p=P)
                for j in range(2):
                    if not (L is L0 and isinstance(i, int) and i == 0):
                        sp.wait_ge(split_lo[j], i + L.w1)
                    sp.dma_start(
                        w_raw[:, j, 0:L.w1_k * L.width].rearrange("p (k n) -> p k n", k=L.w1_k),
                        w[:, j * L.w1_k:(j + 1) * L.w1_k, bass.ds(i * L.width, L.width)],
                    ).then_inc(raw_landed[j], 16)

            def load_second(L, w2, i):
                w = w2.rearrange("(k p) n -> p k n", p=P)
                for j in range(2):
                    if not (L is L0 and isinstance(i, int) and i == 0):
                        sp.wait_ge(split_lo[2 + j], i + L.w2)
                    sp.dma_start(
                        w_raw[:, 2 + j, 0:L.w2_k * D].rearrange("p (k n) -> p k n", k=L.w2_k),
                        w[:, bass.ds(i * L.blocks + j * L.w2_k, L.w2_k), :],
                    ).then_inc(raw_landed[2 + j], 16)

            def load_vectors(L, a_src, a_dst, i):
                width = a_src.shape[1]
                if not (L is L0 and isinstance(i, int) and i == 0):
                    sp.wait_ge(scores_ready, i * 2 * T + 2 * T * L.att)
                for e, a in enumerate((a_src, a_dst)):
                    row = a[bass.ds(i, 1), :] if a.shape[0] > 1 else a[0:1, :]
                    sp.dma_start(att_vec[:, e, 0:width], row.broadcast_to([P, width]))\
                        .then_inc(vec_landed, 16)

            def load_vectors2(L, a_src, a_dst):
                sp.wait_ge(scores_ready, 2 * T * (L.att + L.heads))
                for e, a in enumerate((a_src, a_dst)):
                    sp.dma_start(att_vec[:, e, :], a[0:1, :].broadcast_to([P, D])).then_inc(vec_landed, 16)

            def load_bias(l, b):
                if l:
                    sp.wait_ge(y_ready, 2 * T * l)
                for t in range(T):
                    sp.dma_start(xb[:, t, :], spread(b)).then_inc(bias_landed, 16)

            sp.dma_start(edge_i[:, 0, :], dst.rearrange("(p c) -> p c", p=P)).then_inc(edges_landed, 16)
            sp.dma_start(x_nat[:, :, :], x.rearrange("(t p) n -> p t n", p=P)).then_inc(x_landed, 16)
            load_first(L0, l0_w1, 0)
            sp.wait_ge(padded_zeroed, 1)
            nb0 = L0.heads * L0.blocks
            nb2 = L2.heads * L2.blocks
            sp.dma_start(padded[0:nb0, 0, :], l0_b1.rearrange("(a p) -> a p", p=P)).then_inc(padded_landed, 16)
            sp.dma_start(padded[0:nb2, 1, :], l2_b1.rearrange("(a p) -> a p", p=P)).then_inc(padded_landed, 16)
            for c in range(2):
                sp.dma_start(padded[0:C3, 2, c * C3:(c + 1) * C3], l3_w).then_inc(padded_landed, 16)
                sp.dma_start(padded[0:C3, 3, c * C3:(c + 1) * C3], l3_wres).then_inc(padded_landed, 16)
            sp.dma_start(padded[0:H3, 4, 0:C3], l3_al[0, :, :]).then_inc(padded_landed, 16)
            sp.dma_start(padded[H3:2 * H3, 4, 0:C3], l3_ar[0, :, :]).then_inc(padded_landed, 16)
            load_vectors(L0, l0_as1, l0_ad1, 0)
            load_second(L0, l0_w2, 0)
            load_bias(0, l0_b2)
            load_first(L0, l0_w1, 1)
            with sp.Fori(1, L0.heads - 1) as i:
                load_vectors(L0, l0_as1, l0_ad1, i)
                load_first(L0, l0_w1, i + 1)
                load_second(L0, l0_w2, i)
            load_vectors(L0, l0_as1, l0_ad1, H0 - 1)
            load_first(L2, l2_w1, 0)
            load_second(L0, l0_w2, H0 - 1)
            load_vectors2(L0, l0_as2, l0_ad2)
            w = l1_w.rearrange("(k p) n -> p k n", p=P)
            for j in range(2):
                sp.wait_ge(split_lo[2 + j], H0)
                sp.dma_start(w_raw[:, 2 + j, :].rearrange("p (k n) -> p k n", k=KU),
                             w[:, j * KU:(j + 1) * KU, :]).then_inc(raw_landed[2 + j], 16)
            load_first(L2, l2_w1, 1)
            load_vectors(L2, l2_as1, l2_ad1, 0)
            load_bias(1, l1_b)
            load_second(L2, l2_w2, 0)
            load_bias(2, l2_b2)
            with sp.Fori(1, L2.heads - 1) as i:
                load_vectors(L2, l2_as1, l2_ad1, i)
                load_first(L2, l2_w1, i + 1)
                load_second(L2, l2_w2, i)
            load_vectors(L2, l2_as1, l2_ad1, H2 - 1)
            load_second(L2, l2_w2, H2 - 1)
            load_vectors2(L2, l2_as2, l2_ad2)
            for t in range(T):
                sp.wait_ge(x_ready, T * 3 + t + 1)
                sp.dma_start(out[t * P:(t + 1) * P, :], x_nat[:, t, :]).then_inc(stored, 16)
            sp.wait_ge(stored, 16 * T)

        @block.scalar
        def _(act):
            act.dma_start(edge_i[:, 1, :], src.rearrange("(p c) -> p c", p=P)).then_inc(edges_landed, 16)

            def split_slot(j, use, size):
                act.wait_ge(raw_landed[j], 16 * use + 16)
                act.activation(w_hi[:, j, 0:size], w_raw[:, j, 0:size], ACT.Copy).then_inc(split_hi[j], 1)

            def first_slots(L, i):
                for j in range(2):
                    if not (L is L0 and isinstance(i, int) and i == 0):
                        act.wait_ge(h_done, T * (L.head + i))
                    split_slot(j, i + L.w1, L.w1_k * L.width)

            def second_slot(L, i, j):
                if L is L2 and isinstance(i, int) and i == 0:
                    act.wait_ge(out_done, 2 * T * 2)
                elif not (isinstance(i, int) and i == 0):
                    act.wait_ge(w2_used, i * 2 + (L.w2_used - 2 + j + 1))
                split_slot(2 + j, i + L.w2, L.w2_k * D)

            def xt_high(e):
                for p in range(XP):
                    act.wait_ge(xt_turned, XP * e + p + 1)
                    act.activation(xt_hi[:, 2 * p:2 * p + 2, :], pair_ps(acc_ps, p), ACT.Copy)\
                        .then_inc(xt_hi_ready, 1)

            def exps(a):
                act.wait_ge(logit_ready, 2 * a + 2)
                for d in range(T):
                    act.activation(expd[:, d, :], logit[:, d, :], ACT.Exp, bias=neg_max[:, d:d + 1])\
                        .then_inc(exp_ready, 1)

            def copy_h(L, i, t):
                first = L is L0 and isinstance(i, int) and i == 0
                act.wait_ge(h_done, (i + L.head) * T + t + 1)
                if t == 0 and not first:
                    act.wait_ge(h_lo_ready, i + L.head)
                if t == 0 and first:
                    act.wait_ge(onehot_used, EC)
                at = HEAD_AT[L.width] + 2 * t * BANK
                act.activation(h_raw[:, t, 0:L.width], heads_ps[:, at:at + L.width], ACT.Copy)\
                    .then_inc(h_copied, 1)

            def head(L, i, next_first):
                a = i + L.att
                first = L is L0 and isinstance(i, int) and i == 0
                last = isinstance(i, int) and i == L.heads - 1
                for t in range(T):
                    if t or L is L0 or (isinstance(i, int) and i == 0):
                        copy_h(L, i, t)
                    act.wait_ge(h_copied, a * T + t + 1)
                    act.activation(h_hi[:, t, 0:L.width], h_raw[:, t, 0:L.width], ACT.Copy)\
                        .then_inc(h_hi_ready, 1)
                if next_first is not None:
                    first_slots(*next_first)
                exps(a)
                second_slot(L, i, 0)
                act.wait_ge(attn_turned, a + 1)
                act.activation(at_hi[:, :, :].rearrange("p s n -> p (s n)"), misc_ps[:, :], ACT.Copy)\
                    .then_inc(at_hi_ready, 1)
                if last or L is L2:
                    second_slot(L, i, 1)
                if L is L2 and not last:
                    copy_h(L, i + 1, 0)
                act.wait_ge(bias_now_ready, i + (L.head + 1))

                last, steps = L.steps(i)

                def elu_exponential(u):
                    act.wait_ge(agg_done, i * L.pairs + (L.pair + u + 1))
                    blocks = step_blocks(last, u)
                    if not first:
                        before = blocks.start // 2 + 1 - L.pairs
                        act.wait_ge(z_lo_ready, L.pair if isinstance(i, int) and i == 0 else i * L.pairs + (L.pair + before))
                    for k in range(blocks.start, blocks.stop):
                        act.activation(z[:, k, :], step_ps(last, u)[:, k - blocks.start, :], ACT.Exp,
                                       bias=bias_now[:, 0, k:k + 1]).then_inc(elu_exp, 2 if last else 1)

                def z_high(u):
                    act.wait_ge(z_ready, i * L.pairs + (L.pair + u + 1))
                    act.activation(z_hi[:, step_blocks(last, u), :], z[:, step_blocks(last, u), :], ACT.Copy)\
                        .then_inc(z_hi_ready, 1)

                for u in range(steps):
                    elu_exponential(u)
                    if u:
                        z_high(u - 1)
                z_high(steps - 1)
                if L is L0 and not last:
                    second_slot(L, i, 1)

            def copy_conv():
                act.wait_ge(conv_turned, 1)
                act.wait_ge(dinv_ready, 1)
                for s in range(T):
                    act.activation(conv_t[:, s, :], pair_ps(misc_ps, 0)[:, s, :], ACT.Copy,
                                   scale=dinv[:, s:s + 1]).then_inc(conv_ready, 1)

            def second_attention(L):
                a = L.att + L.heads
                act.wait_ge(w2_used, L.w2_used + 2 * L.heads)
                if L is L0:
                    copy_conv()
                    split_slot(2, H0, UNIT)
                act.wait_ge(h_lo_ready, L.head + L.heads)
                act.wait_ge(scores_ready, 2 * T * (a + 1))
                for t in range(T):
                    act.activation(h_raw[:, t, :], acc_ps[:, t * D:(t + 1) * D], ACT.Copy)\
                        .then_inc(h_copied, 1)
                for t in range(T):
                    act.wait_ge(h_copied, a * T + t + 1)
                    act.activation(h_hi[:, t, :], h_raw[:, t, :], ACT.Copy).then_inc(h2_hi_ready, 1)
                exps(a)
                act.wait_ge(attn_turned, a + 1)
                act.activation(at_hi[:, :, :].rearrange("p s n -> p (s n)"), misc_ps[:, :], ACT.Copy)\
                    .then_inc(at2_hi_ready, 1)
                if L is L0:
                    split_slot(3, H0, UNIT)

            xt_high(0)
            first_slots(L0, 0)
            head(L0, 0, (L0, 1))
            with act.Fori(1, L0.heads - 1) as i:
                head(L0, i, (L0, i + 1))
            head(L0, L0.heads - 1, (L2, 0))
            second_attention(L0)
            xt_high(1)
            xt_high(2)
            head(L2, 0, (L2, 1))
            with act.Fori(1, L2.heads - 1) as i:
                head(L2, i, (L2, i + 1))
            head(L2, L2.heads - 1, None)
            second_attention(L2)
            act.wait_ge(count_turned, 1)
            act.activation(count_t[:, :, :].rearrange("p t n -> p (t n)"), misc_ps[:, :], ACT.Copy)\
                .then_inc(count_t_ready, 1)
            for p in range(XP):
                act.wait_ge(xt_turned, XP * 3 + p + 1)
                act.activation(xt3[:, 2 * p:2 * p + 2, :], pair_ps(acc_ps, p), ACT.Copy).then_inc(xt3_ready, 1)
            act.wait_ge(score3_ready, 1)
            for t in range(T):
                for g in range(2):
                    act.activation(ft3[:, t, g * HG:(g + 1) * HG, 0:C3], features_ps(t, g), ACT.Copy)\
                        .then_inc(ft3_ready, 1)
            act.wait_ge(res3_done, 1)
            for t in range(T):
                act.activation(xb[:, t, :], heads_ps[:, 2 * t * BANK:2 * t * BANK + D], ACT.Copy)\
                    .then_inc(res3_ready, 1)
            act.wait_ge(dst_turned, 1)
            act.activation(dst_rows, misc_ps[0:2 * H3, :], ACT.Copy).then_inc(dst_rows_ready, 1)
            for h in range(H3):
                act.wait_ge(dst_spread, h + 1)
                if h >= 2:
                    act.wait_ge(exp3_maxed, h - 1)
                for s in range(T):
                    for e, by_src in enumerate((score3, fifth3)):
                        ins = act.activation(exp3[:, h % 2, e, s, :], pair_ps(acc_ps, h % 3)[:, e, :], ACT.Exp,
                                             bias=by_src[:, s, 0, h:h + 1])
                ins.then_inc(exp3_ready, 1)
            for t in range(T):
                half = y[:, t, 0:HG * C3]
                act.wait_ge(first_summed3, t + 1)
                act.activation(half, half, ACT.Relu).then_inc(first_rectified3, 1)

        @block.gpsimd
        def _(pool):
            pool.memset(z[:, :, :], 0.0).then_inc(padded_zeroed, 1)
            pool.iota(iota_i[:, :], pattern=[[1, N]], base=0, channel_multiplier=0).then_inc(iota_ready, 1)
            pool.memset(ident[:, :], 0.0).then_inc(consts_zeroed, 1)
            pool.memset(zeros[:, :].bitcast(F32), 0.0)
            pool.memset(w3[:, :], 0.0)
            pool.memset(w3res[:, :], 0.0)
            pool.memset(w3_att[:, :, :], 0.0)
            pool.memset(minus_half[:, :], -0.5)
            pool.wait_ge(consts_zeroed, 1)
            pool.affine_select(out=ident[:, :], in_=ident[:, :], compare_op=ALU.not_equal, fill=1.0,
                               base=0, pattern=[[-1, P]], channel_multiplier=1).then_inc(consts_ready, 1)

            def low_slot(j, use, size):
                pool.wait_ge(split_hi[j], use + 1)
                pool.tensor_tensor(w_lo[:, j, 0:size], w_raw[:, j, 0:size], w_hi[:, j, 0:size].bitcast(F32),
                                   ALU.subtract).then_inc(split_lo[j], 1)

            def head(L, i, next_first):
                last = isinstance(i, int) and i == L.heads - 1
                if not last:
                    Ln, n = next_first
                    if L is L2:
                        low_slot(0, n + Ln.w1, Ln.w1_k * Ln.width)
                    low_slot(1, n + Ln.w1, Ln.w1_k * Ln.width)
                if last or L is L2:
                    low_slot(3, i + L.w2, L.w2_k * D)
                last, steps = L.steps(i)
                for u in range(steps):
                    pool.wait_ge(z_hi_ready, i * L.pairs + (L.pair + u + 1))
                    ks = step_blocks(last, u)
                    pool.tensor_tensor(z_lo[:, ks, :], z[:, ks, :], z_hi[:, ks, :].bitcast(F32),
                                       ALU.subtract).then_inc(z_lo_ready, 1)
                if L is L0 and not last:
                    low_slot(3, i + L.w2, L.w2_k * D)
                elif last and next_first is not None:
                    Ln, n = next_first
                    low_slot(1, n + Ln.w1, Ln.w1_k * Ln.width)

            def low_h2(l):
                for t in range(T):
                    pool.wait_ge(h2_hi_ready, T * (l // 2) + t + 1)
                    pool.tensor_tensor(h_lo[:, t, :], h_raw[:, t, :], h_hi[:, t, :].bitcast(F32), ALU.subtract)\
                        .then_inc(h2_lo_ready, 1)

            def rstd_of(l):
                for t in range(T):
                    pool.wait_ge(var_ready, T * l + t + 1)
                    pool.tensor_scalar(var_eps[:, t:t + 1], mean_var[:, t, 1:2], LN_EPS, None, ALU.add)\
                        .then_inc(eps_added, 1)
                    pool.wait_ge(eps_added, T * l + t + 1)
                    pool.tensor_tensor(rstd[:, t:t + 1], var_eps[:, t:t + 1], minus_half[:, t:t + 1], ALU.pow)\
                        .then_inc(rstd_ready, 1)

            def add_bias(l):
                pool.wait_ge(bias_landed, 16 * T * (l + 1))
                for t in range(T):
                    if l:
                        pool.wait_ge(x_ready, T * (l - 1) + t + 1)
                    pool.tensor_tensor(xb[:, t, :], xb[:, t, :], x_nat[:, t, :], ALU.add)\
                        .then_inc(xb_ready, 1)

            low_slot(1, 0, UNIT)
            pool.wait_ge(x_landed, 16)
            add_bias(0)
            head(L0, 0, (L0, 1))
            with pool.Fori(1, L0.heads - 1) as i:
                head(L0, i, (L0, i + 1))
            head(L0, L0.heads - 1, (L2, 0))
            pool.wait_ge(degree_ready, 1)
            pool.tensor_tensor(dinv[:, :], degree[:, :], minus_half[:, :], ALU.pow).then_inc(dinv_ready, 1)
            low_h2(0)
            rstd_of(0)
            low_slot(3, H0, UNIT)
            add_bias(1)
            rstd_of(1)
            add_bias(2)
            head(L2, 0, (L2, 1))
            with pool.Fori(1, L2.heads - 1) as i:
                head(L2, i, (L2, i + 1))
            head(L2, L2.heads - 1, None)
            low_h2(2)
            pool.wait_ge(w2_used, L2.w2_used + 2 * H2)
            pool.tensor_copy(w3_wide[:, :, 0:P], w3[:, :].rearrange("p (a n) -> p a n", a=1).broadcast_to([P, KD, P]))
            pool.tensor_copy(w3_wide[:, :, P:KC], w3_att[:, :, :]).then_inc(w3_widened, 1)
            pool.memset(ft3[:, :, :, C3:C3 + 1], 1.0)
            pool.tensor_tensor(sel_col[0:2 * H3, :], ident[0:2 * H3, 0:H3], ident[0:2 * H3, H3:2 * H3], ALU.add)\
                .then_inc(sel_col_ready, 1)
            rstd_of(2)
            pool.wait_ge(sel_col_ready, 1)
            pool.tensor_copy(sel3, sel_col[0:2 * H3, :].rearrange("p (h a) -> p h a", a=1)
                             .broadcast_to([2 * H3, H3, P])).then_inc(sel_ready, 1)
            pool.wait_ge(res3_ready, T)
            cols = slice(0, HG * C3)
            for t in range(T):
                half = y[:, t, cols]
                pool.wait_ge(scaled3, t + 1)
                pool.tensor_tensor(half, half, xb[:, t, cols], ALU.add).then_inc(first_summed3, 1)
            for t in range(T):
                half = y[:, t, cols]
                pool.wait_ge(first_rectified3, t + 1)
                pool.tensor_tensor(half, half, x_nat[:, t, cols], ALU.add).then_inc(first_ready3, 1)
            rstd_of(3)

        @block.vector
        def _(dve):
            def low_slot(j, use, size):
                dve.wait_ge(split_hi[j], use + 1)
                dve.tensor_tensor(w_lo[:, j, 0:size], w_raw[:, j, 0:size], w_hi[:, j, 0:size].bitcast(F32),
                                  ALU.subtract).then_inc(split_lo[j], 1)

            def xt_low(e):
                for p in range(XP):
                    dve.wait_ge(xt_hi_ready, XP * e + p + 1)
                    ks = slice(2 * p, 2 * p + 2)
                    dve.tensor_tensor(xt_lo[:, ks, :], pair_ps(acc_ps, p), xt_hi[:, ks, :].bitcast(F32),
                                      ALU.subtract).then_inc(xt_lo_ready, 1)

            def attention(a, width, masks, tile_of, tile_ready, value, meanwhile):
                counts, missing = masks
                dve.wait_ge(vec_landed, a * 32 + 32)
                for t in range(T):
                    dve.wait_ge(tile_ready, value + t)
                    for e, score in enumerate((score_src, score_dst)):
                        if t:
                            dve.wait_ge(scores_ready, a * 2 * T + e + 1)
                        dve.tensor_tensor_reduce(product[:, e, 0:width], tile_of(t),
                                                 att_vec[:, e, 0:width], 1.0, 0.0, ALU.mult, ALU.add,
                                                 score[:, t:t + 1]).then_inc(scores_ready, 1)
                meanwhile()
                for d in range(T):
                    ins = dve.tensor_tensor_reduce(logit[:, d, :], misc_ps[:, 0:N], missing[:, d, :], 1.0, -3e38,
                                                   ALU.add, ALU.max, top[:, d:d + 1])
                ins.then_inc(logit_masked, 1)
                dve.wait_ge(logit_masked, a + 1)
                dve.scalar_tensor_tensor(neg_top[:, :], top[:, :], -1.0, score_dst[:, :], ALU.mult, ALU.subtract)
                for d in range(T):
                    ins = dve.tensor_scalar(logit[:, d, :], logit[:, d, :], score_dst[:, d:d + 1], None, ALU.add)
                ins.then_inc(logit_summed, 1)
                dve.wait_ge(logit_summed, a + 1)
                dve.scalar_tensor_tensor(neg_max[:, :], neg_top[:, :], NEG_SLOPE, neg_top[:, :], ALU.mult, ALU.min)\
                    .then_inc(logit_ready, 1)
                dve.scalar_tensor_tensor(logit[:, :, :], logit[:, :, :], NEG_SLOPE, logit[:, :, :], ALU.mult, ALU.max)\
                    .then_inc(logit_ready, 1)
                for d in range(T):
                    dve.wait_ge(exp_ready, a * T + d + 1)
                    ins = dve.tensor_tensor_reduce(attn[:, d, :], expd[:, d, :], counts[:, d, :], 1.0, ATT_EPS,
                                                   ALU.mult, ALU.add, denom[:, d:d + 1])
                ins.then_inc(exp_counted, 1)
                dve.wait_ge(exp_counted, a + 1)
                dve.reciprocal(rdenom[:, :], denom[:, :]).then_inc(rdenom_ready, 1)

            def collect_w3():
                dve.wait_ge(w3_scored, 1)
                for c in range(2):
                    q = slice(c * C3, (c + 1) * C3)
                    scored = acc_ps[q, BANK + 2 * P:BANK + 2 * P + 2 * H3].rearrange("p (e k c) -> p k e c", e=2, c=2)
                    ins = dve.tensor_copy(w3_att[q, :, c:c + 3:2], scored[:, :, :, c])
                ins.then_inc(w3_ready, 1)

            def head(L, i, masks, next_first):
                a = i + L.att
                first = L is L0 and isinstance(i, int) and i == 0
                nb = 0 if L is L0 else L0.heads * L0.blocks
                late = isinstance(i, int) and (i == 0 or (L is L2 and i == L.heads - 1))
                dve.tensor_copy(bias_now[:, :, 0:L.blocks], bias_col[:, :, bass.ds(i * L.blocks + nb, L.blocks)])\
                    .then_inc(bias_now_ready, 1)

                def low_h():
                    for t in range(T):
                        dve.wait_ge(h_hi_ready, (i + L.head) * T + t + 1)
                        if t == T - 1:
                            dve.wait_ge(scores_spread, a + 1)
                        ins = dve.tensor_tensor(h_lo[:, t, 0:L.width], h_raw[:, t, 0:L.width],
                                                h_hi[:, t, 0:L.width].bitcast(F32), ALU.subtract)
                    ins.then_inc(h_lo_ready, 1)

                def await_spread():
                    if first:
                        collect_w3()
                    dve.wait_ge(scores_spread, a + 1)

                attention(a, L.width, masks, lambda t: h_raw[:, t, 0:L.width], h_copied, a * T + 1,
                          await_spread if late else low_h)
                dve.wait_ge(rdenom_ready, a + 1)
                for d in range(T):
                    ins = dve.tensor_scalar(attn[:, d, :], attn[:, d, :], rdenom[:, d:d + 1], None, ALU.mult)
                ins.then_inc(attn_ready, 1)
                if late:
                    low_h()
                dve.wait_ge(at_hi_ready, i + (L.head + 1))
                dve.tensor_tensor(at_lo[:, :, :].rearrange("p s n -> p (s n)"), misc_ps[:, :],
                                  at_hi[:, :, :].rearrange("p s n -> p (s n)").bitcast(F32), ALU.subtract)\
                    .then_inc(at_lo_ready, 1)
                last = isinstance(i, int) and i == L.heads - 1
                if last or L is L2:
                    low_slot(2, i + L.w2, L.w2_k * D)
                else:
                    Ln, n = next_first
                    low_slot(0, n + Ln.w1, Ln.w1_k * Ln.width)
                last, steps = L.steps(i)
                for u in range(steps):
                    ks = step_blocks(last, u)
                    dve.wait_ge(elu_exp, i * (2 * L.pairs) + 2 * (L.pair + u + 1))
                    pos = z_pos[:, u % 2:u % 2 + 1, :] if last else z_pos[:, :, :]
                    if last and u >= 2:
                        dve.wait_ge(z_ready, i * L.pairs + (L.pair + u - 1))
                    elif not last and u:
                        dve.wait_ge(z_ready, i * L.pairs + (L.pair + u))
                    for k in range(ks.start, ks.stop):
                        ins = dve.tensor_scalar(pos[:, k - ks.start, :], step_ps(last, u)[:, k - ks.start, :],
                                                bias_now[:, 1, k:k + 1], bias_now[:, 2, k:k + 1], ALU.max, ALU.add)
                    ins.then_inc(elu_pos, 1)
                    dve.wait_ge(elu_pos, i * L.pairs + (L.pair + u + 1))
                    dve.scalar_tensor_tensor(z[:, ks, :], z[:, ks, :], 1.0, pos, ALU.min, ALU.add)\
                        .then_inc(z_ready, 1)
                if not last and L is L0:
                    low_slot(2, i + L.w2, L.w2_k * D)
                elif last and next_first is not None:
                    Ln, n = next_first
                    low_slot(0, n + Ln.w1, Ln.w1_k * Ln.width)

            sums = [0]
            halves = [0]

            def sum_piece(t, c, ins):
                sums[0] += 1
                ins.then_inc(y_ready, 1)
                dve.wait_ge(y_ready, sums[0])
                moments(t, c)

            def moments(t, c):
                halves[0] += 1
                dve.bn_stats(stats[:, t, c, :], y[:, t, c * (D // 2):(c + 1) * (D // 2)]).then_inc(stats_ready, 1)

            def variance(l, t):
                dve.wait_ge(stats_ready, halves[0])
                dve.bn_aggr(mean_var[:, t, :], stats[:, t, :, :].rearrange("p c s -> p (c s)"))\
                    .then_inc(var_ready, 1)

            def normalise(l):
                for t in range(T):
                    dve.wait_ge(rstd_ready, T * l + t + 1)
                    dve.tensor_scalar(x_nat[:, t, :], y[:, t, :], mean_var[:, t, 0:1], rstd[:, t:t + 1],
                                      ALU.subtract, ALU.mult).then_inc(x_ready, 1)

            def layer_norm(l, piece):
                for t in range(T):
                    dve.wait_ge(xb_ready, T * l + t + 1)
                    for c, (at, size) in enumerate(HEAD_PIECES[D]):
                        dve.wait_ge(out_done, 2 * (T * l + t) + c + 1)
                        sum_piece(t, c, piece(t, slice(at, at + size), heads_ps[:, 2 * t * BANK + at:
                                                                                2 * t * BANK + at + size]))
                    variance(l, t)
                normalise(l)

            def second_attention(L, l, masks):
                attention(L.att + L.heads, D, masks, lambda t: acc_ps[:, t * D:(t + 1) * D],
                          w2_used, L.w2_used + 2 * L.heads - 1,
                          lambda: dve.wait_ge(scores_spread, L.att + L.heads + 1))
                dve.wait_ge(at2_hi_ready, l // 2 + 1)
                dve.tensor_tensor(at_lo[:, :, :].rearrange("p s n -> p (s n)"), misc_ps[:, :],
                                  at_hi[:, :, :].rearrange("p s n -> p (s n)").bitcast(F32), ALU.subtract)\
                    .then_inc(at2_lo_ready, 1)
                dve.wait_ge(rdenom_ready, L.att + L.heads + 1)
                layer_norm(l, lambda t, q, ps: dve.scalar_tensor_tensor(
                    y[:, t, q], ps, rdenom[:, t:t + 1], xb[:, t, q], ALU.mult, ALU.add))

            dve.wait_ge(iota_ready, 1)
            dve.tensor_copy(iota_b[:, :], iota_i[:, :])
            dve.wait_ge(edges_landed, 32)
            dve.tensor_copy(edge_f[:, :, :], edge_i[:, :, :]).then_inc(edges_ready, 1)
            dve.wait_ge(edges_ready, 1)

            def onehots(c, b):
                for e in range(2):
                    ins = dve.tensor_scalar(onehot[:, b, e, :], iota_b[:, :], edge_f[:, e, bass.ds(c, 1)], None,
                                            ALU.is_equal)
                ins.then_inc(onehot_ready, 1)

            for c in range(LEAD):
                if c >= RING:
                    dve.wait_ge(onehot_used, c - RING + 1)
                onehots(c, c % RING)
            with dve.Fori(0, (EC - LEAD - LATE) // RING) as g:
                for b in range(RING):
                    dve.wait_ge(onehot_used, g * RING + (LEAD + b - RING + 1))
                    onehots(g * RING + (LEAD + b), (LEAD + b) % RING)
            xt_low(0)
            low_slot(0, 0, UNIT)
            for c in range(EC - LATE, EC):
                if c == EC - RING:
                    nb0 = L0.heads * L0.blocks
                    dve.wait_ge(padded_turned, 1)
                    dve.tensor_copy(attn3_t[:, :], acc_ps[:, BANK:BANK + 2 * H3])
                    dve.tensor_copy(bias_col[:, 0, 0:nb0], acc_ps[:, 0:nb0])
                    dve.tensor_copy(bias_col[:, 0, nb0:NB], acc_ps[:, P:P + NB - nb0])
                    for e in range(2):
                        q = slice(e * C3, (e + 1) * C3)
                        dve.tensor_copy(w3[q, q], acc_ps[q, 2 * P:2 * P + C3])
                        ins = dve.tensor_copy(w3res[q, q], acc_ps[q, 3 * P:3 * P + C3])
                    ins.then_inc(padded_copied, 1)
                    dve.wait_ge(padded_copied, 1)
                    dve.tensor_scalar(bias_col[:, 1, :], bias_col[:, 0, :], -1.0, None, ALU.mult)
                    dve.tensor_scalar(bias_col[:, 2, :], bias_col[:, 0, :], -1.0, None, ALU.add)\
                        .then_inc(padded_copied, 1)
                dve.wait_ge(onehot_used, c - RING + 1)
                onehots(c, c % RING)
            dve.wait_ge(padded_copied, 2)
            dve.wait_ge(onehot_used, EC)
            dve.tensor_copy(count[:, :, :].rearrange("p t n -> p (t n)"), misc_ps[:, :]).then_inc(count_ready, 1)
            dve.wait_ge(count_ready, 1)
            dve.wait_ge(consts_ready, 1)
            dve.tensor_scalar(absent[:, :, :], count[:, :, :], 0.0, MASKED, ALU.is_equal, ALU.mult)

            def add_loops():
                dve.tensor_copy(count_loop[:, :, :], count[:, :, :]).then_inc(count_ready, 1)
                dve.wait_ge(count_ready, 2)
                for t in range(T):
                    diagonal = count_loop[:, t, t * P:(t + 1) * P]
                    ins = dve.tensor_tensor(diagonal, diagonal, ident[:, :], ALU.add)
                ins.then_inc(count_ready, 1)
                dve.wait_ge(count_ready, 3)
                dve.tensor_reduce(degree[:, :], count_loop[:, :, :], mybir.AxisListType.X, ALU.add)\
                    .then_inc(degree_ready, 1)
                dve.tensor_scalar(absent_loop[:, :, :], count_loop[:, :, :], 0.0, MASKED, ALU.is_equal, ALU.mult)
                dve.wait_ge(dinv_ready, 1)
                for t in range(T):
                    ins = dve.tensor_scalar(attn[:, t, :], count_loop[:, t, :], dinv[:, t:t + 1], None, ALU.mult)
                ins.then_inc(conv_scaled, 1)

            plain, looped = (count, absent), (count_loop, absent_loop)
            head(L0, 0, plain, (L0, 1))
            with dve.Fori(1, L0.heads - 1) as i:
                head(L0, i, plain, (L0, i + 1))
            head(L0, L0.heads - 1, plain, (L2, 0))
            add_loops()
            second_attention(L0, 0, plain)
            low_slot(2, H0, UNIT)
            xt_low(1)
            layer_norm(1, lambda t, q, ps: dve.tensor_tensor(y[:, t, q], ps, xb[:, t, q], ALU.add))
            xt_low(2)
            head(L2, 0, looped, (L2, 1))
            with dve.Fori(1, L2.heads - 1) as i:
                head(L2, i, looped, (L2, i + 1))
            head(L2, L2.heads - 1, looped, None)
            second_attention(L2, 2, looped)
            for t in range(T):
                dve.wait_ge(ft3_done, t + 1)
                for g in range(2):
                    scored = wide_ps(t, g)[:, :, P:KC].rearrange("p k (e c) -> p e k c", e=2)
                    ins = dve.tensor_copy(score3[:, t, :, g * HG:(g + 1) * HG]
                                          .rearrange("p e (k c) -> p e k c", c=2), scored)
            ins.then_inc(score3_ready, 1)
            dve.wait_ge(score3_ready, 1)
            dve.tensor_scalar(fifth3[:, :, :, :], score3[:, :, :, :], NEG_SLOPE, None, ALU.mult)\
                .then_inc(score3_ready, 1)
            for p in range(H3 // 2):
                dve.wait_ge(src_spread, p + 1)
                if p >= 3:
                    dve.wait_ge(masked3, p - 2)
                ps = src_bank(p)
                for c in range(2):
                    for d in range(T):
                        ins = dve.tensor_tensor_reduce(discard3[:, (4 * p + 2 * c + d) % 12, :], ps[:, c, :],
                                                       absent[:, d, :], 1.0, -3e38, ALU.add, ALU.max,
                                                       top3[:, d, 2 * p + c:2 * p + c + 1])
                ins.then_inc(masked3, 1)
            dve.wait_ge(masked3, H3 // 2)
            dve.scalar_tensor_tensor(neg_top3[:, :, :], top3[:, :, :], -1.0, score3[:, :, 1, :], ALU.mult, ALU.subtract)\
                .then_inc(neg_top3_ready, 1)
            dve.wait_ge(neg_top3_ready, 1)
            dve.scalar_tensor_tensor(neg_max3[:, :, :], neg_top3[:, :, :], NEG_SLOPE, neg_top3[:, :, :],
                                     ALU.mult, ALU.min).then_inc(neg_max3_ready, 1)
            dve.wait_ge(neg_max3_ready, 1)
            dve.tensor_tensor(shift3[:, :, 0, :], score3[:, :, 1, :], neg_max3[:, :, :], ALU.add)
            dve.tensor_tensor(shift3[:, :, 1, :], fifth3[:, :, 1, :], neg_max3[:, :, :], ALU.add)\
                .then_inc(shift3_ready, 1)
            dve.wait_ge(shift3_ready, 1)
            dve.tensor_copy(dst_parts[:, :, :, 0, :], shift3[:, :, :, :]).then_inc(dst_split, 1)
            dve.wait_ge(dst_split, 1)
            dve.tensor_tensor(dst_parts[:, :, :, 1, :], shift3[:, :, :, :], dst_parts[:, :, :, 0, :].bitcast(F32),
                              ALU.subtract).then_inc(dst_split, 1)

            def invert3(g):
                dve.wait_ge(agg3_done, HG * (g + 1))
                hs = slice(g * HG, (g + 1) * HG)
                for t in range(T):
                    ins = dve.tensor_scalar(denom3[:, t, hs], sums_ps(t, g)[:, :, C3], ATT_EPS, None, ALU.max)
                ins.then_inc(denom3_ready, 1)
                dve.wait_ge(denom3_ready, g + 1)
                dve.reciprocal(rdenom3[:, :, hs], denom3[:, :, hs]).then_inc(rdenom3_ready, 1)

            def scale3(g, t):
                dve.wait_ge(rdenom3_ready, g + 1)
                inverse = rdenom3[:, t, g * HG:(g + 1) * HG].rearrange("p (h a) -> p h a", a=1)\
                    .broadcast_to([P, HG, C3])
                dve.tensor_tensor(y[:, t, g * HG * C3:(g + 1) * HG * C3].rearrange("p (h c) -> p h c", h=HG),
                                  sums_ps(t, g)[:, :, 0:C3], inverse, ALU.mult).then_inc(scaled3, 1)

            dve.wait_ge(count_t_ready, 1)
            for h in range(H3):
                dve.wait_ge(exp3_ready, h + 1)
                if h >= 2:
                    dve.wait_ge(agg3_done, h - 1)
                b = h % 2
                dve.tensor_tensor(weight3[:, b, :, :], exp3[:, b, 0, :, :], exp3[:, b, 1, :, :], ALU.max)\
                    .then_inc(exp3_maxed, 1)
                dve.wait_ge(exp3_maxed, h + 1)
                dve.scalar_tensor_tensor(weight3[:, b, :, :], weight3[:, b, :, :], 1.0, count_t[:, :, :],
                                         ALU.min, ALU.mult).then_inc(weight3_ready, 1)
                if h == HG + 2:
                    invert3(0)
                if h >= HG + 3 and h < HG + 3 + T:
                    scale3(0, h - HG - 3)

            q = slice(HG * C3, H3 * C3)
            dve.wait_ge(first_ready3, 1)
            moments(0, 0)
            invert3(1)
            for t in range(T):
                scale3(1, t)
            for t in range(1, T):
                dve.wait_ge(first_ready3, t + 1)
                moments(t, 0)
            for t in range(T):
                dve.wait_ge(scaled3, T + t + 1)
                dve.tensor_tensor(y[:, t, q], y[:, t, q], xb[:, t, q], ALU.add).then_inc(summed3, 1)
            for t in range(T):
                dve.wait_ge(summed3, t + 1)
                sum_piece(t, 1, dve.scalar_tensor_tensor(y[:, t, q], y[:, t, q], 0.0, x_nat[:, t, q],
                                                         ALU.max, ALU.add))
                variance(3, t)
            normalise(3)

        @block.tensor
        def _(pe):
            def product_d(slots, width, use, per_slot, tiles=range(T), turns=None):
                for t in tiles:
                    for k in range(KD):
                        j = slots + k // per_slot
                        o = (k % per_slot) * width
                        if t == 0 and k % per_slot == 0:
                            pe.wait_ge(split_lo[j], use + 1)
                        if turns is not None and t == 0 and k % 2 == 0:
                            pe.wait_ge(xt_lo_ready, XP * turns + k // 2 + 1)
                        tile_k = slice(t * P, (t + 1) * P)
                        for x_part, w_parts in ((xt_hi, (w_hi, w_lo)), (xt_lo, (w_hi,))):
                            for w_part in w_parts:
                                for at, size in HEAD_PIECES[width]:
                                    to = HEAD_AT[width] + 2 * t * BANK + at
                                    ins = pe.matmul(heads_ps[:, to:to + size],
                                                    x_part[:, k, tile_k], w_part[:, j, o + at:o + at + size],
                                                    start=(k == 0 and x_part is xt_hi and w_part is w_hi),
                                                    stop=(k == KD - 1 and x_part is xt_lo))
                        if k % per_slot == per_slot - 1:
                            yield t, k == KD - 1, ins

            def product_z_last(L):
                i = L.heads - 1
                for k in range(L.blocks):
                    j = 2 + k // L.w2_k
                    o = (k % L.w2_k) * D
                    pe.wait_ge(z_hi_ready, i * L.pairs + (L.pair + k + 1))
                    if k % L.w2_k == 0:
                        pe.wait_ge(split_lo[j], i + (L.w2 + 1))
                    for t in range(T):
                        for w_part in (w_hi, w_lo):
                            for at, size in ACC_PIECES[t]:
                                pe.matmul(acc_ps[:, t * D + at:t * D + at + size],
                                          z_hi[:, k, t * P:(t + 1) * P], w_part[:, j, o + at:o + at + size],
                                          start=False, stop=False, skip_group_check=True)
                for t in range(T):
                    for at, size in ACC_PIECES[t]:
                        for k in range(L.blocks):
                            j = 2 + k // L.w2_k
                            o = (k % L.w2_k) * D
                            if t == 0 and at == 0:
                                pe.wait_ge(z_lo_ready, i * L.pairs + (L.pair + k + 1))
                            ins = pe.matmul(acc_ps[:, t * D + at:t * D + at + size],
                                            z_lo[:, k, t * P:(t + 1) * P], w_hi[:, j, o + at:o + at + size],
                                            start=False, stop=False, skip_group_check=True)
                        if (t, at) in ((1, 0), (1, D - BANK)):
                            ins.then_inc(w2_used, 1)

            def product_z(L, i, ks):
                for z_part, w_parts, ready in ((z_hi, (w_hi, w_lo), z_hi_ready), (z_lo, (w_hi,), z_lo_ready)):
                    for k in ks:
                        j = 2 + k // L.w2_k
                        o = (k % L.w2_k) * D
                        if k % 2 == 0:
                            pe.wait_ge(ready, i * L.pairs + (L.pair + k // 2 + 1))
                        if k % L.w2_k == 0 and z_part is z_hi:
                            pe.wait_ge(split_lo[j], i + (L.w2 + 1))
                        for t in range(T):
                            for w_part in w_parts:
                                for at, size in ACC_PIECES[t]:
                                    ins = pe.matmul(acc_ps[:, t * D + at:t * D + at + size],
                                                    z_part[:, k, t * P:(t + 1) * P],
                                                    w_part[:, j, o + at:o + at + size],
                                                    start=False, stop=False, skip_group_check=True)
                        if k % L.w2_k == L.w2_k - 1 and z_part is z_lo:
                            ins.then_inc(w2_used, 1)

            def spread_column(ps, column):
                return pe.matmul(ps, column.broadcast_to([P, P]), ident[:, :], start=True, stop=True)

            def spread_scores(a):
                pe.wait_ge(scores_ready, a * 2 * T + 2 * T)
                for t in range(T):
                    ins = spread_column(misc_ps[:, t * P:(t + 1) * P], score_src[:, t:t + 1])
                ins.then_inc(scores_spread, 1)

            def turn_attention(a, ready, value):
                pe.wait_ge(ready, value)
                for s in range(T):
                    for d in range(T):
                        o = s * N + d * P
                        ins = pe.transpose(misc_ps[:, o:o + P], attn[:, d, s * P:(s + 1) * P], ident[:, :])
                ins.then_inc(attn_turned, 1)

            def turn_padded():
                pe.wait_ge(padded_landed, 16 * 8)
                for n in range(5):
                    ins = pe.transpose(acc_ps[:, n * P:(n + 1) * P], padded[:, n, :], ident[:, :])
                ins.then_inc(padded_turned, 1)

            def score_w3():
                pe.wait_ge(padded_copied, 1)
                pe.matmul(acc_ps[:, BANK + 2 * P:BANK + 2 * P + 2 * H3], padded[:, 2, :], attn3_t[:, :],
                          start=True, stop=True).then_inc(w3_scored, 1)

            def turn_conv():
                pe.wait_ge(conv_scaled, 1)
                for s in range(T):
                    for d in range(T):
                        o = s * N + d * P
                        ins = pe.transpose(misc_ps[:, o:o + P], attn[:, d, s * P:(s + 1) * P], ident[:, :])
                ins.then_inc(conv_turned, 1)

            def count_chunk(b, start, stop):
                for t in range(T):
                    ins = pe.matmul(misc_ps[:, t * N:(t + 1) * N], onehot[:, b, 0, t * P:(t + 1) * P],
                                    onehot[:, b, 1, :], start=start and t == 0, stop=stop and t == T - 1,
                                    skip_group_check=True)
                ins.then_inc(onehot_used, 1)

            def keep_warm(ps, count):
                for _ in range(count):
                    pe.matmul(ps, zeros[:, :], xt_hi[:, 0:2, :].rearrange("p k n -> p (k n)"),
                              start=True, stop=True)

            def head(L, i):
                a = i + L.att
                first = L is L0 and isinstance(i, int) and i == 0
                fresh = isinstance(i, int) and i == 0
                ahead = L is L2
                if ahead and not fresh:
                    tiles = range(1, T)
                else:
                    tiles = range(T)
                    if not fresh:
                        pe.wait_ge(z_ready, i * L.pairs + (L.pair + 1 - L.pairs))
                turns = (0 if first else 2) if fresh else None
                for t, tile_done, ins in product_d(0, L.width, i + L.w1, L.w1_k, tiles, turns):
                    if tile_done:
                        ins.then_inc(h_done, 1)
                        if t == 0 and not fresh:
                            pe.wait_ge(z_ready, i * L.pairs + L.pair)
                    if first and not (t == T - 1 and tile_done):
                        start = EC - LATE + (2 * t + tile_done) * RING
                        for c in range(start, start + RING):
                            pe.wait_ge(onehot_ready, c + 1)
                            count_chunk(c % RING, False, False)
                        if t == 0 and not tile_done:
                            turn_padded()
                if first:
                    score_w3()
                if fresh:
                    pe.wait_ge(h_copied, a * T + 1)
                    keep_warm(heads_ps[:, 0:BANK], WARM_HEAD)
                if first:
                    pe.wait_ge(count_ready, 1)
                if not fresh:
                    product_z(L, i - 1, range(0, 2))
                spread_scores(a)
                if fresh:
                    keep_warm(heads_ps[:, 0:BANK], WARM_HEAD)
                    if first:
                        pe.wait_ge(w3_ready, 1)
                    clear_sums()
                else:
                    product_z(L, i - 1, range(2, L.blocks if ahead else L.blocks - 1))
                next_tile = None
                if ahead and not (isinstance(i, int) and i == L.heads - 1):
                    next_tile = product_d(0, L.width, i + (L.w1 + 1), L.w1_k, range(1))
                    next(next_tile)
                alone = first or (ahead and isinstance(i, int) and i == L.heads - 1)
                if alone:
                    keep_warm(heads_ps[:, 0:BANK], WARM_HEAD if first else WARM_HEAD // 3)
                turn_attention(a, attn_ready, i + (L.head + 1))
                if alone:
                    keep_warm(heads_ps[:, 0:BANK], WARM_HEAD // 2)
                if next_tile is not None:
                    t, tile_done, ins = next(next_tile)
                    ins.then_inc(h_done, 1)
                if not fresh and not ahead:
                    product_z(L, i - 1, range(L.blocks - 1, L.blocks))
                pe.wait_ge(h_lo_ready, i + (L.head + 1))
                pe.wait_ge(at_lo_ready, i + (L.head + 1))
                last, steps = L.steps(i)
                for u in range(steps):
                    if last and u == 5:
                        pe.wait_ge(z_ready, i * L.pairs + (L.pair + 1))
                    blocks = step_blocks(last, u)
                    for k in range(blocks.start, blocks.stop):
                        for s in range(T):
                            for h_part, a_part in ((h_hi, at_hi), (h_hi, at_lo), (h_lo, at_hi)):
                                ins = pe.matmul(step_ps(last, u)[:, k - blocks.start, :],
                                                h_part[:, s, k * P:(k + 1) * P], a_part[:, s, :],
                                                start=(s == 0 and a_part is at_hi and h_part is h_hi),
                                                stop=(s == T - 1 and h_part is h_lo))
                    ins.then_inc(agg_done, 1)

            def clear_sums():
                for b in range(3):
                    pe.matmul(acc_ps[:, b * BANK:(b + 1) * BANK], zeros[:, :],
                              xt_hi[:, 0:2, :].rearrange("p k n -> p (k n)"), start=True, stop=False,
                              skip_group_check=True)

            def second_attention(L, l):
                a = L.att + L.heads
                if L is L0:
                    turn_conv()
                keep_warm(heads_ps[:, 0:BANK], WARM_SCORES)
                if L is L0:
                    pe.wait_ge(conv_ready, T)
                spread_scores(a)
                keep_warm(heads_ps[:, 0:BANK], WARM_SOFTMAX)
                turn_attention(a, exp_counted, a + 1)
                pe.wait_ge(at2_hi_ready, l // 2 + 1)
                for t in range(T):
                    for at, size in HEAD_PIECES[D]:
                        for a_part, h_part in ((at_hi, h_hi), (at_hi, h_lo), (at_lo, h_hi)):
                            for s in range(T):
                                if t == 0 and at == 0 and h_part is h_lo:
                                    pe.wait_ge(h2_lo_ready, T * (l // 2) + s + 1)
                                if t == 0 and at == 0 and a_part is at_lo and s == 0:
                                    pe.wait_ge(at2_lo_ready, l // 2 + 1)
                                ins = pe.matmul(heads_ps[:, 2 * t * BANK + at:2 * t * BANK + at + size],
                                                a_part[:, s, t * P:(t + 1) * P], h_part[:, s, at:at + size],
                                                start=(s == 0 and a_part is at_hi and h_part is h_hi),
                                                stop=(s == T - 1 and a_part is at_lo))
                        ins.then_inc(out_done, 1)

            def turn_x(ready, values):
                for t in range(T):
                    pe.wait_ge(ready, values[t])
                    for p in range(XP):
                        for c in range(2):
                            k = 2 * p + c
                            ins = pe.transpose(pair_ps(acc_ps, p)[:, c, t * P:(t + 1) * P],
                                               x_nat[:, t, k * P:(k + 1) * P], ident[:, :])
                        if t == T - 1:
                            ins.then_inc(xt_turned, 1)

            for c in range(LEAD):
                pe.wait_ge(onehot_ready, c + 1)
                count_chunk(c % RING, c == 0, False)
            pe.wait_ge(consts_ready, 1)
            turn_x(x_landed, [16] * T)
            with pe.Fori(0, (EC - LEAD - LATE) // RING) as g:
                for b in range(RING):
                    pe.wait_ge(onehot_ready, g * RING + (LEAD + b + 1))
                    count_chunk((LEAD + b) % RING, False, False)

            pe.wait_ge(xt_hi_ready, 1)
            keep_warm(heads_ps[:, 0:BANK], WARM_START)
            head(L0, 0)
            with pe.Fori(1, L0.heads - 1) as i:
                head(L0, i)
            head(L0, L0.heads - 1)
            product_z_last(L0)
            second_attention(L0, 0)
            keep_warm(misc_ps[:, :], WARM_NORM)
            for s in range(T):
                pe.wait_ge(x_ready, s + 1)
                for p in range(XP):
                    for c in range(2):
                        k = 2 * p + c
                        ins = pe.matmul(pair_ps(acc_ps, p)[:, c, :], x_nat[:, s, k * P:(k + 1) * P],
                                        conv_t[:, s, :], start=(s == 0 and c == 0),
                                        stop=(s == T - 1 and c == 1), skip_group_check=True)
                    if s == T - 1:
                        ins.then_inc(xt_turned, 1)
            for t, tile_done, ins in product_d(2, D, H0, KU, range(T - 1), turns=1):
                if tile_done:
                    ins.then_inc(out_done, 2)
            t = T - 1
            for at, size in HEAD_PIECES[D]:
                for x_part, w_part in ((xt_hi, w_hi), (xt_hi, w_lo), (xt_lo, w_hi)):
                    for k in range(KD):
                        o = k % KU * D + at
                        ins = pe.matmul(heads_ps[:, 2 * t * BANK + at:2 * t * BANK + at + size],
                                        x_part[:, k, t * P:(t + 1) * P], w_part[:, 2 + k // KU, o:o + size],
                                        start=(k == 0 and x_part is xt_hi and w_part is w_hi),
                                        stop=(k == KD - 1 and x_part is xt_lo))
                ins.then_inc(out_done, 1)
            keep_warm(misc_ps[:, :], WARM_NORM)
            turn_x(x_ready, [T * 1 + t + 1 for t in range(T)])
            head(L2, 0)
            with pe.Fori(1, L2.heads - 1) as i:
                head(L2, i)
            head(L2, L2.heads - 1)
            product_z_last(L2)
            second_attention(L2, 2)
            for s in range(T):
                for d in range(T):
                    o = s * N + d * P
                    ins = pe.transpose(misc_ps[:, o:o + P], count[:, d, s * P:(s + 1) * P], ident[:, :])
            ins.then_inc(count_turned, 1)
            keep_warm(acc_ps[:, 0:BANK], WARM_NORM)
            turn_x(x_ready, [T * 2 + t + 1 for t in range(T)])
            pe.wait_ge(w3_widened, 1)
            for t in range(T):
                for k in range(KD):
                    if t == 0 and k % 2 == 0:
                        pe.wait_ge(xt3_ready, k // 2 + 1)
                    ins = pe.matmul(wide_ps(t, k // (KD // 2))[:, k % (KD // 2), :],
                                    xt3[:, k, t * P:(t + 1) * P], w3_wide[:, k, :], start=True, stop=True)
                ins.then_inc(ft3_done, 1)
            pe.wait_ge(score3_ready, 1)
            pe.wait_ge(count_t_ready, 1)
            for p in range(H3 // 2):
                if p == 4:
                    pe.wait_ge(ft3_ready, T * 2)
                    for t in range(T):
                        for k in range(KD):
                            o = 2 * t * BANK + k * P
                            ins = pe.matmul(heads_ps[:, o:o + P], xt3[:, k, t * P:(t + 1) * P], w3res[:, :],
                                            start=True, stop=True)
                    ins.then_inc(res3_done, 1)
                if p >= 4:
                    pe.wait_ge(masked3, p - 2)
                for c in range(2):
                    h = 2 * p + c
                    for t in range(T):
                        ins = spread_column(src_bank(p)[:, c, t * P:(t + 1) * P], score3[:, t, 0, h:h + 1])
                ins.then_inc(src_spread, 1)
            keep_warm(misc_ps[:, :], WARM_SHIFTS)
            pe.wait_ge(dst_split, 2)
            for r in range(2):
                for t in range(T):
                    o = r * N + t * P
                    ins = pe.transpose(misc_ps[0:2 * H3, o:o + P],
                                       dst_parts[:, t, r, :, :].bitcast(F32).rearrange("p a h -> p (a h)"), ident[:, :])
            ins.then_inc(dst_turned, 1)
            pe.wait_ge(dst_rows_ready, 1)
            pe.wait_ge(sel_ready, 1)
            pe.wait_ge(res3_ready, T)
            pe.wait_ge(masked3, H3 // 2)

            def spread3(h):
                if h >= 3:
                    pe.wait_ge(exp3_ready, h - 2)
                pe.matmul(acc_ps[:, h % 3 * BANK:(h % 3 + 1) * BANK], sel3[:, h, :], dst_rows,
                          start=True, stop=True).then_inc(dst_spread, 1)

            def aggregate3(h):
                pe.wait_ge(weight3_ready, h + 1)
                for t in range(T):
                    for s in range(T):
                        ins = pe.matmul(sums_ps(t, h // HG)[:, h % HG, :], weight3[:, h % 2, s, t * P:(t + 1) * P],
                                        ft3[:, s, h, :], start=(s == 0), stop=(s == T - 1))
                ins.then_inc(agg3_done, 1)

            for h in range(H3 + 3):
                if h < H3:
                    spread3(h)
                if h == 2:
                    keep_warm(misc_ps[:, :], WARM_EXPS)
                if h >= 3:
                    aggregate3(h - 3)
                    if h < H3 + 2:
                        keep_warm(misc_ps[:, :], WARM_HEAD3 if h < H3 else 2 * WARM_HEAD3)


_INS = ["x", "src", "dst",
        "L0_gnn_W1", "L0_gnn_a_src1", "L0_gnn_a_dst1", "L0_gnn_b1",
        "L0_gnn_W2", "L0_gnn_a_src2", "L0_gnn_a_dst2", "L0_gnn_b2",
        "L1_gnn_W", "L1_gnn_b",
        "L2_gnn_W1", "L2_gnn_att_src1", "L2_gnn_att_dst1", "L2_gnn_b1",
        "L2_gnn_W2", "L2_gnn_att_src2", "L2_gnn_att_dst2", "L2_gnn_b2",
        "L3_gnn_W", "L3_gnn_attn_l", "L3_gnn_attn_r", "L3_gnn_W_res"]


def kernel(**inputs):
    import numpy as np
    import concourse.bacc as bacc
    from concourse.bass_utils import run_bass_kernel_spmd

    nc = bacc.Bacc("TRN2", target_bir_lowering=False, num_devices=1)
    arrays, args = {}, []
    for name in _INS:
        a = np.ascontiguousarray(inputs[name])
        arrays[f"in_{name}"] = a
        args.append(nc.dram_tensor(f"in_{name}", a.shape, mybir.dt.from_np(a.dtype), kind="ExternalInput").ap())
    out = nc.dram_tensor("out", inputs["x"].shape, F32, kind="ExternalOutput").ap()
    gnn_kernel(nc, *args, out)
    return run_bass_kernel_spmd(nc, [arrays], core_ids=[0]).results[0]["out"]
```
